# Optimizing a Trainium2 kernel written in Bass

```python
import numpy as np
import jax
import jax.numpy as jnp

def _softmax(x, axis=-1):
    return jax.nn.softmax(x, axis=axis)

def _gelu(x):
    return jax.nn.gelu(x, approximate=True)

def _silu(x):
    return jax.nn.silu(x)

def _sigmoid(x):
    return jax.nn.sigmoid(x)

def _layernorm(x, axis=-1, eps=1e-05):
    m = jnp.mean(x, axis=axis, keepdims=True)
    v = jnp.var(x, axis=axis, keepdims=True)
    return (x - m) / jnp.sqrt(v + eps)

def _scatter_add(tgt, idx, src, axis=0):
    return tgt.at[idx].add(src)

def _segment_sum(src, seg, n):
    return jax.ops.segment_sum(src, seg, n)
kernel_name = 'mk_gnn_preln_d4_gnn_r8_4cb9cf'

def setup_inputs(seed: int=0):
    np.random.seed(seed)
    _w = jnp.asarray

    def _rec_inputs():
        import jax
        import jax.numpy as jnp
        _gk = jax.random.key(seed)
        x = -0.0002949 + 1 * jax.random.normal(jax.random.fold_in(_gk, 1), (1250, 512), jnp.float32)
        src = jax.random.randint(jax.random.fold_in(_gk, 2), (20000,), 0, 1250, jnp.int32)
        dst = jax.random.randint(jax.random.fold_in(_gk, 3), (20000,), 0, 1250, jnp.int32)
        _o = jnp.argsort(dst, stable=True)
        src = src[_o]
        dst = dst[_o]
        edge_attr_8 = 0.000735704 + 1.0001 * jax.random.normal(jax.random.fold_in(_gk, 11), (20000, 8), jnp.float32)
        node_vec1 = jax.random.uniform(jax.random.fold_in(_gk, 13), (1250, 1), jnp.float32, 0.0, 0.999957)
        return (x, src, dst, edge_attr_8, node_vec1)
    x, src, dst, edge_attr_8, node_vec1 = _rec_inputs()

    def _L0_gnn_setup():
        import jax, jax.numpy as jnp
        import numpy as np
        N_NODES = 40962
        LATENT_DIM = 512
        N_EDGES = 81924
        NUM_BLOCKS = 4
        NUM_HEADS = 4
        NUM_FREQ = 32
        BASE_PERIOD = 16
        NOISE_EMB_DIM = 16
        EPS = 1e-05

        def _cond_layer_norm(x, cond, sw, sb, bw, bb):
            mu = jnp.mean(x, axis=-1, keepdims=True)
            var = jnp.var(x, axis=-1, keepdims=True)
            xn = (x - mu) * jax.lax.rsqrt(var + EPS)
            scale = cond @ sw + sb
            bias = cond @ bw + bb
            return xn * (1.0 + scale) + bias

        def _sparse_attention(x, src, dst, wq, bq, wk, bk, wv, bv, wo, bo):
            N, D = x.shape
            H, Dh = (NUM_HEADS, D // NUM_HEADS)
            q = (x @ wq + bq).reshape(N, H, Dh) * Dh ** (-0.5)
            k = (x @ wk + bk).reshape(N, H, Dh)
            v = (x @ wv + bv).reshape(N, H, Dh)
            scores = jnp.einsum('ehd,ehd->eh', q[src], k[dst])
            smax = jax.ops.segment_max(scores, src, num_segments=N)
            ex = jnp.exp(scores - smax[src])
            denom = jax.ops.segment_sum(ex, src, num_segments=N)
            attn = ex / denom[src]
            out = jax.ops.segment_sum(attn[:, :, None] * v[dst], src, num_segments=N)
            return out.reshape(N, D) @ wo + bo

        def _forward(x, edge_index, noise_levels, f_w1, f_b1, f_w2, f_b2, s1_w, s1_b, b1_w, b1_b, wq, bq, wk, bk, wv, bv, wo, bo, s2_w, s2_b, b2_w, b2_b, m_w1, m_b1, m_w2, m_b2):
            src, dst = (edge_index[0], edge_index[1])
            freqs = jnp.arange(1, NUM_FREQ + 1, dtype=x.dtype) * (2.0 * np.pi / BASE_PERIOD)
            ph = noise_levels * freqs
            emb = jnp.concatenate([jnp.sin(ph), jnp.cos(ph)], axis=-1)
            cond = jax.nn.silu(emb @ f_w1 + f_b1) @ f_w2 + f_b2
            for i in range(NUM_BLOCKS):
                y = _cond_layer_norm(x, cond, s1_w[i], s1_b[i], b1_w[i], b1_b[i])
                y = _sparse_attention(y, src, dst, wq[i], bq[i], wk[i], bk[i], wv[i], bv[i], wo[i], bo[i])
                x = x + y
                y = _cond_layer_norm(x, cond, s2_w[i], s2_b[i], b2_w[i], b2_b[i])
                y = jax.nn.relu(y @ m_w1[i] + m_b1[i]) @ m_w2[i] + m_b2[i]
                x = x + y
            return x
        key = jax.random.key(seed)
        ks = jax.random.split(key, 20)

        def w(k, shape, s=0.02):
            return jax.random.normal(k, shape, dtype=jnp.float32) * s
        D, B, C = (LATENT_DIM, NUM_BLOCKS, NOISE_EMB_DIM)
        z = lambda *s: jnp.zeros(s, jnp.float32)
        return {'latent_mesh_nodes': jax.random.normal(ks[0], (N_NODES, D), dtype=jnp.float32), 'edge_index': jax.random.randint(ks[1], (2, N_EDGES), 0, N_NODES, dtype=jnp.int32), 'noise_levels': jax.random.uniform(ks[2], (N_NODES, 1), dtype=jnp.float32), 'f_w1': w(ks[3], (2 * NUM_FREQ, C)), 'f_b1': z(C), 'f_w2': w(ks[4], (C, C)), 'f_b2': z(C), 's1_w': w(ks[5], (B, C, D)), 's1_b': z(B, D), 'b1_w': w(ks[6], (B, C, D)), 'b1_b': z(B, D), 'wq': w(ks[7], (B, D, D)), 'bq': z(B, D), 'wk': w(ks[8], (B, D, D)), 'bk': z(B, D), 'wv': w(ks[9], (B, D, D)), 'bv': z(B, D), 'wo': w(ks[10], (B, D, D)), 'bo': z(B, D), 's2_w': w(ks[11], (B, C, D)), 's2_b': z(B, D), 'b2_w': w(ks[12], (B, C, D)), 'b2_b': z(B, D), 'm_w1': w(ks[13], (B, D, D)), 'm_b1': z(B, D), 'm_w2': w(ks[14], (B, D, D)), 'm_b2': z(B, D)}
    _L0_gnn_all = _L0_gnn_setup()
    _L0_gnn_in = {k: v for k, v in _L0_gnn_all.items() if k in ('f_w1', 'f_b1', 'f_w2', 'f_b2', 's1_w', 's1_b', 'b1_w', 'b1_b', 'wq', 'bq', 'wk', 'bk', 'wv', 'bv', 'wo', 'bo', 's2_w', 's2_b', 'b2_w', 'b2_b', 'm_w1', 'm_b1', 'm_w2', 'm_b2')}
    del _L0_gnn_all

    def _L1_gnn_setup():
        import jax, jax.numpy as jnp
        import numpy as np
        N = 6250
        E = 20000
        D = 512
        H = 512
        NEG_SLOPE = 0.01

        def _cheb_norm(src, dst, n):
            deg = jax.ops.segment_sum(jnp.ones((src.shape[0],), jnp.float32), src, num_segments=n)
            dinv = jnp.where(deg > 0, jax.lax.rsqrt(jnp.maximum(deg, 1.0)), 0.0)
            return -dinv[src] * dinv[dst]

        def _cheb_conv(x, src, dst, norm, W0, W1, b):

            def prop(h):
                return jax.ops.segment_sum(h[src] * norm[:, None], dst, num_segments=x.shape[0])
            out = x @ W0
            tx1 = prop(x)
            out = out + tx1 @ W1
            return out + b

        def _layer_norm(x, gamma, beta, eps=1e-05):
            mu = jnp.mean(x, axis=-1, keepdims=True)
            var = jnp.mean(jnp.square(x - mu), axis=-1, keepdims=True)
            return (x - mu) * jax.lax.rsqrt(var + eps) * gamma + beta
        key = jax.random.key(seed)
        ks = jax.random.split(key, 8)
        s_in = 1.0 / np.sqrt(D)
        s_h = 1.0 / np.sqrt(H)
        x = jax.random.normal(ks[0], (N, D), jnp.float32)
        edge_index = jax.random.randint(ks[1], (2, E), 0, N, dtype=jnp.int64)
        return {'x': x, 'W1_0': jax.random.normal(ks[2], (D, H), jnp.float32) * s_in, 'W1_1': jax.random.normal(ks[3], (D, H), jnp.float32) * s_in, 'b1': jnp.zeros((H,), jnp.float32), 'gamma': jnp.ones((H,), jnp.float32), 'beta': jnp.zeros((H,), jnp.float32), 'W2_0': jax.random.normal(ks[4], (H, H), jnp.float32) * s_h, 'W2_1': jax.random.normal(ks[5], (H, H), jnp.float32) * s_h, 'b2': jnp.zeros((H,), jnp.float32), 'edge_index': edge_index}
    _L1_gnn_all = _L1_gnn_setup()
    _L1_gnn_in = {k: v for k, v in _L1_gnn_all.items() if k in ('W1_0', 'W1_1', 'b1', 'gamma', 'beta', 'W2_0', 'W2_1', 'b2')}
    del _L1_gnn_all

    def _L2_gnn_setup():
        import jax, jax.numpy as jnp
        import numpy as np
        L, E = (2500, 40000)
        C, HID, H = (512, 1024, 8)
        D = C // H
        EPS = 1e-05

        def _layernorm(x, g, b):
            mu = jnp.mean(x, axis=-1, keepdims=True)
            var = jnp.mean(jnp.square(x - mu), axis=-1, keepdims=True)
            return (x - mu) * jax.lax.rsqrt(var + EPS) * g + b
        key = jax.random.key(seed)
        ks = jax.random.split(key, 12)
        s_c = 1.0 / np.sqrt(C)
        s_h = 1.0 / np.sqrt(HID)
        inp = {'x': jax.random.normal(ks[0], (L, C), jnp.float32), 'edge_index': jax.random.randint(ks[1], (2, E), 0, L, jnp.int64), 'att_bias': jax.random.normal(ks[2], (E, H), jnp.float32), 'Wq': jax.random.normal(ks[3], (C, C), jnp.float32) * s_c, 'bq': jnp.zeros((C,), jnp.float32), 'Wk': jax.random.normal(ks[4], (C, C), jnp.float32) * s_c, 'bk': jnp.zeros((C,), jnp.float32), 'Wv': jax.random.normal(ks[5], (C, C), jnp.float32) * s_c, 'bv': jnp.zeros((C,), jnp.float32), 'Wo': jax.random.normal(ks[6], (C, C), jnp.float32) * s_c, 'bo': jnp.zeros((C,), jnp.float32), 'ln_att_g': jnp.ones((C,), jnp.float32), 'ln_att_b': jnp.zeros((C,), jnp.float32), 'ln_ff_g': jnp.ones((C,), jnp.float32), 'ln_ff_b': jnp.zeros((C,), jnp.float32), 'W1': jax.random.normal(ks[7], (HID, C), jnp.float32) * s_c, 'b1': jnp.zeros((HID,), jnp.float32), 'W2': jax.random.normal(ks[8], (C, HID), jnp.float32) * s_h, 'b2': jnp.zeros((C,), jnp.float32)}
        return inp
    _L2_gnn_all = _L2_gnn_setup()
    _L2_gnn_in = {k: v for k, v in _L2_gnn_all.items() if k in ('Wq', 'bq', 'Wk', 'bk', 'Wv', 'bv', 'Wo', 'bo', 'ln_att_g', 'ln_att_b', 'ln_ff_g', 'ln_ff_b', 'W1', 'b1', 'W2', 'b2')}
    del _L2_gnn_all

    def _L3_gnn_setup():
        import jax, jax.numpy as jnp
        import numpy as np
        N = 6250
        E = 50000
        D_IN = 512
        D_HID = 256
        D_OUT = 512
        key = jax.random.key(seed)
        k1, k2, k3, k4 = jax.random.split(key, 4)
        x = jax.random.normal(k1, (N, D_IN), dtype=jnp.float32)
        edge_index = jax.random.randint(k2, (2, E), 0, N, dtype=jnp.int64)
        W1 = jax.random.normal(k3, (D_IN, D_HID), dtype=jnp.float32) * (1.0 / np.sqrt(D_IN))
        b1 = jnp.zeros((D_HID,), dtype=jnp.float32)
        W2 = jax.random.normal(k4, (D_HID, D_OUT), dtype=jnp.float32) * (1.0 / np.sqrt(D_HID))
        b2 = jnp.zeros((D_OUT,), dtype=jnp.float32)
        return {'x': x, 'edge_index': edge_index, 'W1': W1, 'b1': b1, 'W2': W2, 'b2': b2}
    _L3_gnn_all = _L3_gnn_setup()
    _L3_gnn_in = {k: v for k, v in _L3_gnn_all.items() if k in ('W1', 'b1', 'W2', 'b2')}
    del _L3_gnn_all
    return {'x': x, 'src': src, 'dst': dst, 'edge_attr_8': edge_attr_8, 'node_vec1': node_vec1, 'L0_gnn_f_w1': _L0_gnn_in['f_w1'], 'L0_gnn_f_b1': _L0_gnn_in['f_b1'], 'L0_gnn_f_w2': _L0_gnn_in['f_w2'], 'L0_gnn_f_b2': _L0_gnn_in['f_b2'], 'L0_gnn_s1_w': _L0_gnn_in['s1_w'], 'L0_gnn_s1_b': _L0_gnn_in['s1_b'], 'L0_gnn_b1_w': _L0_gnn_in['b1_w'], 'L0_gnn_b1_b': _L0_gnn_in['b1_b'], 'L0_gnn_wq': _L0_gnn_in['wq'], 'L0_gnn_bq': _L0_gnn_in['bq'], 'L0_gnn_wk': _L0_gnn_in['wk'], 'L0_gnn_bk': _L0_gnn_in['bk'], 'L0_gnn_wv': _L0_gnn_in['wv'], 'L0_gnn_bv': _L0_gnn_in['bv'], 'L0_gnn_wo': _L0_gnn_in['wo'], 'L0_gnn_bo': _L0_gnn_in['bo'], 'L0_gnn_s2_w': _L0_gnn_in['s2_w'], 'L0_gnn_s2_b': _L0_gnn_in['s2_b'], 'L0_gnn_b2_w': _L0_gnn_in['b2_w'], 'L0_gnn_b2_b': _L0_gnn_in['b2_b'], 'L0_gnn_m_w1': _L0_gnn_in['m_w1'], 'L0_gnn_m_b1': _L0_gnn_in['m_b1'], 'L0_gnn_m_w2': _L0_gnn_in['m_w2'], 'L0_gnn_m_b2': _L0_gnn_in['m_b2'], 'L1_gnn_W1_0': _L1_gnn_in['W1_0'], 'L1_gnn_W1_1': _L1_gnn_in['W1_1'], 'L1_gnn_b1': _L1_gnn_in['b1'], 'L1_gnn_gamma': _L1_gnn_in['gamma'], 'L1_gnn_beta': _L1_gnn_in['beta'], 'L1_gnn_W2_0': _L1_gnn_in['W2_0'], 'L1_gnn_W2_1': _L1_gnn_in['W2_1'], 'L1_gnn_b2': _L1_gnn_in['b2'], 'L2_gnn_Wq': _L2_gnn_in['Wq'], 'L2_gnn_bq': _L2_gnn_in['bq'], 'L2_gnn_Wk': _L2_gnn_in['Wk'], 'L2_gnn_bk': _L2_gnn_in['bk'], 'L2_gnn_Wv': _L2_gnn_in['Wv'], 'L2_gnn_bv': _L2_gnn_in['bv'], 'L2_gnn_Wo': _L2_gnn_in['Wo'], 'L2_gnn_bo': _L2_gnn_in['bo'], 'L2_gnn_ln_att_g': _L2_gnn_in['ln_att_g'], 'L2_gnn_ln_att_b': _L2_gnn_in['ln_att_b'], 'L2_gnn_ln_ff_g': _L2_gnn_in['ln_ff_g'], 'L2_gnn_ln_ff_b': _L2_gnn_in['ln_ff_b'], 'L2_gnn_W1': _L2_gnn_in['W1'], 'L2_gnn_b1': _L2_gnn_in['b1'], 'L2_gnn_W2': _L2_gnn_in['W2'], 'L2_gnn_b2': _L2_gnn_in['b2'], 'L3_gnn_W1': _L3_gnn_in['W1'], 'L3_gnn_b1': _L3_gnn_in['b1'], 'L3_gnn_W2': _L3_gnn_in['W2'], 'L3_gnn_b2': _L3_gnn_in['b2']}

def reference(x, src, dst, edge_attr_8, node_vec1, L0_gnn_f_w1, L0_gnn_f_b1, L0_gnn_f_w2, L0_gnn_f_b2, L0_gnn_s1_w, L0_gnn_s1_b, L0_gnn_b1_w, L0_gnn_b1_b, L0_gnn_wq, L0_gnn_bq, L0_gnn_wk, L0_gnn_bk, L0_gnn_wv, L0_gnn_bv, L0_gnn_wo, L0_gnn_bo, L0_gnn_s2_w, L0_gnn_s2_b, L0_gnn_b2_w, L0_gnn_b2_b, L0_gnn_m_w1, L0_gnn_m_b1, L0_gnn_m_w2, L0_gnn_m_b2, L1_gnn_W1_0, L1_gnn_W1_1, L1_gnn_b1, L1_gnn_gamma, L1_gnn_beta, L1_gnn_W2_0, L1_gnn_W2_1, L1_gnn_b2, L2_gnn_Wq, L2_gnn_bq, L2_gnn_Wk, L2_gnn_bk, L2_gnn_Wv, L2_gnn_bv, L2_gnn_Wo, L2_gnn_bo, L2_gnn_ln_att_g, L2_gnn_ln_att_b, L2_gnn_ln_ff_g, L2_gnn_ln_ff_b, L2_gnn_W1, L2_gnn_b1, L2_gnn_W2, L2_gnn_b2, L3_gnn_W1, L3_gnn_b1, L3_gnn_W2, L3_gnn_b2):
    import jax
    import jax.numpy as jnp

    def _L0_gnn_ref(latent_mesh_nodes, edge_index, noise_levels, f_w1, f_b1, f_w2, f_b2, s1_w, s1_b, b1_w, b1_b, wq, bq, wk, bk, wv, bv, wo, bo, s2_w, s2_b, b2_w, b2_b, m_w1, m_b1, m_w2, m_b2):
        import jax, jax.numpy as jnp
        import numpy as np
        N_NODES = 40962
        LATENT_DIM = 512
        N_EDGES = 81924
        NUM_BLOCKS = 4
        NUM_HEADS = 4
        NUM_FREQ = 32
        BASE_PERIOD = 16
        NOISE_EMB_DIM = 16
        EPS = 1e-05

        def _cond_layer_norm(x, cond, sw, sb, bw, bb):
            mu = jnp.mean(x, axis=-1, keepdims=True)
            var = jnp.var(x, axis=-1, keepdims=True)
            xn = (x - mu) * jax.lax.rsqrt(var + EPS)
            scale = cond @ sw + sb
            bias = cond @ bw + bb
            return xn * (1.0 + scale) + bias

        def _sparse_attention(x, src, dst, wq, bq, wk, bk, wv, bv, wo, bo):
            N, D = x.shape
            H, Dh = (NUM_HEADS, D // NUM_HEADS)
            q = (x @ wq + bq).reshape(N, H, Dh) * Dh ** (-0.5)
            k = (x @ wk + bk).reshape(N, H, Dh)
            v = (x @ wv + bv).reshape(N, H, Dh)
            scores = jnp.einsum('ehd,ehd->eh', q[src], k[dst])
            smax = jax.ops.segment_max(scores, src, num_segments=N)
            ex = jnp.exp(scores - smax[src])
            denom = jax.ops.segment_sum(ex, src, num_segments=N)
            attn = ex / denom[src]
            out = jax.ops.segment_sum(attn[:, :, None] * v[dst], src, num_segments=N)
            return out.reshape(N, D) @ wo + bo

        def _forward(x, edge_index, noise_levels, f_w1, f_b1, f_w2, f_b2, s1_w, s1_b, b1_w, b1_b, wq, bq, wk, bk, wv, bv, wo, bo, s2_w, s2_b, b2_w, b2_b, m_w1, m_b1, m_w2, m_b2):
            src, dst = (edge_index[0], edge_index[1])
            freqs = jnp.arange(1, NUM_FREQ + 1, dtype=x.dtype) * (2.0 * np.pi / BASE_PERIOD)
            ph = noise_levels * freqs
            emb = jnp.concatenate([jnp.sin(ph), jnp.cos(ph)], axis=-1)
            cond = jax.nn.silu(emb @ f_w1 + f_b1) @ f_w2 + f_b2
            for i in range(NUM_BLOCKS):
                y = _cond_layer_norm(x, cond, s1_w[i], s1_b[i], b1_w[i], b1_b[i])
                y = _sparse_attention(y, src, dst, wq[i], bq[i], wk[i], bk[i], wv[i], bv[i], wo[i], bo[i])
                x = x + y
                y = _cond_layer_norm(x, cond, s2_w[i], s2_b[i], b2_w[i], b2_b[i])
                y = jax.nn.relu(y @ m_w1[i] + m_b1[i]) @ m_w2[i] + m_b2[i]
                x = x + y
            return x
        return _forward(latent_mesh_nodes, edge_index, noise_levels, f_w1, f_b1, f_w2, f_b2, s1_w, s1_b, b1_w, b1_b, wq, bq, wk, bk, wv, bv, wo, bo, s2_w, s2_b, b2_w, b2_b, m_w1, m_b1, m_w2, m_b2)

    def _L1_gnn_ref(x, W1_0, W1_1, b1, gamma, beta, W2_0, W2_1, b2, edge_index):
        import jax, jax.numpy as jnp
        import numpy as np
        N = 6250
        E = 20000
        D = 512
        H = 512
        NEG_SLOPE = 0.01

        def _cheb_norm(src, dst, n):
            deg = jax.ops.segment_sum(jnp.ones((src.shape[0],), jnp.float32), src, num_segments=n)
            dinv = jnp.where(deg > 0, jax.lax.rsqrt(jnp.maximum(deg, 1.0)), 0.0)
            return -dinv[src] * dinv[dst]

        def _cheb_conv(x, src, dst, norm, W0, W1, b):

            def prop(h):
                return jax.ops.segment_sum(h[src] * norm[:, None], dst, num_segments=x.shape[0])
            out = x @ W0
            tx1 = prop(x)
            out = out + tx1 @ W1
            return out + b

        def _layer_norm(x, gamma, beta, eps=1e-05):
            mu = jnp.mean(x, axis=-1, keepdims=True)
            var = jnp.mean(jnp.square(x - mu), axis=-1, keepdims=True)
            return (x - mu) * jax.lax.rsqrt(var + eps) * gamma + beta
        src, dst = (edge_index[0], edge_index[1])
        norm = _cheb_norm(src, dst, x.shape[0])
        h = _cheb_conv(x, src, dst, norm, W1_0, W1_1, b1)
        h = _layer_norm(h, gamma, beta)
        h = jnp.where(h >= 0, h, NEG_SLOPE * h)
        out = _cheb_conv(h, src, dst, norm, W2_0, W2_1, b2)
        return out

    def _L2_gnn_ref(x, edge_index, att_bias, Wq, bq, Wk, bk, Wv, bv, Wo, bo, ln_att_g, ln_att_b, ln_ff_g, ln_ff_b, W1, b1, W2, b2):
        import jax, jax.numpy as jnp
        import numpy as np
        L, E = (2500, 40000)
        C, HID, H = (512, 1024, 8)
        D = C // H
        EPS = 1e-05

        def _layernorm(x, g, b):
            mu = jnp.mean(x, axis=-1, keepdims=True)
            var = jnp.mean(jnp.square(x - mu), axis=-1, keepdims=True)
            return (x - mu) * jax.lax.rsqrt(var + EPS) * g + b
        n = x.shape[0]
        src = edge_index[0]
        dst = edge_index[1]
        z = _layernorm(x, ln_att_g, ln_att_b)
        q = (z @ Wq.T + bq).reshape(n, H, D)
        k = (z @ Wk.T + bk).reshape(n, H, D)
        v = (z @ Wv.T + bv).reshape(n, H, D)
        s = jnp.einsum('ehd,ehd->eh', q[src], k[dst]) / np.sqrt(D) + att_bias
        m = jax.ops.segment_max(s, src, num_segments=n)
        p = jnp.exp(s - m[src])
        denom = jax.ops.segment_sum(p, src, num_segments=n)
        alpha = p / jnp.where(denom[src] == 0, 1.0, denom[src])
        agg = jax.ops.segment_sum(alpha[:, :, None] * v[dst], src, num_segments=n)
        att = agg.reshape(n, C) @ Wo.T + bo
        x = x + att
        z = _layernorm(x, ln_ff_g, ln_ff_b)
        h = jax.nn.silu(z @ W1.T + b1)
        ff = h @ W2.T + b2
        return x + ff

    def _L3_gnn_ref(x, edge_index, W1, b1, W2, b2):
        import jax, jax.numpy as jnp
        import numpy as np
        N = 6250
        E = 50000
        D_IN = 512
        D_HID = 256
        D_OUT = 512
        h = jax.nn.relu(x @ W1 + b1) @ W2 + b2
        row, col = (edge_index[0], edge_index[1])
        agg = jax.ops.segment_sum(h[col], row, num_segments=h.shape[0])
        return h + agg
    edge_index = jnp.stack([src, dst])
    h = jnp.maximum(_layernorm(x, axis=-1), 0.0)
    x = x + _L0_gnn_ref(h, edge_index, node_vec1, L0_gnn_f_w1, L0_gnn_f_b1, L0_gnn_f_w2, L0_gnn_f_b2, L0_gnn_s1_w, L0_gnn_s1_b, L0_gnn_b1_w, L0_gnn_b1_b, L0_gnn_wq, L0_gnn_bq, L0_gnn_wk, L0_gnn_bk, L0_gnn_wv, L0_gnn_bv, L0_gnn_wo, L0_gnn_bo, L0_gnn_s2_w, L0_gnn_s2_b, L0_gnn_b2_w, L0_gnn_b2_b, L0_gnn_m_w1, L0_gnn_m_b1, L0_gnn_m_w2, L0_gnn_m_b2)
    h = jnp.maximum(_layernorm(x, axis=-1), 0.0)
    x = x + _L1_gnn_ref(h, L1_gnn_W1_0, L1_gnn_W1_1, L1_gnn_b1, L1_gnn_gamma, L1_gnn_beta, L1_gnn_W2_0, L1_gnn_W2_1, L1_gnn_b2, edge_index)
    h = jnp.maximum(_layernorm(x, axis=-1), 0.0)
    x = x + _L2_gnn_ref(h, edge_index, edge_attr_8, L2_gnn_Wq, L2_gnn_bq, L2_gnn_Wk, L2_gnn_bk, L2_gnn_Wv, L2_gnn_bv, L2_gnn_Wo, L2_gnn_bo, L2_gnn_ln_att_g, L2_gnn_ln_att_b, L2_gnn_ln_ff_g, L2_gnn_ln_ff_b, L2_gnn_W1, L2_gnn_b1, L2_gnn_W2, L2_gnn_b2)
    h = jnp.maximum(_layernorm(x, axis=-1), 0.0)
    x = x + _L3_gnn_ref(h, edge_index, L3_gnn_W1, L3_gnn_b1, L3_gnn_W2, L3_gnn_b2)
    return x

_drawn_inputs = setup_inputs


def setup_inputs(seed=0):
    import zlib

    import numpy as np

    out = dict(_drawn_inputs(seed))
    spreads = {'L0_gnn_f_b1': (0.0, 0.8),
     'L0_gnn_f_b2': (0.0, 0.8),
     'L0_gnn_s1_b': (0.0, 0.8),
     'L0_gnn_b1_b': (0.0, 0.371),
     'L0_gnn_bq': (0.0, 0.8),
     'L0_gnn_bk': (0.0, 0.8),
     'L0_gnn_bv': (0.0, 0.1),
     'L0_gnn_bo': (0.0, 0.1),
     'L0_gnn_s2_b': (0.0, 0.8),
     'L0_gnn_b2_b': (0.0, 0.663),
     'L0_gnn_m_b1': (0.0, 0.295),
     'L0_gnn_m_b2': (0.0, 0.1),
     'L1_gnn_b1': (0.0, 0.1),
     'L1_gnn_gamma': (1.0, 0.2),
     'L1_gnn_beta': (0.0, 0.1),
     'L1_gnn_b2': (0.0, 0.1),
     'L2_gnn_bq': (0.0, 0.8),
     'L2_gnn_bk': (0.0, 0.8),
     'L2_gnn_bv': (0.0, 0.1),
     'L2_gnn_bo': (0.0, 0.1),
     'L2_gnn_ln_att_g': (1.0, 0.2),
     'L2_gnn_ln_att_b': (0.0, 0.1),
     'L2_gnn_ln_ff_g': (1.0, 0.6),
     'L2_gnn_ln_ff_b': (0.0, 0.542),
     'L2_gnn_b1': (0.0, 0.456),
     'L2_gnn_b2': (0.0, 0.299),
     'L3_gnn_b1': (0.0, 0.1),
     'L3_gnn_b2': (0.0, 0.1)}
    factors = {'node_vec1': 8.0,
     'L0_gnn_f_w1': 8.0,
     'L0_gnn_f_w2': 8.0,
     'L0_gnn_s1_w': 8.0,
     'L0_gnn_b1_w': 8.0,
     'L0_gnn_wq': 8.0,
     'L0_gnn_wk': 8.0,
     'L0_gnn_s2_w': 8.0,
     'L0_gnn_b2_w': 8.0}
    for name, (base, spread) in spreads.items():
        noise = np.random.default_rng([zlib.crc32(name.encode()), seed]).standard_normal(out[name].shape)
        drawn = base * np.exp(spread * noise) if base else spread * noise
        out[name] = jnp.asarray(drawn.astype(out[name].dtype))
    for name, factor in factors.items():
        out[name] = (out[name] * factor).astype(out[name].dtype)
    return out
```

```python
import numpy as np
import concourse.bass as bass
from concourse import mybir
from contextlib import ExitStack

F32 = mybir.dt.float32
BF16 = mybir.dt.bfloat16
I32 = mybir.dt.int32
U32 = mybir.dt.uint32
ALU = mybir.AluOpType
ACT = mybir.ActivationFunctionType
AX = mybir.AxisListType

N, D, E = 1250, 512, 20000
P, NT = 125, 10
KC = D // 128
EC = E // P
G = 8
NG = EC // G
BH = 8
LAYERS = 4
CHUNKS = [(0, 500), (500, 500), (1000, 250)]
NO_EDGE = -1.0e30
EPS = 1e-5
CD = 16
WP = 3 * BH + 1
HEADROOM = 40.0
V_LOOP_STEPS = 26


class At:

    def __init__(self, base, per=0, layer=None):
        self.base, self.per, self.layer = base, per, layer

    def value(self, k):
        return self.base + k if self.layer is None else self.layer * self.per + (self.base + k)


def wait(eng, sem, at, k=0):
    if at.layer is not None:
        assert at.base + k > 0, "a loop's wait must be positive in its first turn"
    if at.base + k > 0:
        eng.wait_ge(sem, at.value(k))


def build(nc, A):
    ctx = ExitStack()
    with ctx:
        WORDS = 53200
        arena = ctx.enter_context(nc.sbuf_tensor("arena", [128, WORDS], F32))
        top = [0]

        def region(words):
            a = top[0]
            top[0] += words
            assert top[0] <= WORDS, top[0]
            return a

        def view(at, rows, *shape):
            ap = arena[0:rows, at:at + int(np.prod(shape))]
            if len(shape) == 2:
                ap = ap.rearrange("p (a b) -> p a b", a=shape[0])
            if len(shape) == 3:
                ap = ap.rearrange("p (a b c) -> p a b c", a=shape[0], b=shape[1])
            return ap

        aX, aV = region(NT * D), region(NT * D)
        aT1, aT2, aT3 = region(KC * N), region(KC * N), region(KC * N)
        aP, aPT, aLC = region(2 * N), region(2 * N), region(2 * N)
        aW = region(4 * KC * D)
        aR = region(BH * N)
        aO = region(D)
        SMALL = 1500
        X = view(aX, P, NT, D)
        V = view(aV, P, NT, D)
        T1 = view(aT1, 128, KC, N)
        T2 = view(aT2, 128, KC, N)
        T3 = view(aT3, 128, KC, N)
        H8 = view(aT2, 128, 2 * KC, N)
        DENSE = view(aT3, P, NT, N)
        LC = view(aLC, P, 2, N)
        PR = view(aP, P, 2, N)
        PT = view(aPT, P, 2, NT * P)
        W = view(aW, 128, 4, KC * D)
        BIA = [view(aLC, P, N, BH), view(aR, P, N, BH)]
        CR = view(aW + 2 * KC * D, P, 2, N)
        OS = view(aO, P, D)
        r = aR
        COND = view(r, CD + 2, N)
        DINVB = view(r, P, N); r += N
        CW = [view(r, CD + 2, 2 * D), view(r + 2 * D, CD + 2, 2 * D)]; r += 4 * D
        PHASE = view(r, 64, 2, N)
        XN = view(r, P, 2, D); r += 2 * D
        Y = view(r, P, 2, D); r += 2 * D
        r += 1000
        ROWS = view(r, 1, 3 * D); r += 3 * D
        GB = view(r, P, 2, D); r += 2 * D
        NEG = view(r, P, 625); r += 625
        assert r <= aR + BH * N
        s = [region(SMALL)]

        def small(rows, *shape):
            v = view(s[0], rows, *shape)
            s[0] += int(np.prod(shape))
            assert s[0] <= aO + D + SMALL, s[0]
            return v

        IDENT, ONES = small(128, 128), small(128, 128)
        COLB, QBS = small(128, 12), small(128, 4)
        BN, MV = small(P, NT, 6), small(P, NT, 2)
        VARC = small(P, NT)
        STD, RSTD, NMR = small(P, NT), small(P, NT), small(P, NT)
        DEG, FLAG, DINV, DEG1 = small(P, NT), small(P, NT), small(P, NT), small(P, NT)
        EPSC = small(128, 1)
        MX, NMX = small(P, 2), small(P, 2)
        DEN, RD = small(P, 2, BH), small(P, 2, BH)
        GMX, GALL, SHIFT, BACK = small(P, 1), small(P, 1), small(P, 1), small(P, 1)
        FRQ = small(64, 5)
        FW1, FW2, FB = small(64, CD), small(CD, CD), small(CD, 2)
        LATE, IDLE = small(P, G), small(P, 1)
        KEYI, WIDX = small(P, EC).bitcast(I32), small(P, EC).bitcast(I32)
        MRG = small(P, 5, G * BH)
        NGRP = small(P, EC)

        e = aV
        KEY, SPARE, KEYC = view(e, P, EC), view(e + EC, P, EC), view(e + 2 * EC, P, EC); e += 3 * EC
        SRC, DST, SRCG, DSTG = [view(e + k * EC, P, EC) for k in range(4)]; e += 4 * EC
        SRCI, DSTI, SRCJ, DSTJ = [view(e + k * EC, P, EC).bitcast(I32) for k in range(4)]; e += 4 * EC
        IDX = view(e, P, EC); e += EC
        CNT = view(e, P, EC); e += EC
        EX = view(e, P, EC * BH); e += EC * BH
        TRI = view(e, P, P); e += P
        TRIB = view(e, P, 64).bitcast(BF16)[:, 0:P]; e += 64
        assert e <= aV + NT * D
        e = aT1
        KEYB = view(e, P, 2, G * P); e += 2 * G * P
        EPART = view(e, P, EC * WP // 2).bitcast(BF16).rearrange("p (c w) -> p c w", w=WP); e += EC * WP // 2
        ATTR = view(e, P, EC * BH); e += EC * BH
        EQW = G * (G * P + P)
        EQ = [view(e + k * EQW // 2, P, EQW // 2).bitcast(BF16) for k in range(2)]; e += EQW
        assert e <= aP
        e = aPT
        SUMS = view(e, P, EC, WP); e += EC * WP
        assert e <= aW
        EQD = [view(aP + k * G * P // 2, P, G * P // 2).bitcast(BF16).rearrange("p (c x) -> p c x", c=G) for k in range(2)]
        TMP = view(aP + G * P, P, EC * BH)
        ZERO = view(aW, P, N)

        banks = ctx.enter_context(nc.psum_tensor("banks", [128, 8, 512], F32))

        def bank(b, rows=P, n=512):
            return banks[0:rows, b, 0:n]

        def halves(k):
            return banks[0:P, 3 * k:3 * k + 3, :].rearrange("p b x -> p (b x)").rearrange("p (h x) -> p h x", x=256)[:, 0:5, 0:250]

        def pairs(ap):
            return ap.rearrange("p (h x) -> p h x", x=250)

        cnt_tab = nc.dram_tensor("cnt_tab", [N * N + E, 1], F32)
        bia_tab = nc.dram_tensor("bia_tab", [N * N, BH], F32)
        lc_tab = nc.dram_tensor("lc_tab", [N, N], F32)
        key_dram = nc.dram_tensor("key_dram", [E], F32)
        dinv_dram = nc.dram_tensor("dinv_dram", [NT, P], F32)
        x_dram = nc.dram_tensor("x_dram", [N, D], F32)
        cnt_rows = cnt_tab[0:N * N, :].rearrange("(t p d) o -> t p (d o)", t=NT, p=P)
        lc_rows = lc_tab[:, :].rearrange("(t p) d -> t p d", p=P)
        bia_rows = bia_tab[:, :].rearrange("(t p d) h -> t p (d h)", t=NT, p=P)
        x_rows = A["x"].rearrange("(t p) d -> t p d", p=P)
        xs_rows = x_dram[:, :].rearrange("(t p) d -> t p d", p=P)
        out_rows = A["out"].rearrange("(t p) d -> t p d", p=P)

        names = """edges_in noise_in zero_ready cnt_zeroed neg_ready bia_cleared keyc_ready keyc_out keyb_in0 keyb_in1
            consts_ready gmax_ready gmax_all shift_ready exp_ready eq_ready eqd_ready grp_sum sums_out idx_ready
            counted lsum_ready lse_log lse_ready gathered mrg_diff mrg_exp mrg_log mrg_ready scattered
            cnt_in0 cnt_in1 lc_pre lc_log lc_ready lc_out phase_ready emb_ready emb_mm emb_act cond_mm cond_built cw_clear
            x_in res_in0 res_in1 stats_ready std_ready rstd_ready xn_ready cond_ready y_ready yT_ready yT_out
            w0_in w1_in w2_in w3_in cw0_in cw1_in row_in row2_in col_in gb_in gb_used qbs_ready grp_done out_a out_d upd_done x_upd
            lct_in0 lct_in1 bia_in0 bia_in1 s_done max_ready negmax p_ready t_done t_out_a t_out_d pv_done o_ready oT_done oT_out
            deg_clip deg_sqrt dinv_ready dinv_out dinv_in dense_in dense_ready x_saved c_in0 c_in1 ct_done
            final_ready final_out v_step gate sp_passed""".split()
        S = {n: ctx.enter_context(nc.semaphore(n)) for n in names}
        block = ctx.enter_context(nc.Block())

        timeline = []

        def stage(name, **adds):
            timeline.append((name, adds))

        def norm_stage(name, kind, transposed=True, **more):
            adds = dict(stats_ready=1, std_ready=1, rstd_ready=1, xn_ready=NT, **more)
            if kind != "relu":
                adds.update(y_ready=NT)
            if kind == "cond":
                adds.update(cond_ready=NT)
            if transposed:
                adds.update(yT_ready=NT, yT_out=NT)
            stage(name, **adds)

        def att_stage(name, heads, **more):
            n = heads * NT
            stage(name, s_done=n, max_ready=n, negmax=n, p_ready=n, t_done=n, t_out_a=n, t_out_d=n, pv_done=n,
                  o_ready=NT, oT_done=NT, oT_out=NT, **more)

        stage("start", x_in=16 * NT)
        norm_stage("pre0", "relu", transposed=False)
        stage("loop")
        norm_stage("n1", "cond", cw0_in=16)
        stage("qkv", w0_in=16, w1_in=16, w2_in=16, col_in=16, row_in=16, qbs_ready=1, grp_done=34, out_a=17, out_d=17)
        att_stage("att", 4, lct_in0=8 * NT, lct_in1=8 * NT)
        stage("wo", w3_in=16, upd_done=NT, x_upd=NT)
        norm_stage("n2", "cond", cw1_in=16)
        stage("up", w0_in=16, grp_done=12, out_a=6, out_d=6)
        stage("down", w1_in=16, upd_done=NT, x_upd=NT)
        stage("end")
        stage("res1", res_in0=8 * NT, res_in1=8 * NT, x_upd=NT)
        norm_stage("pre1", "relu")
        stage("dense", dense_in=16, dense_ready=NT)
        stage("prop1", grp_done=12, out_a=6, out_d=6)
        stage("conv1", w0_in=16, w1_in=16, row_in=16, upd_done=NT, x_upd=NT)
        norm_stage("mid1", "affine", gb_in=32)
        stage("prop2", grp_done=12, out_a=6, out_d=6)
        stage("conv2", w2_in=16, w3_in=16, row2_in=16, upd_done=NT, x_upd=NT)
        norm_stage("pre2", "relu", transposed=False)
        norm_stage("z1", "affine", gb_in=32)
        stage("qkv2", w0_in=16, w1_in=16, w2_in=16, col_in=16, row_in=16, qbs_ready=1, grp_done=34, out_a=17, out_d=17)
        att_stage("att2", BH, bia_in0=8 * NT, bia_in1=8 * NT)
        stage("wo2", w3_in=16, row_in=16, upd_done=NT, x_upd=NT)
        norm_stage("z2", "affine", gb_in=32)
        stage("up2", w0_in=16, col_in=16, grp_done=24, out_a=24)
        stage("down2", w2_in=16, upd_done=NT, x_upd=NT)
        stage("res2", res_in0=8 * NT, res_in1=8 * NT, x_upd=NT)
        norm_stage("pre3", "relu")
        stage("r3", w0_in=16, row_in=16, grp_done=NT, out_a=NT // 2, out_d=NT // 2)
        stage("ct", c_in0=8 * NT, c_in1=8 * NT, ct_done=NT, dense_ready=NT)
        stage("prop3", grp_done=6, out_a=3, out_d=3)
        stage("conv3", w1_in=16, gb_in=16, upd_done=NT)
        order = [n for n, _ in timeline]
        per = {n: sum(a.get(n, 0) for _, a in timeline[order.index("loop"):order.index("end")]) for n in names}

        def at(name, layer=None):
            k = order.index(name)
            inside = order.index("loop") < k < order.index("end")
            assert inside == (layer is not None), name

            def get(sem):
                base = sum(a.get(sem, 0) for _, a in timeline[:k])
                if inside:
                    return At(base, per[sem], layer)
                return At(base + (LAYERS - 1) * per[sem] * (k >= order.index("end")))
            return get

        def grp_free(eng, t, g, alternate=True):
            if g < 4:
                return
            if not alternate:
                wait(eng, S["out_a"], t("out_a"), g - 3)
            elif g % 2 == 0:
                wait(eng, S["out_a"], t("out_a"), (g - 4) // 2 + 1)
            else:
                wait(eng, S["out_d"], t("out_d"), (g - 4) // 2 + 1)

        @block.sync
        def _(sp):
            def load(dst, src, name):
                sp.dma_start(dst, src).then_inc(S[name], 16)

            def loop_wait(name, at_, k=0):
                wait(sp, S[name], at_, k)
                sp.sem_inc(S["sp_passed"], 1)

            for dst, key in ((SRCI, "src_pc"), (DSTI, "dst_pc"), (SRCJ, "src_cp"), (DSTJ, "dst_cp"), (ATTR, "edge_attr")):
                load(dst, A[key], "edges_in")
            for i in range(NT):
                load(X[:, i, :], x_rows[i], "x_in")
            load(PHASE[:, 0, :], A["noise"].to_broadcast([64, N]), "noise_in")
            load(FW1, A["f_w1"], "noise_in")
            load(FW2, A["f_w2"], "noise_in")
            load(FB, A["f_b"], "noise_in")
            sp.wait_ge(S["zero_ready"], 1)
            for i in range(NT):
                load(cnt_rows[i], ZERO, "cnt_zeroed")
            load(cnt_tab[N * N:N * N + E, :].rearrange("(p b) o -> p (b o)", p=P), ZERO[:, 0:EC], "cnt_zeroed")
            sp.wait_ge(S["keyc_ready"], 1)
            load(key_dram[:].rearrange("(p c) -> p c", p=P), KEYC, "keyc_out")
            sp.wait_ge(S["keyc_out"], 16)
            kd = key_dram[:].rearrange("(g n) -> g n", g=NG)
            for g in range(NG):
                if g >= 2:
                    sp.wait_ge(S["eq_ready"], g - 1)
                load(KEYB[:, g % 2, :], kd[g:g + 1, :].to_broadcast([P, G * P]), f"keyb_in{g % 2}")
            sp.wait_ge(S["neg_ready"], 1)
            clear = bia_tab[:, :].rearrange("(p a) h -> p (a h)", p=P).rearrange("p (b c) -> p b c", c=625)
            for k in range(4):
                load(clear[:, k * 40:(k + 1) * 40, :], NEG.unsqueeze(1).to_broadcast([P, 40, 625]), "bia_cleared")
            sp.wait_ge(S["counted"], 16 * EC)
            sp.wait_ge(S["lse_ready"], 1)
            for i in range(NT):
                if i >= 2:
                    sp.wait_ge(S["lc_out"], 16 * (i - 1))
                load(LC[:, i % 2, :], cnt_rows[i], f"cnt_in{i % 2}")
                if i >= 1:
                    sp.wait_ge(S["lc_ready"], i)
                    load(lc_rows[i - 1], LC[:, (i - 1) % 2, :], "lc_out")
            sp.wait_ge(S["lc_ready"], NT)
            load(lc_rows[NT - 1], LC[:, (NT - 1) % 2, :], "lc_out")
            sp.wait_ge(S["lc_out"], 16 * NT)
            sp.wait_ge(S["cw_clear"], 1)
            sp.wait_ge(S["grp_sum"], NG)

            with sp.Fori(0, LAYERS) as L:
                w0 = A["w0"][bass.ds(L, 1), :, :, :].rearrange("o m p x -> (o m) p x")
                cw = A["cw"][bass.ds(L, 1), :, :, :].rearrange("o k p x -> (o k) p x")
                load(CW[0][0:CD + 1, :], cw[0], "cw0_in")
                for k in range(3):
                    load(W[:, k, :], w0[k], f"w{k}_in")
                load(COLB, A["colb"][bass.ds(L, 1), :, :].rearrange("o p x -> (o p) x"), "col_in")
                load(ROWS, A["rowb"][bass.ds(L, 1), :], "row_in")
                load(W[:, 3, :], w0[3], "w3_in")
                t = at("n2", L)
                load(CW[1][0:CD + 1, :], cw[1], "cw1_in")
                t = at("att", L)
                for i in range(NT):
                    if i >= 2:
                        loop_wait("max_ready", t("max_ready"), 4 * (i - 1))
                    load(LC[:, i % 2, :], lc_rows[i], f"lct_in{i % 2}")
                    if i == 1:
                        loop_wait("grp_done", t("grp_done"))
                        load(W[:, 0, :], w0[4], "w0_in")
                        load(W[:, 1, :], w0[5], "w1_in")
                t = at("down", L)
                loop_wait("x_upd", t("x_upd"), NT)

            t = at("res1")
            for i in range(NT):
                if i >= 2:
                    wait(sp, S["x_upd"], t("x_upd"), i - 1)
                load(Y[:, i % 2, :], x_rows[i], f"res_in{i % 2}")
            load(DENSE, cnt_rows.rearrange("t p d -> p t d"), "dense_in")
            load(W[:, 0, :], A["w1"][0], "w0_in")
            load(W[:, 1, :], A["w1"][1], "w1_in")
            load(ROWS[:, 0:D], A["l1_b1"], "row_in")
            load(GB[:, 0, :], A["l1_gamma"].to_broadcast([P, D]), "gb_in")
            load(GB[:, 1, :], A["l1_beta"].to_broadcast([P, D]), "gb_in")
            load(W[:, 2, :], A["w1"][2], "w2_in")
            load(W[:, 3, :], A["w1"][3], "w3_in")
            load(ROWS[:, D:2 * D], A["l1_b2"], "row2_in")
            sp.wait_ge(S["dinv_ready"], 1)
            with nc.allow_non_contiguous_dma(reason="ten words of each partition, 5 KB in all"):
                load(dinv_dram[:, :].rearrange("t p -> p t"), DINV, "dinv_out")
            sp.wait_ge(S["dinv_out"], 16)
            load(DINVB, dinv_dram[:, :].rearrange("(o t) p -> o (t p)", o=1).to_broadcast([P, N]), "dinv_in")
            t = at("pre2")
            wait(sp, S["x_upd"], t("x_upd"))
            for i in range(NT):
                load(xs_rows[i], X[:, i, :], "x_saved")
            wait(sp, S["gb_used"], At(0), 1)
            for k in range(2):
                load(GB[:, k, :], A["l2_lnb"][k:k + 1, :].to_broadcast([P, D]), "gb_in")
            for k in range(3):
                load(W[:, k, :], A["w2"][k], f"w{k}_in")
            load(COLB[:, 0:8], A["l2_colb"], "col_in")
            load(ROWS[:, 0:D], A["l2_bv"], "row_in")
            t = at("att2")
            wait(sp, S["grp_done"], t("grp_done"))
            wait(sp, S["yT_out"], t("yT_out"))
            wait(sp, S["out_a"], t("out_a"))
            wait(sp, S["out_d"], t("out_d"))
            sp.wait_ge(S["scattered"], 16 * EC)
            for i in range(NT):
                if i >= 2:
                    wait(sp, S["max_ready"], t("max_ready"), BH * (i - 1))
                load(BIA[i % 2].rearrange("p d h -> p (d h)"), bia_rows[i], f"bia_in{i % 2}")
            wait(sp, S["max_ready"], t("max_ready"), BH * NT)
            load(W[:, 3, :], A["w2"][3], "w3_in")
            load(ROWS[:, 0:2 * D], A["l2_bo_b2"], "row_in")
            for k in range(2):
                load(GB[:, k, :], A["l2_lnb"][2 + k:3 + k, :].to_broadcast([P, D]), "gb_in")
            load(COLB[:, 0:8], A["l2_b1"], "col_in")
            load(W[:, 0:2, :].rearrange("p a b -> p (a b)"), A["l2_w1"], "w0_in")
            t = at("z2")
            wait(sp, S["upd_done"], t("upd_done"))
            load(W[:, 2:4, :].rearrange("p a b -> p (a b)"), A["l2_w2"], "w2_in")
            t = at("res2")
            wait(sp, S["x_upd"], t("x_upd"))
            sp.wait_ge(S["x_saved"], 16 * NT)
            for i in range(NT):
                if i >= 2:
                    wait(sp, S["x_upd"], t("x_upd"), i - 1)
                load(Y[:, i % 2, :], xs_rows[i], f"res_in{i % 2}")
            load(W[:, 0, 0:1024], A["l3_w1"], "w0_in")
            load(ROWS[:, 0:256], A["l3_b1"], "row_in")
            load(W[:, 1, 0:1024], A["l3_w2"], "w1_in")
            load(GB[:, 0, :], A["l3_b2"].to_broadcast([P, D]), "gb_in")
            t = at("ct")
            for i in range(NT):
                if i >= 2:
                    wait(sp, S["ct_done"], t("ct_done"), i - 1)
                load(CR[:, i % 2, :], cnt_rows[i], f"c_in{i % 2}")
            for i in range(NT):
                sp.wait_ge(S["final_ready"], i + 1)
                load(out_rows[i], X[:, i, :], "final_out")
            sp.wait_ge(S["final_out"], 16 * NT)

        @block.gpsimd
        def _(gp):
            gp.memset(ONES, 1.0).then_inc(S["consts_ready"], 1)
            gp.memset(NEG, NO_EDGE).then_inc(S["neg_ready"], 1)
            gp.wait_ge(S["consts_ready"], 1)
            gp.wait_ge(S["neg_ready"], 1)
            gp.affine_select(out=IDENT, in_=ONES, compare_op=ALU.is_equal, fill=0.0, base=0,
                             pattern=[[1, 128]], channel_multiplier=-1).then_inc(S["consts_ready"], 1)
            gp.affine_select(out=TRI, in_=ONES[0:P, 0:P], compare_op=ALU.is_gt, fill=0.0, base=0,
                             pattern=[[1, P]], channel_multiplier=-1).then_inc(S["consts_ready"], 1)
            for k in range(2):
                gp.wait_ge(S["consts_ready"], 3 + k)
                gp.iota(FRQ[32 * k:32 * k + 32, 0:1].bitcast(I32), pattern=[[0, 1]], base=1,
                        channel_multiplier=1).then_inc(S["consts_ready"], 1)
            gp.wait_ge(S["consts_ready"], 5)
            gp.iota(SRCG.bitcast(I32), pattern=[[1, EC]], base=N * N, channel_multiplier=EC).then_inc(S["consts_ready"], 1)
            gp.wait_ge(S["gmax_ready"], 1)
            gp.wait_ge(S["consts_ready"], 6)
            gp.partition_all_reduce(GALL, GMX, P, bass.bass_isa.ReduceOp.max).then_inc(S["gmax_all"], 1)
            gp.wait_ge(S["cnt_zeroed"], 16 * (NT + 1))
            for g in range(NG):
                gp.wait_ge(S["idx_ready"], g + 1)
                gp.wait_ge(S["sums_out"], g + 1)
                if g:
                    gp.wait_ge(S["counted"], 16 * G * g)
                for k in range(G * g, G * g + G):
                    gp.indirect_dma_start(out=cnt_tab[:, :], out_offset=bass.IndirectOffsetOnAxis(ap=WIDX[:, k:k + 1].bitcast(U32), axis=0),
                                          in_=NGRP[:, k:k + 1], in_offset=None, bounds_check=N * N + E - 1, oob_is_err=True,
                                          compute_op=ALU.add).then_inc(S["counted"], 16)
            gp.wait_ge(S["bia_cleared"], 16 * 4)
            gp.wait_ge(S["lse_ready"], 1)
            for g in range(NG):
                if g:
                    gp.wait_ge(S["scattered"], 16 * G * g)
                for k in range(G * g, G * g + G):
                    c = k % G
                    gp.indirect_dma_start(out=MRG[:, 0, c * BH:(c + 1) * BH], out_offset=None, in_=bia_tab[:, :],
                                          in_offset=bass.IndirectOffsetOnAxis(ap=KEYI[:, k:k + 1].bitcast(U32), axis=0)).then_inc(S["gathered"], 16)
                gp.wait_ge(S["mrg_ready"], g + 1)
                for k in range(G * g, G * g + G):
                    c = k % G
                    gp.indirect_dma_start(out=bia_tab[:, :], out_offset=bass.IndirectOffsetOnAxis(ap=WIDX[:, k:k + 1].bitcast(U32), axis=0),
                                          in_=MRG[:, 4, c * BH:(c + 1) * BH], in_offset=None, bounds_check=N * N - 1,
                                          oob_is_err=False).then_inc(S["scattered"], 16)
            gp.wait_ge(S["scattered"], 16 * EC)

        @block.vector
        def _(v):
            mine = [0, None]

            def step(ins):
                mine[0] += 1
                ins.then_inc(S["v_step"], 1)
                v.wait_ge(S["v_step"], mine[0] if mine[1] is None else mine[1] * V_LOOP_STEPS + mine[0])

            def norm(t, src, kind, dst=None, slope=None, source=None):
                if source is not None:
                    v.wait_ge(S["x_in"], 16 * NT)
                    for i in range(NT):
                        o = v.bn_stats(BN[:, i, :], src[:, i, :])
                    step(o)
                v.memset(VARC, 0.0)
                for i in range(NT):
                    o = v.bn_aggr(MV[:, i, :], BN[:, i, :])
                step(o)
                v.tensor_scalar(VARC, MV[:, :, 1], EPS, None, ALU.add).then_inc(S["stats_ready"], 1)
                wait(v, S["std_ready"], t("std_ready"), 1)
                step(v.reciprocal(RSTD, STD))
                v.scalar_tensor_tensor(NMR, MV[:, :, 0], -1.0, RSTD, ALU.mult, ALU.mult).then_inc(S["rstd_ready"], 1)
                if kind == "relu":
                    return
                if kind == "affine":
                    wait(v, S["gb_in"], t("gb_in"), 32)
                for i in range(NT):
                    y = Y[:, i % 2, :] if dst is None else dst[:, i, :]
                    wait(v, S["xn_ready"], t("xn_ready"), i + 1)
                    if i >= 2 and dst is None:
                        wait(v, S["yT_ready"], t("yT_ready"), i - 1)
                    if kind == "cond":
                        wait(v, S["cond_ready"], t("cond_ready"), i + 1)
                        b = 2 * (i % 2)
                        v.tensor_tensor(y, XN[:, i % 2, :], bank(b), ALU.mult).then_inc(S["gate"], 1)
                        wait_gate()
                        v.tensor_tensor(y, y, bank(b + 1), ALU.add).then_inc(S["y_ready"], 1)
                    else:
                        v.tensor_tensor(y, XN[:, i % 2, :], GB[:, 0, :], ALU.mult).then_inc(S["gate"], 1)
                        wait_gate()
                        if slope is None:
                            v.tensor_tensor(y, y, GB[:, 1, :], ALU.add).then_inc(S["y_ready"], 1)
                        else:
                            v.tensor_tensor(y, y, GB[:, 1, :], ALU.add).then_inc(S["gate"], 1)
                            wait_gate()
                            v.scalar_tensor_tensor(y, y, slope, y, ALU.mult, ALU.max).then_inc(S["y_ready"], 1)

            gates = [0]
            GATES_PER_LAYER = 2 * NT

            def wait_gate():
                gates[0] += 1
                v.wait_ge(S["gate"], gates[0] if mine[1] is None else mine[1] * GATES_PER_LAYER + gates[0])

            def update(t, dst, add=True, stats=True):
                for i in range(NT):
                    wait(v, S["upd_done"], t("upd_done"), i + 1)
                    if add:
                        o = v.tensor_tensor(dst[:, i, :], dst[:, i, :], bank(i % 4), ALU.add)
                    else:
                        o = v.tensor_copy(dst[:, i, :], bank(i % 4))
                    o.then_inc(S["x_upd"], 1)
                    if stats and i:
                        wait(v, S["x_upd"], t("x_upd"), i)
                        v.bn_stats(BN[:, i - 1, :], dst[:, i - 1, :])
                if stats:
                    wait(v, S["x_upd"], t("x_upd"), NT)
                    step(v.bn_stats(BN[:, NT - 1, :], dst[:, NT - 1, :]))

            def residual(t, stats=True):
                for i in range(NT):
                    wait(v, S[f"res_in{i % 2}"], t(f"res_in{i % 2}"), 16 * (i // 2 + 1))
                    v.tensor_tensor(X[:, i, :], X[:, i, :], Y[:, i % 2, :], ALU.add).then_inc(S["x_upd"], 1)
                    if i:
                        wait(v, S["x_upd"], t("x_upd"), i)
                        v.bn_stats(BN[:, i - 1, :], X[:, i - 1, :])
                wait(v, S["x_upd"], t("x_upd"), NT)
                step(v.bn_stats(BN[:, NT - 1, :], X[:, NT - 1, :]))

            def qkv(t, scale):
                wait(v, S["col_in"], t("col_in"), 16)
                v.tensor_scalar(QBS, COLB[:, 0:4], scale, None, ALU.mult).then_inc(S["qbs_ready"], 1)
                g = 0
                for j, (a, n) in enumerate(CHUNKS):
                    for which, dst in ((0, T2), (1, T3)):
                        for m in range(KC):
                            if g % 2:
                                wait(v, S["grp_done"], t("grp_done"), g + 1)
                                b = COLB[:, 4 * which + m:4 * which + m + 1]
                                if which == 0:
                                    o = v.tensor_scalar(dst[:, m, a:a + n], bank(g % 4, 128, n), b, scale, ALU.add, ALU.mult)
                                else:
                                    o = v.tensor_scalar(dst[:, m, a:a + n], bank(g % 4, 128, n), b, None, ALU.add)
                                o.then_inc(S["out_d"], 1)
                            g += 1
                for i in range(NT):
                    if g % 2:
                        wait(v, S["grp_done"], t("grp_done"), g + 1)
                        v.tensor_copy(V[:, i, :], bank(g % 4)).then_inc(S["out_d"], 1)
                    g += 1

            def up(t, cols):
                g = 0
                for j, (a, n) in enumerate(CHUNKS):
                    for m in range(KC):
                        if g % 2:
                            wait(v, S["grp_done"], t("grp_done"), g + 1)
                            v.tensor_scalar(T2[:, m, a:a + n], bank(g % 4, 128, n), cols[:, m:m + 1], 0.0, ALU.add, ALU.max).then_inc(S["out_d"], 1)
                        g += 1

            def take_groups(t, dst, chunks):
                g = 0
                for j, (a, n) in enumerate(CHUNKS):
                    for m in range(chunks):
                        if g % 2:
                            wait(v, S["grp_done"], t("grp_done"), g + 1)
                            v.tensor_copy(dst[:, m, a:a + n], bank(g % 4, 128, n)).then_inc(S["out_d"], 1)
                        g += 1

            def attention(t, heads, third):
                steps = heads * NT

                def scores_max(n):
                    i, h = divmod(n, heads)
                    if n >= 2:
                        wait(v, S["t_done"], t("t_done"), n - 1)
                    wait(v, S["s_done"], t("s_done"), n + 1)
                    if third:
                        if h == 0:
                            wait(v, S[f"bia_in{i % 2}"], t(f"bia_in{i % 2}"), 16 * (i // 2 + 1))
                        add = BIA[i % 2][:, :, h].rearrange("p (a x) -> p a x", x=250)
                    else:
                        if h == 0:
                            wait(v, S[f"lct_in{i % 2}"], t(f"lct_in{i % 2}"), 16 * (i // 2 + 1))
                        add = pairs(LC[:, i % 2, :])
                    v.memset(IDLE, 0.0)
                    v.tensor_tensor_reduce(out=pairs(PR[:, n % 2, :]), in0=halves(n % 2), in1=add, scale=1.0, scalar=-3.0e38,
                                           op0=ALU.add, op1=ALU.max, accum_out=MX[:, n % 2:n % 2 + 1]).then_inc(S["max_ready"], 1)
                    wait(v, S["max_ready"], t("max_ready"), n + 1)
                    v.tensor_scalar(NMX[:, n % 2:n % 2 + 1], MX[:, n % 2:n % 2 + 1], -1.0, None, ALU.mult).then_inc(S["negmax"], 1)

                def take_blocks(n):
                    wait(v, S["t_done"], t("t_done"), n + 1)
                    if n >= 2:
                        wait(v, S["pv_done"], t("pv_done"), n - 1)
                    v.tensor_copy(pairs(PT[:, n % 2, :])[:, 0:2, :], halves(n % 2)[:, 0:2, :]).then_inc(S["t_out_d"], 1)

                def take_rows(i):
                    n = heads * (i + 1)
                    wait(v, S["p_ready"], t("p_ready"), n)
                    step(v.reciprocal(RD[:, i % 2, 0:heads], DEN[:, i % 2, 0:heads]))
                    step(v.tensor_scalar(RD[:, i % 2, 0:heads], RD[:, i % 2, 0:heads], FLAG[:, i:i + 1], None, ALU.mult))
                    wait(v, S["pv_done"], t("pv_done"), n)
                    if i >= 1:
                        wait(v, S["oT_done"], t("oT_done"), i)
                    v.tensor_tensor(OS.rearrange("p (h x) -> p h x", h=heads), bank(6 + i % 2).rearrange("p (h x) -> p h x", h=heads),
                                    RD[:, i % 2, 0:heads].unsqueeze(2).to_broadcast([P, heads, D // heads]), ALU.mult).then_inc(S["o_ready"], 1)

                for n in range(steps + 2):
                    if n < steps:
                        scores_max(n)
                    if 1 <= n <= steps:
                        take_blocks(n - 1)
                    if n >= 2 and (n - 2) % heads == heads - 1:
                        take_rows((n - 2) // heads)

            v.memset(ZERO, 0.0).then_inc(S["zero_ready"], 1)
            v.memset(EPSC, EPS)
            v.wait_ge(S["edges_in"], 16 * 5)
            v.tensor_copy(SRC, SRCI)
            v.tensor_copy(DST, DSTI)
            v.tensor_copy(DSTG, DSTJ)
            step(v.tensor_copy(KEYC, SRCJ))
            v.scalar_tensor_tensor(KEYC, KEYC, float(N), DSTG, ALU.mult, ALU.add).then_inc(S["keyc_ready"], 1)
            step(v.scalar_tensor_tensor(KEY, SRC, float(N), DST, ALU.mult, ALU.add))
            v.tensor_copy(KEYI, KEY)
            v.reduce_max(GMX, ATTR, AX.X).then_inc(S["gmax_ready"], 1)
            v.wait_ge(S["consts_ready"], 6)
            step(v.tensor_copy(SPARE, SRCG.bitcast(I32)))
            v.tensor_tensor(SPARE, SPARE, KEY, ALU.subtract)
            v.wait_ge(S["gmax_all"], 1)
            v.tensor_scalar(BACK, GALL, HEADROOM, None, ALU.subtract)
            v.tensor_scalar(SHIFT, GALL, -1.0, HEADROOM, ALU.mult, ALU.add).then_inc(S["shift_ready"], 1)
            v.wait_ge(S["exp_ready"], 1)
            ex = EX.rearrange("p (c h) -> p c h", h=BH)
            step(v.tensor_copy(EPART[:, :, 0:BH], ex))
            step(v.tensor_tensor(ex, ex, EPART[:, :, 0:BH], ALU.subtract))
            step(v.tensor_copy(EPART[:, :, BH:2 * BH], ex))
            step(v.tensor_tensor(ex, ex, EPART[:, :, BH:2 * BH], ALU.subtract))
            v.tensor_copy(EPART[:, :, 2 * BH:3 * BH], ex)
            v.memset(EPART[:, :, 3 * BH:WP], 1.0)
            step(v.tensor_copy(TRIB, TRI))

            def compare(g):
                v.wait_ge(S[f"keyb_in{g % 2}"], 16 * (g // 2 + 1))
                if g >= 2:
                    v.wait_ge(S["grp_sum"], g - 1)
                q = EQ[g % 2]
                for c in range(G):
                    o = v.tensor_scalar(q[:, c * G * P:(c + 1) * G * P], KEYB[:, g % 2, :], KEY[:, G * g + c:G * g + c + 1], None, ALU.is_equal)
                o.then_inc(S["eq_ready"], 1)
                v.wait_ge(S["eq_ready"], g + 1)
                v.tensor_tensor(EQD[g % 2], q.rearrange("p (c x) -> p c x", c=G)[:, :, 0:P],
                                TRIB.unsqueeze(1).to_broadcast([P, G, P]), ALU.mult).then_inc(S["eqd_ready"], 1)

            def take_sums(g):
                v.wait_ge(S["grp_sum"], g + 1)
                b = banks[0:P, g % 2, 0:G * 32].rearrange("p (c x) -> p c x", c=G)
                gs = slice(G * g, G * g + G)
                v.tensor_copy(NGRP[:, gs], b[:, :, WP - 1])
                v.tensor_copy(SUMS[:, gs, :], b[:, :, 0:WP])
                if g:
                    v.wait_ge(S["idx_ready"], g)
                step(v.tensor_scalar(LATE, b[:, :, WP], 0.5, None, ALU.is_ge))
                v.sem_inc(S["sums_out"], 1)
                step(v.tensor_tensor(LATE, LATE, SPARE[:, gs], ALU.mult))
                step(v.tensor_tensor(LATE, LATE, KEY[:, gs], ALU.add))
                v.tensor_copy(WIDX[:, gs], LATE).then_inc(S["idx_ready"], 1)

            for g in range(NG):
                compare(g)
                if g:
                    take_sums(g - 1)
            take_sums(NG - 1)

            tmp = TMP.rearrange("p (c h) -> p c h", h=BH)
            attr = ATTR.rearrange("p (c h) -> p c h", h=BH)
            v.wait_ge(S["idx_ready"], NG)
            step(v.tensor_tensor(tmp, SUMS[:, :, 0:BH], SUMS[:, :, BH:2 * BH], ALU.add))
            step(v.tensor_tensor(tmp, tmp, SUMS[:, :, 2 * BH:3 * BH], ALU.add))
            v.tensor_scalar(tmp, tmp, float(2.0 ** -62), None, ALU.max).then_inc(S["lsum_ready"], 1)
            v.wait_ge(S["lse_log"], 1)
            step(v.scalar_tensor_tensor(tmp, tmp, BACK, attr, ALU.add, ALU.subtract))
            step(v.tensor_scalar(CNT, NGRP, 1.5, None, ALU.is_ge))
            step(v.tensor_tensor(tmp, tmp, CNT.unsqueeze(2).to_broadcast([P, EC, BH]), ALU.mult))
            v.tensor_tensor(attr, attr, tmp, ALU.add).then_inc(S["lse_ready"], 1)

            def merge(g):
                new = ATTR[:, g * G * BH:(g + 1) * G * BH]
                v.wait_ge(S["gathered"], 16 * G * (g + 1))
                if g == 0:
                    v.wait_ge(S["lse_ready"], 1)
                v.tensor_tensor(MRG[:, 1, :], MRG[:, 0, :], new, ALU.max)
                step(v.tensor_tensor(MRG[:, 2, :], MRG[:, 0, :], new, ALU.min))
                v.tensor_tensor(MRG[:, 2, :], MRG[:, 2, :], MRG[:, 1, :], ALU.subtract).then_inc(S["mrg_diff"], 1)
                v.wait_ge(S["mrg_log"], g + 1)
                v.tensor_tensor(MRG[:, 4, :], MRG[:, 1, :], MRG[:, 3, :], ALU.add).then_inc(S["mrg_ready"], 1)

            for g in range(NG):
                merge(g)

            step(v.tensor_copy(FRQ[:, 1:2], FRQ[:, 0:1].bitcast(I32)))
            step(v.tensor_scalar(FRQ[:, 1:2], FRQ[:, 1:2], float(np.float32(2.0 * np.pi / 16)), None, ALU.mult))
            step(v.memset(FRQ[:, 2:4], 0.0))
            v.memset(FRQ[32:64, 2:3], 0.25)
            step(v.memset(FRQ[32:64, 3:4], float(np.float32(np.pi / 2))))
            v.wait_ge(S["noise_in"], 64)
            ph, turns = PHASE[:, 0, :], PHASE[:, 1, :]
            two_pi = 2 * np.pi
            p1 = 6.28125
            p2 = float(np.float32(two_pi - p1))
            step(v.tensor_scalar(ph, ph, FRQ[:, 1:2], None, ALU.mult))
            step(v.tensor_scalar(turns, ph, float(1.0 / two_pi), FRQ[:, 2:3], ALU.mult, ALU.add))
            step(v.tensor_scalar(turns, turns, float(1.5 * 2 ** 23), None, ALU.add))
            step(v.tensor_scalar(turns, turns, float(1.5 * 2 ** 23), None, ALU.subtract))
            for c in (p1, p2, two_pi - p1 - p2):
                step(v.scalar_tensor_tensor(ph, turns, -c, ph, ALU.mult, ALU.add))
            step(v.tensor_scalar(ph, ph, FRQ[:, 3:4], None, ALU.add))
            v.tensor_scalar(ph, ph, 3.1415925, -3.1415925, ALU.min, ALU.max).then_inc(S["phase_ready"], 1)
            v.memset(COND, 1.0)
            for k in range(2):
                v.memset(CW[k][:, 0:D], 1.0)
                o = v.memset(CW[k][:, D:2 * D], 0.0)
            step(o)
            v.sem_inc(S["cw_clear"], 1)
            for j, (a, n) in enumerate(CHUNKS):
                v.wait_ge(S["cond_mm"], j + 1)
                v.tensor_scalar(COND[0:CD, a:a + n], bank(j, CD, n), FB[:, 1:2], None, ALU.add).then_inc(S["cond_built"], 1)

            for i in range(NT):
                c = LC[:, i % 2, :]
                m = PR[:, i % 2, :]
                v.wait_ge(S[f"cnt_in{i % 2}"], 16 * (i // 2 + 1))
                v.reduce_sum(DEG[:, i:i + 1], c, AX.X)
                v.tensor_scalar(m, c, 0.5, NO_EDGE, ALU.is_lt, ALU.mult)
                step(v.tensor_copy(NMX[:, 0:1], EPSC[0:P, :]))
                v.tensor_scalar(c, c, 1.0, None, ALU.max).then_inc(S["lc_pre"], 1)
                v.wait_ge(S["lc_log"], i + 1)
                v.tensor_tensor(c, c, m, ALU.add).then_inc(S["lc_ready"], 1)
            v.wait_ge(S["lc_ready"], NT)
            v.tensor_scalar(FLAG, DEG, 0.5, None, ALU.is_ge)
            step(v.tensor_scalar(DEG1, DEG, 1.0, None, ALU.add))

            norm(at("pre0"), X, "relu", source="x_in")
            start_steps, start_gates = mine[0], gates[0]
            with v.Fori(0, LAYERS) as L:
                mine[1] = L
                t = at("n1", L)
                wait(v, S["xn_ready"], t("xn_ready"))
                for i in range(NT):
                    o = v.bn_stats(BN[:, i, :], X[:, i, :])
                step(o)
                norm(t, X, "cond")
                qkv(at("qkv", L), 128.0 ** -0.5)
                attention(at("att", L), 4, False)
                update(at("wo", L), X)
                norm(at("n2", L), X, "cond")
                up(at("up", L), COLB[:, 8:12])
                update(at("down", L), X, stats=False)
                wait(v, S["x_upd"], at("down", L)("x_upd"), NT)
                per_steps, per_gates = mine[0] - start_steps, gates[0] - start_gates
            assert per_steps == V_LOOP_STEPS, per_steps
            assert per_gates == GATES_PER_LAYER, per_gates
            mine[0], mine[1] = start_steps + LAYERS * per_steps, None
            gates[0] = start_gates + LAYERS * per_gates

            residual(at("res1"))
            norm(at("pre1"), X, "relu")
            v.tensor_scalar(DINV, DEG, 1.0, None, ALU.max).then_inc(S["deg_clip"], 1)
            v.wait_ge(S["deg_sqrt"], 1)
            step(v.reciprocal(DINV, DINV))
            v.tensor_tensor(DINV, DINV, FLAG, ALU.mult).then_inc(S["dinv_ready"], 1)
            t = at("dense")
            v.wait_ge(S["dinv_in"], 16)
            step(v.tensor_scalar(DINVB, DINVB, -1.0, None, ALU.mult))
            wait(v, S["dense_in"], t("dense_in"), 16)
            for i in range(NT):
                v.scalar_tensor_tensor(DENSE[:, i, :], DENSE[:, i, :], DINV[:, i:i + 1], DINVB, ALU.mult, ALU.mult).then_inc(S["dense_ready"], 1)
            take_groups(at("prop1"), T2, KC)
            update(at("conv1"), V, add=False)
            norm(at("mid1"), V, "affine", dst=V, slope=0.01)
            wait(v, S["y_ready"], at("mid1")("y_ready"), NT)
            v.sem_inc(S["gb_used"], 1)
            take_groups(at("prop2"), T2, KC)
            update(at("conv2"), X)
            norm(at("pre2"), X, "relu")
            t = at("z1")
            for i in range(NT):
                wait(v, S["xn_ready"], t("xn_ready"), i + 1 - NT)
                o = v.bn_stats(BN[:, i, :], X[:, i, :])
            step(o)
            norm(t, X, "affine")
            qkv(at("qkv2"), 0.125)
            attention(at("att2"), BH, True)
            update(at("wo2"), X)
            norm(at("z2"), X, "affine")
            update(at("down2"), X, stats=False)
            wait(v, S["x_upd"], at("down2")("x_upd"), NT)
            residual(at("res2"))
            norm(at("pre3"), X, "relu")
            t = at("r3")
            for g in range(1, NT, 2):
                wait(v, S["grp_done"], t("grp_done"), g + 1)
                v.tensor_scalar(V[:, g, 0:256], bank(g % 4, P, 256), 0.0, None, ALU.max).then_inc(S["out_d"], 1)
            t = at("ct")
            for i in range(NT):
                wait(v, S["ct_done"], t("ct_done"), i + 1)
                blocks = halves(i % 2).rearrange("p h (k x) -> p h k x", k=2)
                d = DENSE[:, :, i * P:(i + 1) * P].rearrange("p (h k) x -> p h k x", k=2)
                step(v.tensor_copy(d, blocks))
                v.tensor_tensor(DENSE[:, i, i * P:(i + 1) * P], DENSE[:, i, i * P:(i + 1) * P], IDENT[0:P, 0:P], ALU.add).then_inc(S["dense_ready"], 1)
            take_groups(at("prop3"), T2, 2)
            t = at("conv3")
            wait(v, S["gb_in"], t("gb_in"), 16)
            for i in range(NT):
                wait(v, S["upd_done"], t("upd_done"), i + 1)
                step(v.tensor_tensor(X[:, i, :], X[:, i, :], bank(i % 4), ALU.add))
                v.sem_inc(S["x_upd"], 1)
                v.scalar_tensor_tensor(X[:, i, :], GB[:, 0, :], DEG1[:, i:i + 1], X[:, i, :], ALU.mult, ALU.add).then_inc(S["final_ready"], 1)

        @block.scalar
        def _(act):
            def norm(t, src, kind, dst=None, transposed=True):
                wait(act, S["stats_ready"], t("stats_ready"), 1)
                act.activation(STD, VARC, ACT.Sqrt).then_inc(S["std_ready"], 1)
                wait(act, S["rstd_ready"], t("rstd_ready"), 1)
                if kind == "relu":
                    for i in range(NT):
                        d = Y[:, i % 2, :] if dst is None else dst[:, i, :]
                        if dst is None and i >= 2:
                            wait(act, S["yT_ready"], t("yT_ready"), i - 1)
                        act.activation(d, src[:, i, :], ACT.Relu, bias=NMR[:, i:i + 1], scale=RSTD[:, i:i + 1]).then_inc(S["xn_ready"], 1)
                        if transposed and i:
                            take_T(t, i - 1)
                    if transposed:
                        take_T(t, NT - 1)
                    return
                for i in range(NT):
                    if i >= 2:
                        wait(act, S["y_ready"], t("y_ready"), i - 1)
                    act.activation(XN[:, i % 2, :], src[:, i, :], ACT.Identity, bias=NMR[:, i:i + 1], scale=RSTD[:, i:i + 1]).then_inc(S["xn_ready"], 1)
                    if i >= 2:
                        take_T(t, i - 2)
                take_T(t, NT - 2)
                take_T(t, NT - 1)

            def take_T(t, i):
                wait(act, S["yT_ready"], t("yT_ready"), i + 1)
                act.activation(T1[:, :, i * P:(i + 1) * P], banks[0:128, 4 + i % 2, 0:500].rearrange("p (c x) -> p c x", c=KC), ACT.Copy).then_inc(S["yT_out"], 1)

            def qkv(t, scale):
                wait(act, S["col_in"], t("col_in"), 16)
                wait(act, S["qbs_ready"], t("qbs_ready"), 1)
                g = 0
                for j, (a, n) in enumerate(CHUNKS):
                    for which, dst in ((0, T2), (1, T3)):
                        for m in range(KC):
                            if g % 2 == 0:
                                wait(act, S["grp_done"], t("grp_done"), g + 1)
                                if which == 0:
                                    o = act.activation(dst[:, m, a:a + n], bank(g % 4, 128, n), ACT.Identity, bias=QBS[:, m:m + 1], scale=scale)
                                else:
                                    o = act.activation(dst[:, m, a:a + n], bank(g % 4, 128, n), ACT.Identity, bias=COLB[:, 4 + m:5 + m])
                                o.then_inc(S["out_a"], 1)
                            g += 1
                for i in range(NT):
                    if g % 2 == 0:
                        wait(act, S["grp_done"], t("grp_done"), g + 1)
                        act.activation(V[:, i, :], bank(g % 4), ACT.Copy).then_inc(S["out_a"], 1)
                    g += 1

            def take_groups(t, dst, chunks, func=ACT.Copy, cols=None, every=False):
                g = 0
                for j, (a, n) in enumerate(CHUNKS):
                    for m in range(chunks):
                        if g % 2 == 0 or every:
                            wait(act, S["grp_done"], t("grp_done"), g + 1)
                            if cols is None:
                                o = act.activation(dst[:, m, a:a + n], bank(g % 4, 128, n), func)
                            else:
                                o = act.activation(dst[:, m, a:a + n], bank(g % 4, 128, n), func, bias=cols[:, m:m + 1])
                            o.then_inc(S["out_a"], 1)
                        g += 1

            def attention(t, heads):
                steps = heads * NT
                for n in range(steps + 3):
                    if n < steps:
                        i, h = divmod(n, heads)
                        wait(act, S["negmax"], t("negmax"), n + 1)
                        act.activation(PR[:, n % 2, :], PR[:, n % 2, :], ACT.Exp, bias=NMX[:, n % 2:n % 2 + 1],
                                       accum_out=DEN[:, i % 2, h:h + 1]).then_inc(S["p_ready"], 1)
                    if 1 <= n <= steps:
                        m = n - 1
                        wait(act, S["t_done"], t("t_done"), m + 1)
                        if m >= 2:
                            wait(act, S["pv_done"], t("pv_done"), m - 1)
                        act.activation(pairs(PT[:, m % 2, :])[:, 2:5, :], halves(m % 2)[:, 2:5, :], ACT.Copy).then_inc(S["t_out_a"], 1)
                    if n >= 3 and (n - 3) % heads == heads - 1:
                        i = (n - 3) // heads
                        wait(act, S["oT_done"], t("oT_done"), i + 1)
                        act.activation(T1[:, :, i * P:(i + 1) * P], banks[0:128, 6 + i % 2, 0:500].rearrange("p (c x) -> p c x", c=KC), ACT.Copy).then_inc(S["oT_out"], 1)

            act.wait_ge(S["shift_ready"], 1)
            act.wait_ge(S["edges_in"], 16 * 5)
            act.activation(EX, ATTR, ACT.Exp, bias=SHIFT).then_inc(S["exp_ready"], 1)
            act.wait_ge(S["lsum_ready"], 1)
            act.activation(TMP, TMP, ACT.Ln).then_inc(S["lse_log"], 1)
            for g in range(NG):
                act.wait_ge(S["mrg_diff"], g + 1)
                act.activation(MRG[:, 3, :], MRG[:, 2, :], ACT.Exp).then_inc(S["mrg_exp"], 1)
                act.wait_ge(S["mrg_exp"], g + 1)
                act.activation(MRG[:, 3, :], MRG[:, 3, :], ACT.Ln, bias=1.0).then_inc(S["mrg_log"], 1)
            act.wait_ge(S["phase_ready"], 1)
            act.activation(PHASE[:, 0, :], PHASE[:, 0, :], ACT.Sin).then_inc(S["emb_ready"], 1)
            for j, (a, n) in enumerate(CHUNKS):
                act.wait_ge(S["emb_mm"], j + 1)
                act.activation(PHASE[0:CD, 1, a:a + n], bank(4 + j, CD, n), ACT.Silu, bias=FB[:, 0:1]).then_inc(S["emb_act"], 1)
            for i in range(NT):
                act.wait_ge(S["lc_pre"], i + 1)
                act.activation(LC[:, i % 2, :], LC[:, i % 2, :], ACT.Ln).then_inc(S["lc_log"], 1)
            norm(at("pre0"), X, "relu", dst=X, transposed=False)
            with act.Fori(0, LAYERS) as L:
                norm(at("n1", L), X, "cond")
                qkv(at("qkv", L), 128.0 ** -0.5)
                attention(at("att", L), 4)
                norm(at("n2", L), X, "cond")
                take_groups(at("up", L), T2, KC, ACT.Relu, COLB[:, 8:12])
            norm(at("pre1"), X, "relu", dst=V)
            act.wait_ge(S["deg_clip"], 1)
            act.activation(DINV, DINV, ACT.Sqrt).then_inc(S["deg_sqrt"], 1)
            take_groups(at("prop1"), T2, KC)
            norm(at("mid1"), V, "affine")
            take_groups(at("prop2"), T2, KC)
            act.wait_ge(S["x_saved"], 16 * NT)
            norm(at("pre2"), X, "relu", dst=X, transposed=False)
            norm(at("z1"), X, "affine")
            qkv(at("qkv2"), 0.125)
            attention(at("att2"), BH)
            norm(at("z2"), X, "affine")
            t = at("up2")
            wait(act, S["col_in"], t("col_in"), 16)
            take_groups(t, H8, 2 * KC, ACT.Silu, COLB[:, 0:8], every=True)
            norm(at("pre3"), X, "relu")
            t = at("r3")
            for g in range(0, NT, 2):
                wait(act, S["grp_done"], t("grp_done"), g + 1)
                act.activation(V[:, g, 0:256], bank(g % 4, P, 256), ACT.Relu).then_inc(S["out_a"], 1)
            take_groups(at("prop3"), T2, 2)

        @block.tensor
        def _(pe):
            one = ONES[0:1, 0:P]

            def transposes(t, src, source):
                for i in range(NT):
                    wait(pe, S[source], t(source), i + 1)
                    if i >= 2:
                        wait(pe, S["yT_out"], t("yT_out"), i - 1)
                    row = Y[:, i % 2, :] if src is None else src[:, i, :]
                    for c in range(KC):
                        o = pe.transpose(banks[0:128, 4 + i % 2, c * P:(c + 1) * P], row[:, c * 128:(c + 1) * 128], IDENT[0:P, 0:P])
                    o.then_inc(S["yT_ready"], 1)

            def cond_norm(t, cw, load):
                wait(pe, S["rstd_ready"], t("rstd_ready"), 1)
                wait(pe, S[load], t(load), 16)
                for i in range(NT + 1):
                    if i < NT:
                        if i >= 2:
                            wait(pe, S["y_ready"], t("y_ready"), i - 1)
                        b = 2 * (i % 2)
                        pe.matmul(bank(b), COND[:, i * P:(i + 1) * P], cw[:, 0:D], start=True, stop=True)
                        pe.matmul(bank(b + 1), COND[:, i * P:(i + 1) * P], cw[:, D:2 * D], start=True, stop=True).then_inc(S["cond_ready"], 1)
                    if i >= 1:
                        k = i - 1
                        wait(pe, S["y_ready"], t("y_ready"), k + 1)
                        if k >= 2:
                            wait(pe, S["yT_out"], t("yT_out"), k - 1)
                        for c in range(KC):
                            o = pe.transpose(banks[0:128, 4 + k % 2, c * P:(c + 1) * P], Y[:, k % 2, c * 128:(c + 1) * 128], IDENT[0:P, 0:P])
                        o.then_inc(S["yT_ready"], 1)

            def project(out, w, m, a, n, k=KC, width=D, src=T1):
                for c in range(k):
                    o = pe.matmul(out, w[:, c * width + m * 128:c * width + (m + 1) * 128], src[:, c, a:a + n], start=(c == 0), stop=(c == k - 1))
                return o

            def rows_of(out, i, parts, row, n=D):
                first = True
                for src, w, k in parts:
                    for c in range(k):
                        pe.matmul(out, src[:, c, i * P:(i + 1) * P], w[:, c * n:(c + 1) * n], start=first, stop=(row is None and c == k - 1 and (src, w, k) is parts[-1]))
                        first = False
                return pe.matmul(out, one, row, start=False, stop=True) if row is not None else None

            def T1_chunk(t, name, j):
                a, n = CHUNKS[j]
                wait(pe, S["yT_out"], t("yT_out"), (a + n) // P - NT)

            def qkv(t):
                g = 0
                for j, (a, n) in enumerate(CHUNKS):
                    T1_chunk(t, "yT_out", j)
                    for which in (0, 1):
                        wait(pe, S[f"w{which}_in"], t(f"w{which}_in"), 16)
                        for m in range(KC):
                            grp_free(pe, t, g)
                            project(bank(g % 4, 128, n), W[:, which, :], m, a, n).then_inc(S["grp_done"], 1)
                            g += 1
                wait(pe, S["w2_in"], t("w2_in"), 16)
                wait(pe, S["row_in"], t("row_in"), 16)
                for i in range(NT):
                    grp_free(pe, t, g)
                    rows_of(bank(g % 4), i, [(T1, W[:, 2, :], KC)], ROWS[:, 0:D]).then_inc(S["grp_done"], 1)
                    g += 1

            def attention(t, heads):
                dh, steps = D // heads, heads * NT
                per_chunk = 128 // dh

                def scores(n):
                    i, h = divmod(n, heads)
                    if n >= 2:
                        wait(pe, S["t_out_a"], t("t_out_a"), n - 1)
                        wait(pe, S["t_out_d"], t("t_out_d"), n - 1)
                    lo = dh * (h % per_chunk)
                    q, k = T2[lo:lo + dh, h // per_chunk, i * P:(i + 1) * P], T3[lo:lo + dh, h // per_chunk, :]
                    hv = halves(n % 2)
                    for a, w in ((0, 2), (2, 2), (4, 1)):
                        o = pe.matmul(hv[:, a:a + w, :], q, k[:, a * 250:(a + w) * 250], start=True, stop=True)
                    o.then_inc(S["s_done"], 1)

                def turn(n):
                    wait(pe, S["p_ready"], t("p_ready"), n + 1)
                    hv = halves(n % 2)
                    for j in range(NT):
                        o = pe.transpose(hv[:, j // 2, (j % 2) * P:(j % 2 + 1) * P], PR[:, n % 2, j * P:(j + 1) * P], IDENT[0:P, 0:P])
                    o.then_inc(S["t_done"], 1)

                def product(n):
                    i, h = divmod(n, heads)
                    wait(pe, S["t_out_a"], t("t_out_a"), n + 1)
                    wait(pe, S["t_out_d"], t("t_out_d"), n + 1)
                    if h == 0 and i >= 2:
                        wait(pe, S["oT_out"], t("oT_out"), i - 1)
                    for j in range(NT):
                        o = pe.matmul(bank(6 + i % 2)[:, h * dh:(h + 1) * dh], PT[:, n % 2, j * P:(j + 1) * P], V[:, j, h * dh:(h + 1) * dh],
                                      start=(j == 0), stop=(j == NT - 1))
                    o.then_inc(S["pv_done"], 1)

                def turn_rows(i):
                    wait(pe, S["o_ready"], t("o_ready"), i + 1)
                    for c in range(KC):
                        o = pe.transpose(banks[0:128, 6 + i % 2, c * P:(c + 1) * P], OS[:, c * 128:(c + 1) * 128], IDENT[0:P, 0:P])
                    o.then_inc(S["oT_done"], 1)

                wait(pe, S["out_a"], t("out_a"))
                wait(pe, S["out_d"], t("out_d"))
                scores(0)
                for n in range(steps + 2):
                    if n + 1 < steps:
                        scores(n + 1)
                    if n >= 2 and (n - 2) % heads == heads - 1:
                        turn_rows((n - 2) // heads)
                    if n < steps:
                        turn(n)
                    if 1 <= n <= steps:
                        product(n - 1)

            def update(t, parts, row, waits=()):
                for i in range(NT):
                    if i >= 4:
                        wait(pe, S["x_upd"], t("x_upd"), i - 3)
                    rows_of(bank(i % 4), i, parts, row).then_inc(S["upd_done"], 1)

            def groups(t, w, chunks, k=KC, width=D, alternate=True):
                g = 0
                for j, (a, n) in enumerate(CHUNKS):
                    T1_chunk(t, "yT_out", j)
                    for m in range(chunks):
                        grp_free(pe, t, g, alternate)
                        project(bank(g % 4, 128, n), w, m, a, n, width=width).then_inc(S["grp_done"], 1)
                        g += 1

            def propagate(t, chunks):
                g = 0
                for j, (a, n) in enumerate(CHUNKS):
                    for m in range(chunks):
                        grp_free(pe, t, g)
                        for s_ in range(NT):
                            o = pe.matmul(bank(g % 4, 128, n), V[:, s_, m * 128:(m + 1) * 128], DENSE[:, s_, a:a + n], start=(s_ == 0), stop=(s_ == NT - 1))
                        o.then_inc(S["grp_done"], 1)
                        g += 1

            for g in range(NG):
                pe.wait_ge(S["eqd_ready"], g + 1)
                if g >= 2:
                    pe.wait_ge(S["sums_out"], g - 1)
                b = banks[0:P, g % 2, 0:G * 32].rearrange("p (c x) -> p c x", c=G)
                for c in range(G):
                    for c2 in range(G):
                        pe.matmul(b[:, c, 0:WP], EQ[g % 2][:, c2 * G * P + c * P:c2 * G * P + (c + 1) * P], EPART[:, G * g + c2, :], start=(c2 == 0), stop=(c2 == G - 1))
                    for c2 in range(c):
                        pe.matmul(b[:, c, WP:WP + 1], EQ[g % 2][:, c2 * G * P + c * P:c2 * G * P + (c + 1) * P], EPART[:, 0, WP - 1:WP], start=(c2 == 0), stop=False)
                    o = pe.matmul(b[:, c, WP:WP + 1], EQD[g % 2][:, c, :], EPART[:, 0, WP - 1:WP], start=(c == 0), stop=True)
                o.then_inc(S["grp_sum"], 1)
            pe.wait_ge(S["emb_ready"], 1)
            pe.wait_ge(S["sums_out"], NG)
            for j, (a, n) in enumerate(CHUNKS):
                pe.matmul(bank(4 + j, CD, n), FW1, PHASE[:, 0, a:a + n], start=True, stop=True).then_inc(S["emb_mm"], 1)
            for j, (a, n) in enumerate(CHUNKS):
                pe.wait_ge(S["emb_act"], j + 1)
                pe.matmul(bank(j, CD, n), FW2, PHASE[0:CD, 1, a:a + n], start=True, stop=True).then_inc(S["cond_mm"], 1)
            pe.wait_ge(S["cond_built"], 3)
            pe.wait_ge(S["consts_ready"], 2)

            with pe.Fori(0, LAYERS) as L:
                cond_norm(at("n1", L), CW[0], "cw0_in")
                qkv(at("qkv", L))
                attention(at("att", L), 4)
                t = at("wo", L)
                wait(pe, S["w3_in"], t("w3_in"), 16)
                wait(pe, S["oT_out"], t("oT_out"))
                wait(pe, S["t_out_d"], t("t_out_d"))
                update(t, [(T1, W[:, 3, :], KC)], ROWS[:, D:2 * D])
                cond_norm(at("n2", L), CW[1], "cw1_in")
                wait(pe, S["w0_in"], at("up", L)("w0_in"), 16)
                groups(at("up", L), W[:, 0, :], KC)
                t = at("down", L)
                wait(pe, S["w1_in"], t("w1_in"), 16)
                wait(pe, S["out_a"], t("out_a"))
                wait(pe, S["out_d"], t("out_d"))
                update(t, [(T2, W[:, 1, :], KC)], ROWS[:, 2 * D:3 * D])

            transposes(at("pre1"), V, "xn_ready")
            t = at("prop1")
            wait(pe, S["dense_ready"], t("dense_ready"))
            wait(pe, S["x_upd"], t("x_upd"))
            propagate(t, KC)
            t = at("conv1")
            wait(pe, S["out_a"], t("out_a"))
            wait(pe, S["out_d"], t("out_d"))
            wait(pe, S["yT_out"], t("yT_out"))
            wait(pe, S["w0_in"], t("w0_in"), 16)
            wait(pe, S["w1_in"], t("w1_in"), 16)
            wait(pe, S["row_in"], t("row_in"), 16)
            update(t, [(T1, W[:, 0, :], KC), (T2, W[:, 1, :], KC)], ROWS[:, 0:D])
            transposes(at("mid1"), V, "y_ready")
            t = at("prop2")
            propagate(t, KC)
            t = at("conv2")
            wait(pe, S["out_a"], t("out_a"))
            wait(pe, S["out_d"], t("out_d"))
            wait(pe, S["yT_out"], t("yT_out"))
            wait(pe, S["w2_in"], t("w2_in"), 16)
            wait(pe, S["w3_in"], t("w3_in"), 16)
            wait(pe, S["row2_in"], t("row2_in"), 16)
            update(t, [(T1, W[:, 2, :], KC), (T2, W[:, 3, :], KC)], ROWS[:, D:2 * D])
            transposes(at("z1"), None, "y_ready")
            qkv(at("qkv2"))
            attention(at("att2"), BH)
            t = at("wo2")
            wait(pe, S["w3_in"], t("w3_in"), 16)
            wait(pe, S["row_in"], t("row_in"), 16)
            wait(pe, S["oT_out"], t("oT_out"))
            wait(pe, S["t_out_d"], t("t_out_d"))
            update(t, [(T1, W[:, 3, :], KC)], ROWS[:, 0:D])
            transposes(at("z2"), None, "y_ready")
            t = at("up2")
            wait(pe, S["w0_in"], t("w0_in"), 16)
            groups(t, W[:, 0:2, :].rearrange("p a b -> p (a b)"), 2 * KC, width=2 * D, alternate=False)
            t = at("down2")
            wait(pe, S["w2_in"], t("w2_in"), 16)
            wait(pe, S["out_a"], t("out_a"))
            update(t, [(H8, W[:, 2:4, :].rearrange("p a b -> p (a b)"), 2 * KC)], ROWS[:, D:2 * D])
            transposes(at("pre3"), None, "xn_ready")
            t = at("r3")
            wait(pe, S["w0_in"], t("w0_in"), 16)
            wait(pe, S["row_in"], t("row_in"), 16)
            wait(pe, S["yT_out"], t("yT_out"))
            for g in range(NT):
                grp_free(pe, t, g)
                rows_of(bank(g % 4, P, 256), g, [(T1, W[:, 0, :], KC)], ROWS[:, 0:256], n=256).then_inc(S["grp_done"], 1)
            t = at("ct")
            wait(pe, S["out_a"], t("out_a"))
            wait(pe, S["out_d"], t("out_d"))
            for i in range(NT):
                wait(pe, S[f"c_in{i % 2}"], t(f"c_in{i % 2}"), 16 * (i // 2 + 1))
                if i >= 2:
                    wait(pe, S["dense_ready"], t("dense_ready"), i - 1)
                hv = halves(i % 2)
                for j in range(NT):
                    o = pe.transpose(hv[:, j // 2, (j % 2) * P:(j % 2 + 1) * P], CR[:, i % 2, j * P:(j + 1) * P], IDENT[0:P, 0:P])
                o.then_inc(S["ct_done"], 1)
            t = at("prop3")
            wait(pe, S["dense_ready"], t("dense_ready"))
            propagate(t, 2)
            t = at("conv3")
            wait(pe, S["w1_in"], t("w1_in"), 16)
            wait(pe, S["out_a"], t("out_a"))
            wait(pe, S["out_d"], t("out_d"))
            for i in range(NT):
                if i >= 4:
                    wait(pe, S["x_upd"], t("x_upd"), i - 3)
                for c in range(2):
                    o = pe.matmul(bank(i % 4), T2[:, c, i * P:(i + 1) * P], W[:, 1, c * D:(c + 1) * D], start=(c == 0), stop=(c == 1))
                o.then_inc(S["upd_done"], 1)


def kernel(**inputs):
    import concourse.bacc as _bacc
    from concourse import mybir as _mybir
    from concourse.bass_utils import run_bass_kernel_spmd as _run

    nc = _bacc.Bacc("TRN2", target_bir_lowering=False, num_devices=1)
    f = {k: np.asarray(v) for k, v in inputs.items()}

    def parts(w):
        *lead, k, m = w.shape
        w = w.reshape(*lead, k // 128, 128, m)
        return np.moveaxis(w, -3, -2).reshape(*lead, 128, k // 128 * m)

    def cols(b):
        return np.moveaxis(b.reshape(*b.shape[:-1], -1, 128), -1, -2)

    src, dst = f["src"].reshape(P, EC), f["dst"].reshape(P, EC)
    L0, L1, L2, L3 = (lambda n, k=k: f[f"L{k}_gnn_{n}"] for k in range(4))
    arr = {
        "x": f["x"],
        "src_pc": src, "dst_pc": dst,
        "src_cp": np.ascontiguousarray(src.T).reshape(P, EC), "dst_cp": np.ascontiguousarray(dst.T).reshape(P, EC),
        "edge_attr": f["edge_attr_8"].reshape(P, EC * BH),
        "noise": f["node_vec1"].reshape(1, N),
        "f_w1": L0("f_w1"), "f_w2": L0("f_w2"), "f_b": np.stack([L0("f_b1"), L0("f_b2")], 1),
        "w0": np.stack([parts(L0(n)) for n in ("wq", "wk", "wv", "wo", "m_w1", "m_w2")], 1),
        "colb": np.concatenate([cols(L0(n)) for n in ("bq", "bk", "m_b1")], 2),
        "rowb": np.concatenate([L0(n) for n in ("bv", "bo", "m_b2")], 1),
        "cw": np.stack([np.concatenate([np.concatenate([L0(f"s{k}_w"), L0(f"b{k}_w")], 2),
                                        np.concatenate([L0(f"s{k}_b"), L0(f"b{k}_b")], 1)[:, None, :]], 1) for k in (1, 2)], 1),
        "w1": np.stack([parts(L1(n)) for n in ("W1_0", "W1_1", "W2_0", "W2_1")]),
        "l1_b1": L1("b1").reshape(1, D), "l1_b2": L1("b2").reshape(1, D),
        "l1_gamma": L1("gamma").reshape(1, D), "l1_beta": L1("beta").reshape(1, D),
        "w2": np.stack([parts(L2(n).T) for n in ("Wq", "Wk", "Wv", "Wo")]),
        "l2_colb": np.concatenate([cols(L2("bq")), cols(L2("bk"))], 1),
        "l2_bv": L2("bv").reshape(1, D), "l2_bo_b2": np.concatenate([L2("bo"), L2("b2")]).reshape(1, 2 * D),
        "l2_lnb": np.stack([L2("ln_att_g"), L2("ln_att_b"), L2("ln_ff_g"), L2("ln_ff_b")]),
        "l2_b1": cols(L2("b1")), "l2_w1": parts(L2("W1").T), "l2_w2": parts(L2("W2").T),
        "l3_w1": parts(L3("W1")), "l3_w2": parts(L3("W2")),
        "l3_b1": L3("b1").reshape(1, 256), "l3_b2": L3("b2").reshape(1, D),
    }
    arr = {k: np.ascontiguousarray(a) for k, a in arr.items()}
    A = {k: nc.dram_tensor("in_" + k, a.shape, _mybir.dt.from_np(a.dtype), kind="ExternalInput").ap() for k, a in arr.items()}
    A["out"] = nc.dram_tensor("out", (N, D), _mybir.dt.float32, kind="ExternalOutput").ap()
    build(nc, A)
    r = _run(nc, [{"in_" + k: a for k, a in arr.items()}], core_ids=[0])
    return r.results[0]["out"]
```

```python
import numpy as np
import concourse.bass as bass
from concourse import mybir
from contextlib import ExitStack

F32 = mybir.dt.float32
BF16 = mybir.dt.bfloat16
I32 = mybir.dt.int32
U32 = mybir.dt.uint32
ALU = mybir.AluOpType
ACT = mybir.ActivationFunctionType
AX = mybir.AxisListType

N, D, E = 1250, 512, 20000
P, NT = 125, 10
KC = D // 128
EC = E // P
G = 8
NG = EC // G
BH = 8
LAYERS = 4
CHUNKS = [(0, 500), (500, 500), (1000, 250)]
NO_EDGE = -1.0e30
EPS = 1e-5
CD = 16
WP = 3 * BH + 1
SK = 111
BIAS_ROW = 96
CR_ROWS = CD + 2
STACK = [(0, 0, 0), (1, 0, 18), (2, 0, 36), (0, 1, 54), (1, 1, 72), (0, 2, 90)]
HEADROOM = 40.0
COND_GROUP, NORM_GROUP = 3, 6
CLEAR_STEP, CLEAR_LATE = 5, 14
CLEARED = CLEAR_STEP * (NG - 2)
V_LOOP_STEPS = 41


class At:

    def __init__(self, base, per=0, layer=None):
        self.base, self.per, self.layer = base, per, layer

    def value(self, k):
        return self.base + k if self.layer is None else self.layer * self.per + (self.base + k)


def wait(eng, sem, at, k=0):
    if at.layer is not None:
        assert at.base + k > 0, "a loop's wait must be positive in its first turn"
    if at.base + k > 0:
        eng.wait_ge(sem, at.value(k))


def build(nc, A):
    ctx = ExitStack()
    with ctx:
        WORDS = 53200
        arena = ctx.enter_context(nc.sbuf_tensor("arena", [128, WORDS], F32))
        top = [0]

        def region(words):
            a = top[0]
            top[0] += words
            assert top[0] <= WORDS, top[0]
            return a

        def view(at, rows, *shape):
            ap = arena[0:rows, at:at + int(np.prod(shape))]
            if len(shape) == 2:
                ap = ap.rearrange("p (a b) -> p a b", a=shape[0])
            if len(shape) == 3:
                ap = ap.rearrange("p (a b c) -> p a b c", a=shape[0], b=shape[1])
            return ap

        aX, aV = region(NT * D), region(NT * D)
        aT1, aT2, aT3 = region(KC * N), region(KC * N), region(KC * N)
        aP, aPT, aLC = region(2 * N), region(2 * N), region(2 * N)
        aW = region(4 * KC * D)
        aR = region(BH * N)
        aO = region(D)
        SMALL = 1500
        X = view(aX, P, NT, D)
        V = view(aV, P, NT, D)
        T1 = view(aT1, 128, KC, N)
        T2 = view(aT2, 128, KC, N)
        T3 = view(aT3, 128, KC, N)
        H8 = view(aT2, 128, 2 * KC, N)
        DENSE = view(aT3, P, NT, N)
        LC = view(aLC, P, 2, N)
        PR = view(aP, P, 2, N)
        PT = view(aPT, P, 2, NT * P)
        W = view(aW, 128, 4, KC * D)
        BIA = [view(aLC, P, N, BH), view(aR, P, N, BH)]
        CR = view(aW + 2 * KC * D, P, 2, N)
        OS = view(aO, P, D)
        r = aR
        CONDS = view(r, SK, N // 2).bitcast(BF16)
        DINVB = view(r, P, N); r += N // 2
        CWR = view(r, SK, 2 * D); r += 2 * D
        CWH, CWM = [view(r + k * D, SK, D).bitcast(BF16) for k in range(2)]; r += 2 * D
        CWS = [view(r + k * D, SK, D).bitcast(BF16) for k in range(2)]; r += 2 * D
        XN = view(r, P, 2, D); r += 2 * D
        Y = view(r, P, 2, D); r += 2 * D
        ATTR = view(r, P, EC * BH); r += EC * BH
        GB = view(r, P, 2, D); r += 2 * D
        NEG = view(r, P, 625); r += 625
        assert r <= aR + BH * N
        s = [region(SMALL)]

        def small(rows, *shape):
            v = view(s[0], rows, *shape)
            s[0] += int(np.prod(shape))
            assert s[0] <= aO + D + SMALL, s[0]
            return v

        IDENT, ONES = small(128, 128), small(128, 128)
        COLB, QBS = small(128, 12), small(128, 4)
        BN, MV = small(P, NT, 6), small(P, NT, 2)
        VARC = small(P, NT)
        STD, RSTD, NMR = small(P, NT), small(P, NT), small(P, NT)
        DEG, FLAG, DINV, DEG1 = small(P, NT), small(P, NT), small(P, NT), small(P, NT)
        PARTM = small(SK, 3)
        BSEL = small(SK, 64).bitcast(BF16)[:, 0:P]
        EPSC = small(128, 1)
        MX, NMX = small(P, 2, BH), small(P, 2)
        DEN, RD = small(P, 2, BH), small(P, 2, BH)
        GMX, GALL, SHIFT, BACK = small(P, 1), small(P, 1), small(P, 1), small(P, 1)
        FRQ = small(64, 5)
        FW1, FW2, FB = small(64, CD), small(CD, CD), small(CD, 2)
        LATE, IDLE = small(P, G), small(P, 1)
        KEYI, WIDX = small(P, EC).bitcast(I32), small(P, EC).bitcast(I32)
        MRG = small(P, 5, G * BH)
        NGRP = small(P, EC)

        e = aV
        KEY, SPARE, KEYC = view(e, P, EC), view(e + EC, P, EC), view(e + 2 * EC, P, EC); e += 3 * EC
        SRC, DST, SRCG, DSTG = [view(e + k * EC, P, EC) for k in range(4)]; e += 4 * EC
        SRCI, DSTI, SRCJ, DSTJ = [view(e + k * EC, P, EC).bitcast(I32) for k in range(4)]; e += 4 * EC
        IDX = view(e, P, EC); e += EC
        CNT = view(e, P, EC); e += EC
        EX = view(e, P, EC * BH); e += EC * BH
        TRI = view(e, P, P); e += P
        TRIB = view(e, P, 64).bitcast(BF16)[:, 0:P]; e += 64
        assert e <= aV + NT * D
        e = aT1
        KEYB = view(e, P, 2, G * P); e += 2 * G * P
        EPART = view(e, P, EC * (WP + 1) // 2).bitcast(BF16).rearrange("p (c w) -> p c w", w=WP + 1); e += EC * (WP + 1) // 2
        EQW = G * (G * P + P)
        EQ = [view(e + k * EQW // 2, P, EQW // 2).bitcast(BF16) for k in range(2)]; e += EQW
        assert e <= aP
        e = aPT
        SUMS = view(e, P, EC, WP); e += EC * WP
        assert e <= aW
        EQD = [view(aP + k * G * P // 2, P, G * P // 2).bitcast(BF16).rearrange("p (c x) -> p c x", c=G) for k in range(2)]
        TMP = view(aP + G * P, P, EC * BH)
        ZERO = view(aW, P, N)
        PHASE = view(aW + N, 64, 2, N)
        CONDF = view(aW + 3 * N, CR_ROWS, N)
        CONDP = view(aW + 4 * N, CR_ROWS, 3 * N // 2).bitcast(BF16).rearrange("p (k n) -> p k n", k=3)

        banks = ctx.enter_context(nc.psum_tensor("banks", [128, 8, 512], F32))

        def bank(b, rows=P, n=512):
            return banks[0:rows, b, 0:n]

        def halves(k):
            return banks[0:P, 3 * k:3 * k + 3, :].rearrange("p b x -> p (b x)").rearrange("p (h x) -> p h x", x=256)[:, 0:5, 0:250]

        def pairs(ap):
            return ap.rearrange("p (h x) -> p h x", x=250)

        cnt_tab = nc.dram_tensor("cnt_tab", [N * N + E, 1], F32)
        bia_tab = nc.dram_tensor("bia_tab", [N * N, BH], F32)
        key_dram = nc.dram_tensor("key_dram", [E], F32)
        dinv_dram = nc.dram_tensor("dinv_dram", [NT, P], F32)
        x_dram = nc.dram_tensor("x_dram", [N, D], F32)
        cnt_rows = cnt_tab[0:N * N, :].rearrange("(t p d) o -> t p (d o)", t=NT, p=P)
        bia_rows = bia_tab[:, :].rearrange("(t p d) h -> t p (d h)", t=NT, p=P)
        x_rows = A["x"].rearrange("(t p) d -> t p d", p=P)
        xs_rows = x_dram[:, :].rearrange("(t p) d -> t p d", p=P)
        out_rows = A["out"].rearrange("(t p) d -> t p d", p=P)

        def clear_biases(eng, a, n, done):
            rows = bia_tab[:, :].rearrange("(p a) h -> p (a h)", p=P).rearrange("p (b c) -> p b c", c=625)
            eng.dma_start(rows[:, a:a + n, :], NEG.unsqueeze(1).to_broadcast([P, n, 625])).then_inc(S[done], 16)

        names = """ends_in edges_in noise_in zero_ready cnt_zeroed neg_ready bia_cleared bia_cleared_late keyc_ready keyc_out keyb_in0 keyb_in1
            consts_ready gmax_ready gmax_all shift_ready exp_ready eq_ready eqd_ready grp_sum sums_out idx_ready
            counted lsum_ready lse_log lse_ready gathered mrg_diff mrg_exp mrg_log mrg_ready scattered
            lc_pre lc_log lc_ready phase_ready emb_ready emb_mm emb_act cond_mm cond_built cond_parts conds_clear
            conds_in cwr_in cws_ready
            x_in res_in0 res_in1 stats_ready std_ready rstd_ready xn_ready cond_ready y_ready yT_ready yT_out
            w0_in w1_in w2_in w3_in col_in gb_in gb_used qbs_ready grp_done out_a out_d upd_done x_upd
            lct_in0 lct_in1 bia_in0 bia_in1 s_done max_ready negmax p_ready t_done t_out_a t_out_d pv_done o_ready oT_done oT_out
            deg_clip deg_sqrt dinv_ready dinv_out dinv_in dense_in dense_ready x_saved c_in0 c_in1 ct_done
            final_ready final_out v_step gate sp_passed""".split()
        S = {n: ctx.enter_context(nc.semaphore(n)) for n in names}
        block = ctx.enter_context(nc.Block())

        timeline = []

        def stage(name, **adds):
            timeline.append((name, adds))

        def norm_stage(name, kind, transposed=True, **more):
            adds = dict(stats_ready=1, std_ready=1, rstd_ready=1, xn_ready=NT, **more)
            if kind != "relu":
                adds.update(y_ready=NT)
            if kind == "cond":
                adds.update(cond_ready=NT)
            if transposed:
                adds.update(yT_ready=NT, yT_out=NT)
            stage(name, **adds)

        def att_stage(name, heads, **more):
            n = heads * NT
            stage(name, s_done=n, max_ready=n, negmax=n, p_ready=n, t_done=n, t_out_a=n, t_out_d=n, pv_done=n,
                  o_ready=NT, oT_done=NT, oT_out=NT, **more)

        stage("start", x_in=16 * NT, cws_ready=1)
        norm_stage("pre0", "relu", transposed=False)
        stage("loop")
        norm_stage("n1", "cond")
        stage("qkv", w0_in=16, w1_in=16, w2_in=16, col_in=16, cws_ready=1, qbs_ready=1, grp_done=34, out_a=17, out_d=17)
        att_stage("att", 4, lct_in0=8 * NT, lct_in1=8 * NT, lc_pre=NT, lc_log=NT, lc_ready=NT, gathered=16 * EC // LAYERS,
                  mrg_diff=NG // LAYERS, mrg_exp=NG // LAYERS, mrg_log=NG // LAYERS, mrg_ready=NG // LAYERS)
        stage("wo", w3_in=16, upd_done=NT, x_upd=NT)
        norm_stage("n2", "cond")
        stage("up", w0_in=16, cws_ready=1, grp_done=12, out_a=6, out_d=6)
        stage("down", w1_in=16, upd_done=NT, x_upd=NT)
        stage("end")
        stage("res1", res_in0=8 * NT, res_in1=8 * NT, x_upd=NT)
        norm_stage("pre1", "relu")
        stage("dense", dense_in=16, dense_ready=NT)
        stage("prop1", grp_done=12, out_a=6, out_d=6)
        stage("conv1", w0_in=16, w1_in=16, upd_done=NT, x_upd=NT)
        norm_stage("mid1", "affine", gb_in=32)
        stage("prop2", grp_done=12, out_a=6, out_d=6)
        stage("conv2", w2_in=16, w3_in=16, upd_done=NT, x_upd=NT)
        norm_stage("pre2", "relu", transposed=False)
        norm_stage("z1", "affine", gb_in=32, cws_ready=1)
        stage("qkv2", w0_in=16, w1_in=16, w2_in=16, col_in=16, qbs_ready=1, grp_done=34, out_a=17, out_d=17)
        att_stage("att2", BH, cws_ready=1, bia_in0=8 * NT, bia_in1=8 * NT)
        stage("wo2", w3_in=16, upd_done=NT, x_upd=NT)
        norm_stage("z2", "affine", gb_in=32, cws_ready=1)
        stage("up2", w0_in=16, col_in=16, grp_done=24, out_a=24)
        stage("down2", w2_in=16, upd_done=NT, x_upd=NT)
        stage("res2", res_in0=8 * NT, res_in1=8 * NT, x_upd=NT)
        norm_stage("pre3", "relu")
        stage("r3", w0_in=16, grp_done=NT, out_a=NT // 2, out_d=NT // 2)
        stage("ct", c_in0=8 * NT, c_in1=8 * NT, ct_done=NT, dense_ready=NT)
        stage("prop3", grp_done=6, out_a=3, out_d=3)
        stage("conv3", w1_in=16, gb_in=16, upd_done=NT)
        order = [n for n, _ in timeline]
        per = {n: sum(a.get(n, 0) for _, a in timeline[order.index("loop"):order.index("end")]) for n in names}

        def at(name, layer=None):
            k = order.index(name)
            inside = order.index("loop") < k < order.index("end")
            assert inside == (layer is not None), name

            def get(sem):
                base = sum(a.get(sem, 0) for _, a in timeline[:k])
                if inside:
                    return At(base, per[sem], layer)
                return At(base + (LAYERS - 1) * per[sem] * (k >= order.index("end")))
            return get

        def grp_free(eng, t, g, alternate=True):
            if g < 4:
                return
            if not alternate:
                wait(eng, S["out_a"], t("out_a"), g - 3)
            elif g % 2 == 0:
                wait(eng, S["out_a"], t("out_a"), (g - 4) // 2 + 1)
            else:
                wait(eng, S["out_d"], t("out_d"), (g - 4) // 2 + 1)

        @block.sync
        def _(sp):
            def load(dst, src, name):
                sp.dma_start(dst, src).then_inc(S[name], 16)

            def zero_counts():
                sp.wait_ge(S["zero_ready"], 1)
                for i in range(NT):
                    load(cnt_rows[i], ZERO, "cnt_zeroed")
                load(cnt_tab[N * N:N * N + E, :].rearrange("(p b) o -> p (b o)", p=P), ZERO[:, 0:EC], "cnt_zeroed")

            def spread_condition():
                sp.wait_ge(S["cond_parts"], 1)
                sp.wait_ge(S["conds_clear"], 1)
                for part, _, row in STACK:
                    if row < BIAS_ROW < row + CR_ROWS:
                        k = BIAS_ROW - row
                        load(CONDS[row:BIAS_ROW, :], CONDP[0:k, part, :], "conds_in")
                        load(CONDS[BIAS_ROW + 3:SK, :], CONDP[k:CR_ROWS, part, :], "conds_in")
                    else:
                        load(CONDS[row:row + CR_ROWS, :], CONDP[:, part, :], "conds_in")

            def loop_wait(name, at_, k=0):
                wait(sp, S[name], at_, k)
                sp.sem_inc(S["sp_passed"], 1)

            for dst, key in ((SRCJ, "src_cp"), (DSTJ, "dst_cp")):
                load(dst, A[key], "ends_in")
            load(PHASE[:, 0, :], A["noise"].to_broadcast([64, N]), "noise_in")
            load(PARTM, A["part_mask"], "noise_in")
            load(CWR, A["cw"][0, 0], "cwr_in")
            load(FW1, A["f_w1"], "noise_in")
            load(FW2, A["f_w2"], "noise_in")
            load(FB, A["f_b"], "noise_in")
            for dst, key in ((SRCI, "src_pc"), (DSTI, "dst_pc"), (ATTR, "edge_attr")):
                load(dst, A[key], "edges_in")
            sp.wait_ge(S["keyc_ready"], 1)
            load(key_dram[:].rearrange("(p c) -> p c", p=P), KEYC, "keyc_out")
            sp.wait_ge(S["keyc_out"], 16)
            kd = key_dram[:].rearrange("(g n) -> g n", g=NG)
            for g in range(NG):
                if g == COND_GROUP + 2:
                    spread_condition()
                if g >= 2:
                    sp.wait_ge(S["eq_ready"], g - 1)
                load(KEYB[:, g % 2, :], kd[g:g + 1, :].to_broadcast([P, G * P]), f"keyb_in{g % 2}")
                if g == 1:
                    zero_counts()
                    for i in range(NT):
                        load(X[:, i, :], x_rows[i], "x_in")
                    sp.wait_ge(S["neg_ready"], 1)
                if g >= 2:
                    clear_biases(sp, CLEAR_STEP * (g - 2), CLEAR_STEP, "bia_cleared")
            sp.wait_ge(S["cnt_zeroed"], 16 * (NT + 1))
            sp.wait_ge(S["conds_in"], 16 * (len(STACK) + 1))

            with sp.Fori(0, LAYERS) as L:
                w0 = A["w0"][bass.ds(L, 1), :, :, :].rearrange("o m p x -> (o m) p x")
                for k in range(3):
                    load(W[:, k, :], w0[k], f"w{k}_in")
                load(COLB, A["colb"][bass.ds(L, 1), :, :].rearrange("o p x -> (o p) x"), "col_in")
                load(W[:, 3, :], w0[3], "w3_in")
                loop_wait("cws_ready", at("n1", L)("cws_ready"))
                load(CWR, A["cw"][bass.ds(L, 1), 1, :, :].rearrange("o p x -> (o p) x"), "cwr_in")
                t = at("att", L)
                sp.wait_ge(S["counted"], 16 * EC)
                sp.wait_ge(S["lse_ready"], 1)
                for i in range(NT):
                    if i >= 2:
                        loop_wait("max_ready", t("max_ready"), 4 * (i - 1))
                    load(LC[:, i % 2, :], cnt_rows[i], f"lct_in{i % 2}")
                    if i == 1:
                        loop_wait("grp_done", t("grp_done"))
                        load(W[:, 0, :], w0[4], "w0_in")
                        load(W[:, 1, :], w0[5], "w1_in")
                        loop_wait("cws_ready", t("cws_ready"))
                        load(CWR, A["cw"][bass.ds(L + 1, 1), 0, :, :].rearrange("o p x -> (o p) x"), "cwr_in")
                t = at("down", L)
                loop_wait("x_upd", t("x_upd"), NT)

            t = at("res1")
            for i in range(NT):
                if i >= 2:
                    wait(sp, S["x_upd"], t("x_upd"), i - 1)
                load(Y[:, i % 2, :], x_rows[i], f"res_in{i % 2}")
            load(DENSE, cnt_rows.rearrange("t p d -> p t d"), "dense_in")
            load(W[:, 0, :], A["w1"][0], "w0_in")
            load(W[:, 1, :], A["w1"][1], "w1_in")
            load(GB[:, 0, :], A["l1_gamma"].to_broadcast([P, D]), "gb_in")
            load(GB[:, 1, :], A["l1_beta"].to_broadcast([P, D]), "gb_in")
            load(W[:, 2, :], A["w1"][2], "w2_in")
            load(W[:, 3, :], A["w1"][3], "w3_in")
            sp.wait_ge(S["dinv_ready"], 1)
            with nc.allow_non_contiguous_dma(reason="ten words of each partition, 5 KB in all"):
                load(dinv_dram[:, :].rearrange("t p -> p t"), DINV, "dinv_out")
            sp.wait_ge(S["dinv_out"], 16)
            load(DINVB, dinv_dram[:, :].rearrange("(o t) p -> o (t p)", o=1).to_broadcast([P, N]), "dinv_in")
            t = at("pre2")
            wait(sp, S["x_upd"], t("x_upd"))
            for i in range(NT):
                load(xs_rows[i], X[:, i, :], "x_saved")
            wait(sp, S["gb_used"], At(0), 1)
            load(CWR, A["later_rows"][0], "cwr_in")
            for k in range(2):
                load(GB[:, k, :], A["l2_lnb"][k:k + 1, :].to_broadcast([P, D]), "gb_in")
            for k in range(3):
                load(W[:, k, :], A["w2"][k], f"w{k}_in")
            load(COLB[:, 0:8], A["l2_colb"], "col_in")
            t = at("att2")
            wait(sp, S["grp_done"], t("grp_done"))
            wait(sp, S["yT_out"], t("yT_out"))
            wait(sp, S["out_a"], t("out_a"))
            wait(sp, S["out_d"], t("out_d"))
            sp.wait_ge(S["scattered"], 16 * EC)
            for i in range(NT):
                if i >= 2:
                    wait(sp, S["max_ready"], t("max_ready"), BH * (i - 1))
                load(BIA[(i + 1) % 2].rearrange("p d h -> p (d h)"), bia_rows[i], f"bia_in{i % 2}")
            wait(sp, S["max_ready"], t("max_ready"), BH * (NT - 1))
            load(CWR, A["later_rows"][1], "cwr_in")
            wait(sp, S["max_ready"], t("max_ready"), BH * NT)
            load(W[:, 3, :], A["w2"][3], "w3_in")
            for k in range(2):
                load(GB[:, k, :], A["l2_lnb"][2 + k:3 + k, :].to_broadcast([P, D]), "gb_in")
            load(COLB[:, 0:8], A["l2_b1"], "col_in")
            load(W[:, 0:2, :].rearrange("p a b -> p (a b)"), A["l2_w1"], "w0_in")
            wait(sp, S["cws_ready"], at("wo2")("cws_ready"))
            load(CWR, A["later_rows"][2], "cwr_in")
            t = at("z2")
            wait(sp, S["upd_done"], t("upd_done"))
            load(W[:, 2:4, :].rearrange("p a b -> p (a b)"), A["l2_w2"], "w2_in")
            t = at("res2")
            wait(sp, S["x_upd"], t("x_upd"))
            sp.wait_ge(S["x_saved"], 16 * NT)
            for i in range(NT):
                if i >= 2:
                    wait(sp, S["x_upd"], t("x_upd"), i - 1)
                load(Y[:, i % 2, :], xs_rows[i], f"res_in{i % 2}")
            load(W[:, 0, 0:1024], A["l3_w1"], "w0_in")
            load(W[:, 1, 0:1024], A["l3_w2"], "w1_in")
            load(GB[:, 0, :], A["l3_b2"].to_broadcast([P, D]), "gb_in")
            t = at("ct")
            for i in range(NT):
                if i >= 2:
                    wait(sp, S["ct_done"], t("ct_done"), i - 1)
                load(CR[:, i % 2, :], cnt_rows[i], f"c_in{i % 2}")
            for i in range(NT):
                sp.wait_ge(S["final_ready"], i + 1)
                load(out_rows[i], X[:, i, :], "final_out")
            sp.wait_ge(S["final_out"], 16 * NT)

        @block.gpsimd
        def _(gp):
            gp.memset(ONES, 1.0).then_inc(S["consts_ready"], 1)
            gp.memset(NEG, NO_EDGE).then_inc(S["neg_ready"], 1)
            gp.wait_ge(S["consts_ready"], 1)
            gp.wait_ge(S["neg_ready"], 1)
            gp.affine_select(out=IDENT, in_=ONES, compare_op=ALU.is_equal, fill=0.0, base=0,
                             pattern=[[1, 128]], channel_multiplier=-1).then_inc(S["consts_ready"], 1)
            gp.affine_select(out=TRI, in_=ONES[0:P, 0:P], compare_op=ALU.is_gt, fill=0.0, base=0,
                             pattern=[[1, P]], channel_multiplier=-1).then_inc(S["consts_ready"], 1)
            for k in range(2):
                gp.wait_ge(S["consts_ready"], 3 + k)
                gp.iota(FRQ[32 * k:32 * k + 32, 0:1].bitcast(I32), pattern=[[0, 1]], base=1,
                        channel_multiplier=1).then_inc(S["consts_ready"], 1)
            gp.wait_ge(S["consts_ready"], 5)
            gp.iota(SRCG.bitcast(I32), pattern=[[1, EC]], base=N * N, channel_multiplier=EC).then_inc(S["consts_ready"], 1)
            gp.wait_ge(S["gmax_ready"], 1)
            gp.wait_ge(S["consts_ready"], 6)
            gp.partition_all_reduce(GALL, GMX, P, bass.bass_isa.ReduceOp.max).then_inc(S["gmax_all"], 1)
            gp.wait_ge(S["cnt_zeroed"], 16 * (NT + 1))
            for g in range(NG):
                gp.wait_ge(S["idx_ready"], g + 1)
                gp.wait_ge(S["sums_out"], g + 1)
                if g:
                    gp.wait_ge(S["counted"], 16 * G * g)
                for k in range(G * g, G * g + G):
                    gp.indirect_dma_start(out=cnt_tab[:, :], out_offset=bass.IndirectOffsetOnAxis(ap=WIDX[:, k:k + 1].bitcast(U32), axis=0),
                                          in_=NGRP[:, k:k + 1], in_offset=None, bounds_check=N * N + E - 1, oob_is_err=True,
                                          compute_op=ALU.add).then_inc(S["counted"], 16)
            for a in range(CLEARED, 160, CLEAR_LATE):
                clear_biases(gp, a, CLEAR_LATE, "bia_cleared_late")
            gp.wait_ge(S["bia_cleared"], 16 * (NG - 2))
            gp.wait_ge(S["bia_cleared_late"], 16 * ((160 - CLEARED) // CLEAR_LATE))
            gp.wait_ge(S["lse_ready"], 1)
            for g in range(NG):
                if g:
                    gp.wait_ge(S["scattered"], 16 * G * g)
                for k in range(G * g, G * g + G):
                    c = k % G
                    gp.indirect_dma_start(out=MRG[:, 0, c * BH:(c + 1) * BH], out_offset=None, in_=bia_tab[:, :],
                                          in_offset=bass.IndirectOffsetOnAxis(ap=KEYI[:, k:k + 1].bitcast(U32), axis=0)).then_inc(S["gathered"], 16)
                gp.wait_ge(S["mrg_ready"], g + 1)
                for k in range(G * g, G * g + G):
                    c = k % G
                    gp.indirect_dma_start(out=bia_tab[:, :], out_offset=bass.IndirectOffsetOnAxis(ap=WIDX[:, k:k + 1].bitcast(U32), axis=0),
                                          in_=MRG[:, 4, c * BH:(c + 1) * BH], in_offset=None, bounds_check=N * N - 1,
                                          oob_is_err=False).then_inc(S["scattered"], 16)
            gp.wait_ge(S["scattered"], 16 * EC)

        @block.vector
        def _(v):
            mine = [0, None]

            def step(ins):
                mine[0] += 1
                ins.then_inc(S["v_step"], 1)
                v.wait_ge(S["v_step"], mine[0] if mine[1] is None else mine[1] * V_LOOP_STEPS + mine[0])

            def norm(t, src, kind, dst=None, slope=None, source=None):
                if source is not None:
                    v.wait_ge(S["x_in"], 16 * NT)
                    for i in range(NT):
                        o = v.bn_stats(BN[:, i, :], src[:, i, :])
                    step(o)
                v.memset(IDLE, 0.0)
                for i in range(NT):
                    o = v.bn_aggr(MV[:, i, :], BN[:, i, :])
                step(o)
                v.tensor_scalar(VARC, MV[:, :, 1], EPS, None, ALU.add).then_inc(S["stats_ready"], 1)
                wait(v, S["std_ready"], t("std_ready"), 1)
                step(v.reciprocal(RSTD, STD))
                v.scalar_tensor_tensor(NMR, MV[:, :, 0], -1.0, RSTD, ALU.mult, ALU.mult).then_inc(S["rstd_ready"], 1)
                if kind == "relu":
                    return
                if kind == "affine":
                    wait(v, S["gb_in"], t("gb_in"), 32)
                for i in range(NT):
                    y = Y[:, i % 2, :] if dst is None else dst[:, i, :]
                    wait(v, S["xn_ready"], t("xn_ready"), i + 1)
                    if i >= 2 and dst is None:
                        wait(v, S["yT_ready"], t("yT_ready"), i - 1)
                    if kind == "cond":
                        wait(v, S["cond_ready"], t("cond_ready"), i + 1)
                        b = 2 * (i % 2)
                        v.tensor_tensor(y, XN[:, i % 2, :], bank(b), ALU.mult).then_inc(S["gate"], 1)
                        wait_gate()
                        v.tensor_tensor(y, y, bank(b + 1), ALU.add).then_inc(S["y_ready"], 1)
                    else:
                        v.tensor_tensor(y, XN[:, i % 2, :], GB[:, 0, :], ALU.mult).then_inc(S["gate"], 1)
                        wait_gate()
                        if slope is None:
                            v.tensor_tensor(y, y, GB[:, 1, :], ALU.add).then_inc(S["y_ready"], 1)
                        else:
                            v.tensor_tensor(y, y, GB[:, 1, :], ALU.add).then_inc(S["gate"], 1)
                            wait_gate()
                            v.scalar_tensor_tensor(y, y, slope, y, ALU.mult, ALU.max).then_inc(S["y_ready"], 1)

            gates = [0]
            GATES_PER_LAYER = 2 * NT

            def wait_gate():
                gates[0] += 1
                v.wait_ge(S["gate"], gates[0] if mine[1] is None else mine[1] * GATES_PER_LAYER + gates[0])

            def update(t, dst, add=True, stats=True):
                for i in range(NT):
                    wait(v, S["upd_done"], t("upd_done"), i + 1)
                    if add:
                        o = v.tensor_tensor(dst[:, i, :], dst[:, i, :], bank(i % 4), ALU.add)
                    else:
                        o = v.tensor_copy(dst[:, i, :], bank(i % 4))
                    o.then_inc(S["x_upd"], 1)
                    if stats and i:
                        wait(v, S["x_upd"], t("x_upd"), i)
                        v.bn_stats(BN[:, i - 1, :], dst[:, i - 1, :])
                if stats:
                    wait(v, S["x_upd"], t("x_upd"), NT)
                    step(v.bn_stats(BN[:, NT - 1, :], dst[:, NT - 1, :]))

            def residual(t, stats=True):
                for i in range(NT):
                    wait(v, S[f"res_in{i % 2}"], t(f"res_in{i % 2}"), 16 * (i // 2 + 1))
                    v.tensor_tensor(X[:, i, :], X[:, i, :], Y[:, i % 2, :], ALU.add).then_inc(S["x_upd"], 1)
                    if i:
                        wait(v, S["x_upd"], t("x_upd"), i)
                        v.bn_stats(BN[:, i - 1, :], X[:, i - 1, :])
                wait(v, S["x_upd"], t("x_upd"), NT)
                step(v.bn_stats(BN[:, NT - 1, :], X[:, NT - 1, :]))

            def qkv(t, scale):
                wait(v, S["col_in"], t("col_in"), 16)
                v.tensor_scalar(QBS, COLB[:, 0:4], scale, None, ALU.mult).then_inc(S["qbs_ready"], 1)
                g = 0
                for j, (a, n) in enumerate(CHUNKS):
                    for which, dst in ((0, T2), (1, T3)):
                        for m in range(KC):
                            if g % 2:
                                wait(v, S["grp_done"], t("grp_done"), g + 1)
                                b = COLB[:, 4 * which + m:4 * which + m + 1]
                                if which == 0:
                                    o = v.tensor_scalar(dst[:, m, a:a + n], bank(g % 4, 128, n), b, scale, ALU.add, ALU.mult)
                                else:
                                    o = v.tensor_scalar(dst[:, m, a:a + n], bank(g % 4, 128, n), b, None, ALU.add)
                                o.then_inc(S["out_d"], 1)
                            g += 1
                for i in range(NT):
                    if g % 2:
                        wait(v, S["grp_done"], t("grp_done"), g + 1)
                        v.tensor_copy(V[:, i, :], bank(g % 4)).then_inc(S["out_d"], 1)
                    g += 1

            def up(t, cols):
                g = 0
                for j, (a, n) in enumerate(CHUNKS):
                    for m in range(KC):
                        if g % 2:
                            wait(v, S["grp_done"], t("grp_done"), g + 1)
                            v.tensor_scalar(T2[:, m, a:a + n], bank(g % 4, 128, n), cols[:, m:m + 1], 0.0, ALU.add, ALU.max).then_inc(S["out_d"], 1)
                        g += 1

            def take_groups(t, dst, chunks):
                g = 0
                for j, (a, n) in enumerate(CHUNKS):
                    for m in range(chunks):
                        if g % 2:
                            wait(v, S["grp_done"], t("grp_done"), g + 1)
                            v.tensor_copy(dst[:, m, a:a + n], bank(g % 4, 128, n)).then_inc(S["out_d"], 1)
                        g += 1

            splits = [0]

            def split(dst, at_, extra=None):
                wait(v, S["cwr_in"], at_, 16)
                step(v.tensor_copy(CWH, CWR))
                step(v.tensor_tensor(CWR, CWR, CWH, ALU.subtract))
                step(v.tensor_copy(CWM, CWR))
                v.tensor_scalar(dst, CWH, PARTM[:, 0:1], None, ALU.mult)
                step(v.tensor_tensor(CWR, CWR, CWM, ALU.subtract))
                step(v.scalar_tensor_tensor(dst, CWM, PARTM[:, 1:2], dst, ALU.mult, ALU.add))
                v.scalar_tensor_tensor(dst, CWR, PARTM[:, 2:3], dst, ALU.mult, ALU.add).then_inc(S["cws_ready"], 1)

            def cwr(stage_name, layer=None):
                a = at(stage_name, layer)("cws_ready")
                return At(16 * a.base, 16 * a.per, layer)

            def log_counts(t, i, part):
                c = LC[:, i % 2, :]
                if part == 0:
                    wait(v, S[f"lct_in{i % 2}"], t(f"lct_in{i % 2}"), 16 * (i // 2 + 1))
                    v.tensor_scalar(c, c, float(2.0 ** -60), None, ALU.max).then_inc(S["lc_pre"], 1)
                else:
                    wait(v, S["lc_log"], t("lc_log"), i + 1)
                    v.scalar_tensor_tensor(c, c, 1.0e30, c, ALU.mult, ALU.min).then_inc(S["lc_ready"], 1)

            def merge(t, k, part):
                new = ATTR[:, bass.ds(t("gathered").layer * (EC // LAYERS * BH) + k * G * BH, G * BH)]
                if part == 0:
                    wait(v, S["gathered"], t("gathered"), 16 * G * (k + 1))
                    v.tensor_tensor(MRG[:, 1, :], MRG[:, 0, :], new, ALU.max)
                    step(v.tensor_tensor(MRG[:, 2, :], MRG[:, 0, :], new, ALU.min))
                    v.tensor_tensor(MRG[:, 2, :], MRG[:, 2, :], MRG[:, 1, :], ALU.subtract).then_inc(S["mrg_diff"], 1)
                else:
                    wait(v, S["mrg_log"], t("mrg_log"), k + 1)
                    v.tensor_tensor(MRG[:, 4, :], MRG[:, 1, :], MRG[:, 3, :], ALU.add).then_inc(S["mrg_ready"], 1)

            def attention(t, heads, third):
                steps = heads * NT

                def scores_max(n):
                    i, h = divmod(n, heads)
                    if n >= 2:
                        wait(v, S["t_done"], t("t_done"), n - 1)
                    wait(v, S["s_done"], t("s_done"), n + 1)
                    if third:
                        if h == 0:
                            wait(v, S[f"bia_in{i % 2}"], t(f"bia_in{i % 2}"), 16 * (i // 2 + 1))
                        add = BIA[(i + 1) % 2][:, :, h].rearrange("p (a x) -> p a x", x=250)
                    else:
                        if h == 0:
                            wait(v, S["lc_ready"], t("lc_ready"), i + 1)
                        add = pairs(LC[:, i % 2, :])
                    v.memset(IDLE, 0.0)
                    v.tensor_tensor_reduce(out=pairs(PR[:, n % 2, :]), in0=halves(n % 2), in1=add, scale=1.0, scalar=-3.0e38,
                                           op0=ALU.add, op1=ALU.max, accum_out=MX[:, i % 2, h:h + 1]).then_inc(S["max_ready"], 1)
                    wait(v, S["max_ready"], t("max_ready"), n + 1)
                    v.tensor_scalar(NMX[:, n % 2:n % 2 + 1], MX[:, i % 2, h:h + 1], -1.0, None, ALU.mult).then_inc(S["negmax"], 1)

                def take_blocks(n):
                    wait(v, S["t_done"], t("t_done"), n + 1)
                    if n >= 2:
                        wait(v, S["pv_done"], t("pv_done"), n - 1)
                    v.tensor_copy(pairs(PT[:, n % 2, :])[:, 0:2, :], halves(n % 2)[:, 0:2, :]).then_inc(S["t_out_d"], 1)

                def take_rows(i):
                    n = heads * (i + 1)
                    wait(v, S["p_ready"], t("p_ready"), n)
                    rd = RD[:, i % 2, 0:heads]
                    step(v.reciprocal(rd, DEN[:, i % 2, 0:heads]))
                    step(v.scalar_tensor_tensor(rd, MX[:, i % 2, 0:heads], 0.1 * NO_EDGE, rd, ALU.is_ge, ALU.mult))
                    wait(v, S["pv_done"], t("pv_done"), n)
                    if i >= 1:
                        wait(v, S["oT_done"], t("oT_done"), i)
                    v.tensor_tensor(OS.rearrange("p (h x) -> p h x", h=heads), bank(6 + i % 2).rearrange("p (h x) -> p h x", h=heads),
                                    rd.unsqueeze(2).to_broadcast([P, heads, D // heads]), ALU.mult).then_inc(S["o_ready"], 1)

                if not third:
                    for part in range(2):
                        for i in range(2):
                            log_counts(t, i, part)
                for n in range(steps + 2):
                    if n < steps:
                        scores_max(n)
                    if 1 <= n <= steps:
                        take_blocks(n - 1)
                    if n >= 2 and (n - 2) % heads == heads - 1:
                        take_rows((n - 2) // heads)
                    if not third and n < steps:
                        i, h = divmod(n, heads)
                        if 1 <= i < NT - 1 and h in (0, 2):
                            log_counts(t, i + 1, h // 2)
                        if n % 8 in (3, 6):
                            merge(t, n // 8, n % 8 // 4)

            v.memset(ZERO, 0.0).then_inc(S["zero_ready"], 1)
            v.memset(EPSC, EPS)
            v.wait_ge(S["ends_in"], 16 * 2)
            v.tensor_copy(DSTG, DSTJ)
            step(v.tensor_copy(KEYC, SRCJ))
            v.scalar_tensor_tensor(KEYC, KEYC, float(N), DSTG, ALU.mult, ALU.add).then_inc(S["keyc_ready"], 1)

            v.wait_ge(S["consts_ready"], 5)
            step(v.tensor_copy(FRQ[:, 1:2], FRQ[:, 0:1].bitcast(I32)))
            step(v.tensor_scalar(FRQ[:, 1:2], FRQ[:, 1:2], float(np.float32(2.0 * np.pi / 16)), None, ALU.mult))
            step(v.memset(FRQ[:, 2:4], 0.0))
            v.memset(FRQ[32:64, 2:3], 0.25)
            step(v.memset(FRQ[32:64, 3:4], float(np.float32(np.pi / 2))))
            v.wait_ge(S["noise_in"], 16 * 5)
            ph, turns = PHASE[:, 0, :], PHASE[:, 1, :]
            two_pi = 2 * np.pi
            p1 = 6.28125
            p2 = float(np.float32(two_pi - p1))
            step(v.tensor_scalar(ph, ph, FRQ[:, 1:2], None, ALU.mult))
            step(v.tensor_scalar(turns, ph, float(1.0 / two_pi), FRQ[:, 2:3], ALU.mult, ALU.add))
            step(v.tensor_scalar(turns, turns, float(1.5 * 2 ** 23), None, ALU.add))
            step(v.tensor_scalar(turns, turns, float(1.5 * 2 ** 23), None, ALU.subtract))
            for c in (p1, p2, two_pi - p1 - p2):
                step(v.scalar_tensor_tensor(ph, turns, -c, ph, ALU.mult, ALU.add))
            step(v.tensor_scalar(ph, ph, FRQ[:, 3:4], None, ALU.add))
            v.tensor_scalar(ph, ph, 3.1415925, -3.1415925, ALU.min, ALU.max).then_inc(S["phase_ready"], 1)
            v.memset(CONDS, 0.0).then_inc(S["conds_clear"], 1)
            v.memset(BSEL, 0.0)
            step(v.memset(CONDF, 1.0))
            v.memset(BSEL[BIAS_ROW:BIAS_ROW + 3, :], 1.0)
            split(CWS[0], At(0))

            v.wait_ge(S["edges_in"], 16 * 3)
            v.tensor_copy(SRC, SRCI)
            step(v.tensor_copy(DST, DSTI))
            step(v.scalar_tensor_tensor(KEY, SRC, float(N), DST, ALU.mult, ALU.add))
            v.tensor_copy(KEYI, KEY)
            v.reduce_max(GMX, ATTR, AX.X).then_inc(S["gmax_ready"], 1)
            v.wait_ge(S["consts_ready"], 6)
            step(v.tensor_copy(SPARE, SRCG.bitcast(I32)))
            v.tensor_tensor(SPARE, SPARE, KEY, ALU.subtract)
            v.wait_ge(S["gmax_all"], 1)
            v.tensor_scalar(BACK, GALL, HEADROOM, None, ALU.subtract)
            v.tensor_scalar(SHIFT, GALL, -1.0, HEADROOM, ALU.mult, ALU.add).then_inc(S["shift_ready"], 1)
            v.wait_ge(S["exp_ready"], 1)
            ex = EX.rearrange("p (c h) -> p c h", h=BH)
            step(v.tensor_copy(EPART[:, :, 0:BH], ex))
            step(v.tensor_tensor(ex, ex, EPART[:, :, 0:BH], ALU.subtract))
            step(v.tensor_copy(EPART[:, :, BH:2 * BH], ex))
            step(v.tensor_tensor(ex, ex, EPART[:, :, BH:2 * BH], ALU.subtract))
            v.tensor_copy(EPART[:, :, 2 * BH:3 * BH], ex)
            v.memset(EPART[:, :, 3 * BH:WP + 1], 1.0)
            step(v.tensor_copy(TRIB, TRI))

            def compare(g):
                v.wait_ge(S[f"keyb_in{g % 2}"], 16 * (g // 2 + 1))
                if g >= 2:
                    v.wait_ge(S["grp_sum"], g - 1)
                q = EQ[g % 2]
                for c in range(G):
                    o = v.tensor_scalar(q[:, c * G * P:(c + 1) * G * P], KEYB[:, g % 2, :], KEY[:, G * g + c:G * g + c + 1], None, ALU.is_equal)
                o.then_inc(S["eq_ready"], 1)
                v.wait_ge(S["eq_ready"], g + 1)
                v.tensor_tensor(EQD[g % 2], q.rearrange("p (c x) -> p c x", c=G)[:, :, 0:P],
                                TRIB.unsqueeze(1).to_broadcast([P, G, P]), ALU.mult).then_inc(S["eqd_ready"], 1)

            def take_sums(g):
                v.wait_ge(S["grp_sum"], g + 1)
                b = banks[0:P, g % 2, 0:G * 32].rearrange("p (c x) -> p c x", c=G)
                gs = slice(G * g, G * g + G)
                v.tensor_copy(NGRP[:, gs], b[:, :, WP - 1])
                v.tensor_copy(SUMS[:, gs, :], b[:, :, 0:WP])
                if g:
                    v.wait_ge(S["idx_ready"], g)
                step(v.tensor_scalar(LATE, b[:, :, WP], 0.5, None, ALU.is_ge))
                v.sem_inc(S["sums_out"], 1)
                step(v.tensor_tensor(LATE, LATE, SPARE[:, gs], ALU.mult))
                step(v.tensor_tensor(LATE, LATE, KEY[:, gs], ALU.add))
                v.tensor_copy(WIDX[:, gs], LATE).then_inc(S["idx_ready"], 1)

            def take_condition():
                for j, (a, n) in enumerate(CHUNKS):
                    v.wait_ge(S["cond_mm"], j + 1)
                    v.tensor_scalar(CONDF[0:CD, a:a + n], bank(4 + j, CD, n), FB[:, 1:2], None, ALU.add).then_inc(S["cond_built"], 1)
                v.wait_ge(S["cond_built"], len(CHUNKS))
                step(v.tensor_copy(CONDP[:, 0, :], CONDF))
                step(v.tensor_tensor(CONDF, CONDF, CONDP[:, 0, :], ALU.subtract))
                step(v.tensor_copy(CONDP[:, 1, :], CONDF))
                step(v.tensor_tensor(CONDF, CONDF, CONDP[:, 1, :], ALU.subtract))
                v.tensor_copy(CONDP[:, 2, :], CONDF).then_inc(S["cond_parts"], 1)

            for g in range(NG):
                compare(g)
                if g:
                    take_sums(g - 1)
                if g == COND_GROUP:
                    take_condition()
                if g == NORM_GROUP:
                    norm(at("pre0"), X, "relu", source="x_in")
            take_sums(NG - 1)

            tmp = TMP.rearrange("p (c h) -> p c h", h=BH)
            attr = ATTR.rearrange("p (c h) -> p c h", h=BH)
            v.wait_ge(S["idx_ready"], NG)
            step(v.tensor_tensor(tmp, SUMS[:, :, 0:BH], SUMS[:, :, BH:2 * BH], ALU.add))
            step(v.tensor_tensor(tmp, tmp, SUMS[:, :, 2 * BH:3 * BH], ALU.add))
            v.tensor_scalar(tmp, tmp, float(2.0 ** -62), None, ALU.max).then_inc(S["lsum_ready"], 1)
            v.wait_ge(S["lse_log"], 1)
            step(v.scalar_tensor_tensor(tmp, tmp, BACK, attr, ALU.add, ALU.subtract))
            step(v.tensor_scalar(CNT, NGRP, 1.5, None, ALU.is_ge))
            step(v.tensor_tensor(tmp, tmp, CNT.unsqueeze(2).to_broadcast([P, EC, BH]), ALU.mult))
            v.tensor_tensor(attr, attr, tmp, ALU.add).then_inc(S["lse_ready"], 1)

            start_steps, start_gates = mine[0], gates[0]
            with v.Fori(0, LAYERS) as L:
                mine[1] = L
                t = at("n1", L)
                wait(v, S["xn_ready"], t("xn_ready"))
                for i in range(NT):
                    o = v.bn_stats(BN[:, i, :], X[:, i, :])
                step(o)
                norm(t, X, "cond")
                qkv(at("qkv", L), 128.0 ** -0.5)
                split(CWS[1], cwr("qkv", L))
                attention(at("att", L), 4, False)
                update(at("wo", L), X)
                norm(at("n2", L), X, "cond")
                up(at("up", L), COLB[:, 8:12])
                split(CWS[0], cwr("up", L))
                update(at("down", L), X, stats=False)
                wait(v, S["x_upd"], at("down", L)("x_upd"), NT)
                per_steps, per_gates = mine[0] - start_steps, gates[0] - start_gates
            assert per_steps == V_LOOP_STEPS, per_steps
            assert per_gates == GATES_PER_LAYER, per_gates
            mine[0], mine[1] = start_steps + LAYERS * per_steps, None
            gates[0] = start_gates + LAYERS * per_gates

            residual(at("res1"))
            norm(at("pre1"), X, "relu")
            t = at("dense")
            wait(v, S["dense_in"], t("dense_in"), 16)
            step(v.reduce_sum(DEG, DENSE, AX.X))
            v.tensor_scalar(FLAG, DEG, 0.5, None, ALU.is_ge)
            v.tensor_scalar(DEG1, DEG, 1.0, None, ALU.add)
            v.tensor_scalar(DINV, DEG, 1.0, None, ALU.max).then_inc(S["deg_clip"], 1)
            v.wait_ge(S["deg_sqrt"], 1)
            step(v.reciprocal(DINV, DINV))
            v.tensor_tensor(DINV, DINV, FLAG, ALU.mult).then_inc(S["dinv_ready"], 1)
            t = at("dense")
            v.wait_ge(S["dinv_in"], 16)
            step(v.tensor_scalar(DINVB, DINVB, -1.0, None, ALU.mult))
            for i in range(NT):
                v.scalar_tensor_tensor(DENSE[:, i, :], DENSE[:, i, :], DINV[:, i:i + 1], DINVB, ALU.mult, ALU.mult).then_inc(S["dense_ready"], 1)
            take_groups(at("prop1"), T2, KC)
            update(at("conv1"), V, add=False)
            norm(at("mid1"), V, "affine", dst=V, slope=0.01)
            wait(v, S["y_ready"], at("mid1")("y_ready"), NT)
            v.sem_inc(S["gb_used"], 1)
            take_groups(at("prop2"), T2, KC)
            update(at("conv2"), X)
            norm(at("pre2"), X, "relu")
            t = at("z1")
            for i in range(NT):
                wait(v, S["xn_ready"], t("xn_ready"), i + 1 - NT)
                o = v.bn_stats(BN[:, i, :], X[:, i, :])
            step(o)
            split(CWS[1], cwr("z1"))
            norm(t, X, "affine")
            qkv(at("qkv2"), 0.125)
            attention(at("att2"), BH, True)
            split(CWS[0], cwr("att2"))
            update(at("wo2"), X)
            norm(at("z2"), X, "affine")
            split(CWS[1], cwr("z2"))
            update(at("down2"), X, stats=False)
            wait(v, S["x_upd"], at("down2")("x_upd"), NT)
            residual(at("res2"))
            norm(at("pre3"), X, "relu")
            t = at("r3")
            for g in range(1, NT, 2):
                wait(v, S["grp_done"], t("grp_done"), g + 1)
                v.tensor_scalar(V[:, g, 0:256], bank(g % 4, P, 256), 0.0, None, ALU.max).then_inc(S["out_d"], 1)
            t = at("ct")
            for i in range(NT):
                wait(v, S["ct_done"], t("ct_done"), i + 1)
                blocks = halves(i % 2).rearrange("p h (k x) -> p h k x", k=2)
                d = DENSE[:, :, i * P:(i + 1) * P].rearrange("p (h k) x -> p h k x", k=2)
                step(v.tensor_copy(d, blocks))
                v.tensor_tensor(DENSE[:, i, i * P:(i + 1) * P], DENSE[:, i, i * P:(i + 1) * P], IDENT[0:P, 0:P], ALU.add).then_inc(S["dense_ready"], 1)
            take_groups(at("prop3"), T2, 2)
            t = at("conv3")
            wait(v, S["gb_in"], t("gb_in"), 16)
            for i in range(NT):
                wait(v, S["upd_done"], t("upd_done"), i + 1)
                step(v.tensor_tensor(X[:, i, :], X[:, i, :], bank(i % 4), ALU.add))
                v.sem_inc(S["x_upd"], 1)
                v.scalar_tensor_tensor(X[:, i, :], GB[:, 0, :], DEG1[:, i:i + 1], X[:, i, :], ALU.mult, ALU.add).then_inc(S["final_ready"], 1)

        @block.scalar
        def _(act):
            def norm(t, src, kind, dst=None, transposed=True):
                wait(act, S["stats_ready"], t("stats_ready"), 1)
                act.activation(STD, VARC, ACT.Sqrt).then_inc(S["std_ready"], 1)
                wait(act, S["rstd_ready"], t("rstd_ready"), 1)
                if kind == "relu":
                    for i in range(NT):
                        d = Y[:, i % 2, :] if dst is None else dst[:, i, :]
                        if dst is None and i >= 2:
                            wait(act, S["yT_ready"], t("yT_ready"), i - 1)
                        act.activation(d, src[:, i, :], ACT.Relu, bias=NMR[:, i:i + 1], scale=RSTD[:, i:i + 1]).then_inc(S["xn_ready"], 1)
                        if transposed and i:
                            take_T(t, i - 1)
                    if transposed:
                        take_T(t, NT - 1)
                    return
                for i in range(NT):
                    if i >= 2:
                        wait(act, S["y_ready"], t("y_ready"), i - 1)
                    act.activation(XN[:, i % 2, :], src[:, i, :], ACT.Identity, bias=NMR[:, i:i + 1], scale=RSTD[:, i:i + 1]).then_inc(S["xn_ready"], 1)
                    if i >= 2:
                        take_T(t, i - 2)
                take_T(t, NT - 2)
                take_T(t, NT - 1)

            def take_T(t, i):
                wait(act, S["yT_ready"], t("yT_ready"), i + 1)
                act.activation(T1[:, :, i * P:(i + 1) * P], banks[0:128, 4 + i % 2, 0:500].rearrange("p (c x) -> p c x", c=KC), ACT.Copy).then_inc(S["yT_out"], 1)

            def qkv(t, scale):
                wait(act, S["col_in"], t("col_in"), 16)
                wait(act, S["qbs_ready"], t("qbs_ready"), 1)
                g = 0
                for j, (a, n) in enumerate(CHUNKS):
                    for which, dst in ((0, T2), (1, T3)):
                        for m in range(KC):
                            if g % 2 == 0:
                                wait(act, S["grp_done"], t("grp_done"), g + 1)
                                if which == 0:
                                    o = act.activation(dst[:, m, a:a + n], bank(g % 4, 128, n), ACT.Identity, bias=QBS[:, m:m + 1], scale=scale)
                                else:
                                    o = act.activation(dst[:, m, a:a + n], bank(g % 4, 128, n), ACT.Identity, bias=COLB[:, 4 + m:5 + m])
                                o.then_inc(S["out_a"], 1)
                            g += 1
                for i in range(NT):
                    if g % 2 == 0:
                        wait(act, S["grp_done"], t("grp_done"), g + 1)
                        act.activation(V[:, i, :], bank(g % 4), ACT.Copy).then_inc(S["out_a"], 1)
                    g += 1

            def take_groups(t, dst, chunks, func=ACT.Copy, cols=None, every=False):
                g = 0
                for j, (a, n) in enumerate(CHUNKS):
                    for m in range(chunks):
                        if g % 2 == 0 or every:
                            wait(act, S["grp_done"], t("grp_done"), g + 1)
                            if cols is None:
                                o = act.activation(dst[:, m, a:a + n], bank(g % 4, 128, n), func)
                            else:
                                o = act.activation(dst[:, m, a:a + n], bank(g % 4, 128, n), func, bias=cols[:, m:m + 1])
                            o.then_inc(S["out_a"], 1)
                        g += 1

            def attention(t, heads):
                steps = heads * NT

                def log_counts(i):
                    wait(act, S["lc_pre"], t("lc_pre"), i + 1)
                    act.activation(LC[:, i % 2, :], LC[:, i % 2, :], ACT.Ln).then_inc(S["lc_log"], 1)

                def merge(k):
                    wait(act, S["mrg_diff"], t("mrg_diff"), k + 1)
                    act.activation(MRG[:, 3, :], MRG[:, 2, :], ACT.Exp).then_inc(S["mrg_exp"], 1)
                    wait(act, S["mrg_exp"], t("mrg_exp"), k + 1)
                    act.activation(MRG[:, 3, :], MRG[:, 3, :], ACT.Ln, bias=1.0).then_inc(S["mrg_log"], 1)

                if heads == 4:
                    for i in range(2):
                        log_counts(i)
                for n in range(steps + 3):
                    if 1 <= n <= steps:
                        m = n - 1
                        wait(act, S["t_done"], t("t_done"), m + 1)
                        if m >= 2:
                            wait(act, S["pv_done"], t("pv_done"), m - 1)
                        act.activation(pairs(PT[:, m % 2, :])[:, 2:5, :], halves(m % 2)[:, 2:5, :], ACT.Copy).then_inc(S["t_out_a"], 1)
                    if n < steps:
                        i, h = divmod(n, heads)
                        wait(act, S["negmax"], t("negmax"), n + 1)
                        act.activation(PR[:, n % 2, :], PR[:, n % 2, :], ACT.Exp, bias=NMX[:, n % 2:n % 2 + 1],
                                       accum_out=DEN[:, i % 2, h:h + 1]).then_inc(S["p_ready"], 1)
                        if heads == 4 and 1 <= i < NT - 1 and h == 1:
                            log_counts(i + 1)
                        if heads == 4 and n % 8 == 5:
                            merge(n // 8)
                    if n >= 3 and (n - 3) % heads == heads - 1:
                        i = (n - 3) // heads
                        wait(act, S["oT_done"], t("oT_done"), i + 1)
                        act.activation(T1[:, :, i * P:(i + 1) * P], banks[0:128, 6 + i % 2, 0:500].rearrange("p (c x) -> p c x", c=KC), ACT.Copy).then_inc(S["oT_out"], 1)

            act.wait_ge(S["phase_ready"], 1)
            act.activation(PHASE[:, 0, :], PHASE[:, 0, :], ACT.Sin).then_inc(S["emb_ready"], 1)
            act.wait_ge(S["shift_ready"], 1)
            act.wait_ge(S["edges_in"], 16 * 3)
            act.activation(EX, ATTR, ACT.Exp, bias=SHIFT).then_inc(S["exp_ready"], 1)
            for j, (a, n) in enumerate(CHUNKS):
                act.wait_ge(S["emb_mm"], j + 1)
                act.activation(PHASE[0:CD, 1, a:a + n], bank(4 + j, CD, n), ACT.Silu, bias=FB[:, 0:1]).then_inc(S["emb_act"], 1)
            norm(at("pre0"), X, "relu", dst=X, transposed=False)
            act.wait_ge(S["lsum_ready"], 1)
            act.activation(TMP, TMP, ACT.Ln).then_inc(S["lse_log"], 1)
            with act.Fori(0, LAYERS) as L:
                norm(at("n1", L), X, "cond")
                qkv(at("qkv", L), 128.0 ** -0.5)
                attention(at("att", L), 4)
                norm(at("n2", L), X, "cond")
                take_groups(at("up", L), T2, KC, ACT.Relu, COLB[:, 8:12])
            norm(at("pre1"), X, "relu", dst=V)
            act.wait_ge(S["deg_clip"], 1)
            act.activation(DINV, DINV, ACT.Sqrt).then_inc(S["deg_sqrt"], 1)
            take_groups(at("prop1"), T2, KC)
            norm(at("mid1"), V, "affine")
            take_groups(at("prop2"), T2, KC)
            act.wait_ge(S["x_saved"], 16 * NT)
            norm(at("pre2"), X, "relu", dst=X, transposed=False)
            norm(at("z1"), X, "affine")
            qkv(at("qkv2"), 0.125)
            attention(at("att2"), BH)
            norm(at("z2"), X, "affine")
            t = at("up2")
            wait(act, S["col_in"], t("col_in"), 16)
            take_groups(t, H8, 2 * KC, ACT.Silu, COLB[:, 0:8], every=True)
            norm(at("pre3"), X, "relu")
            t = at("r3")
            for g in range(0, NT, 2):
                wait(act, S["grp_done"], t("grp_done"), g + 1)
                act.activation(V[:, g, 0:256], bank(g % 4, P, 256), ACT.Relu).then_inc(S["out_a"], 1)
            take_groups(at("prop3"), T2, 2)

        @block.tensor
        def _(pe):
            def transposes(t, src, source):
                for i in range(NT):
                    wait(pe, S[source], t(source), i + 1)
                    if i >= 2:
                        wait(pe, S["yT_out"], t("yT_out"), i - 1)
                    row = Y[:, i % 2, :] if src is None else src[:, i, :]
                    for c in range(KC):
                        o = pe.transpose(banks[0:128, 4 + i % 2, c * P:(c + 1) * P], row[:, c * 128:(c + 1) * 128], IDENT[0:P, 0:P])
                    o.then_inc(S["yT_ready"], 1)

            def cond_norm(t, cw):
                wait(pe, S["rstd_ready"], t("rstd_ready"), 1)
                wait(pe, S["cws_ready"], t("cws_ready"))
                for i in range(NT + 1):
                    if i < NT:
                        if i >= 2:
                            wait(pe, S["y_ready"], t("y_ready"), i - 1)
                        b = 2 * (i % 2)
                        pe.matmul(bank(b), CONDS[:, i * P:(i + 1) * P], cw[:, 0:D], start=True, stop=True)
                        pe.matmul(bank(b + 1), CONDS[:, i * P:(i + 1) * P], cw[:, D:2 * D], start=True, stop=True).then_inc(S["cond_ready"], 1)
                    if i >= 1:
                        k = i - 1
                        wait(pe, S["y_ready"], t("y_ready"), k + 1)
                        if k >= 2:
                            wait(pe, S["yT_out"], t("yT_out"), k - 1)
                        for c in range(KC):
                            o = pe.transpose(banks[0:128, 4 + k % 2, c * P:(c + 1) * P], Y[:, k % 2, c * 128:(c + 1) * 128], IDENT[0:P, 0:P])
                        o.then_inc(S["yT_ready"], 1)

            def project(out, w, m, a, n, k=KC, width=D, src=T1):
                for c in range(k):
                    o = pe.matmul(out, w[:, c * width + m * 128:c * width + (m + 1) * 128], src[:, c, a:a + n], start=(c == 0), stop=(c == k - 1))
                return o

            def rows_of(out, i, parts, row, n=D):
                first = True
                for src, w, k in parts:
                    for c in range(k):
                        pe.matmul(out, src[:, c, i * P:(i + 1) * P], w[:, c * n:(c + 1) * n], start=first, stop=False)
                        first = False
                return pe.matmul(out, BSEL, row, start=False, stop=True)

            def T1_chunk(t, name, j):
                a, n = CHUNKS[j]
                wait(pe, S["yT_out"], t("yT_out"), (a + n) // P - NT)

            def qkv(t, row):
                g = 0
                for j, (a, n) in enumerate(CHUNKS):
                    T1_chunk(t, "yT_out", j)
                    for which in (0, 1):
                        wait(pe, S[f"w{which}_in"], t(f"w{which}_in"), 16)
                        for m in range(KC):
                            grp_free(pe, t, g)
                            project(bank(g % 4, 128, n), W[:, which, :], m, a, n).then_inc(S["grp_done"], 1)
                            g += 1
                wait(pe, S["w2_in"], t("w2_in"), 16)
                for i in range(NT):
                    grp_free(pe, t, g)
                    rows_of(bank(g % 4), i, [(T1, W[:, 2, :], KC)], row).then_inc(S["grp_done"], 1)
                    g += 1

            def attention(t, heads):
                dh, steps = D // heads, heads * NT
                per_chunk = 128 // dh

                def scores(n):
                    i, h = divmod(n, heads)
                    if n >= 2:
                        wait(pe, S["t_out_a"], t("t_out_a"), n - 1)
                        wait(pe, S["t_out_d"], t("t_out_d"), n - 1)
                    lo = dh * (h % per_chunk)
                    q, k = T2[lo:lo + dh, h // per_chunk, i * P:(i + 1) * P], T3[lo:lo + dh, h // per_chunk, :]
                    hv = halves(n % 2)
                    for a, w in ((0, 2), (2, 2), (4, 1)):
                        o = pe.matmul(hv[:, a:a + w, :], q, k[:, a * 250:(a + w) * 250], start=True, stop=True)
                    o.then_inc(S["s_done"], 1)

                def turn(n):
                    wait(pe, S["p_ready"], t("p_ready"), n + 1)
                    hv = halves(n % 2)
                    for j in range(NT):
                        o = pe.transpose(hv[:, j // 2, (j % 2) * P:(j % 2 + 1) * P], PR[:, n % 2, j * P:(j + 1) * P], IDENT[0:P, 0:P])
                    o.then_inc(S["t_done"], 1)

                def product(n):
                    i, h = divmod(n, heads)
                    wait(pe, S["t_out_a"], t("t_out_a"), n + 1)
                    wait(pe, S["t_out_d"], t("t_out_d"), n + 1)
                    if h == 0 and i >= 2:
                        wait(pe, S["oT_out"], t("oT_out"), i - 1)
                    for j in range(NT):
                        o = pe.matmul(bank(6 + i % 2)[:, h * dh:(h + 1) * dh], PT[:, n % 2, j * P:(j + 1) * P], V[:, j, h * dh:(h + 1) * dh],
                                      start=(j == 0), stop=(j == NT - 1))
                    o.then_inc(S["pv_done"], 1)

                def turn_rows(i):
                    wait(pe, S["o_ready"], t("o_ready"), i + 1)
                    for c in range(KC):
                        o = pe.transpose(banks[0:128, 6 + i % 2, c * P:(c + 1) * P], OS[:, c * 128:(c + 1) * 128], IDENT[0:P, 0:P])
                    o.then_inc(S["oT_done"], 1)

                wait(pe, S["out_a"], t("out_a"))
                wait(pe, S["out_d"], t("out_d"))
                scores(0)
                for n in range(steps + 2):
                    if n + 1 < steps:
                        scores(n + 1)
                    if n >= 2 and (n - 2) % heads == heads - 1:
                        turn_rows((n - 2) // heads)
                    if n < steps:
                        turn(n)
                    if 1 <= n <= steps:
                        product(n - 1)

            def update(t, parts, row):
                for i in range(NT):
                    if i >= 4:
                        wait(pe, S["x_upd"], t("x_upd"), i - 3)
                    rows_of(bank(i % 4), i, parts, row).then_inc(S["upd_done"], 1)

            def groups(t, w, chunks, k=KC, width=D, alternate=True):
                g = 0
                for j, (a, n) in enumerate(CHUNKS):
                    T1_chunk(t, "yT_out", j)
                    for m in range(chunks):
                        grp_free(pe, t, g, alternate)
                        project(bank(g % 4, 128, n), w, m, a, n, width=width).then_inc(S["grp_done"], 1)
                        g += 1

            def propagate(t, chunks):
                g = 0
                for j, (a, n) in enumerate(CHUNKS):
                    for m in range(chunks):
                        grp_free(pe, t, g)
                        for s_ in range(NT):
                            o = pe.matmul(bank(g % 4, 128, n), V[:, s_, m * 128:(m + 1) * 128], DENSE[:, s_, a:a + n], start=(s_ == 0), stop=(s_ == NT - 1))
                        o.then_inc(S["grp_done"], 1)
                        g += 1

            pe.wait_ge(S["emb_ready"], 1)
            for j, (a, n) in enumerate(CHUNKS):
                pe.matmul(bank(4 + j, CD, n), FW1, PHASE[:, 0, a:a + n], start=True, stop=True).then_inc(S["emb_mm"], 1)
            for g in range(NG):
                pe.wait_ge(S["eqd_ready"], g + 1)
                if g >= 2:
                    pe.wait_ge(S["sums_out"], g - 1)
                b = banks[0:P, g % 2, 0:G * 32].rearrange("p (c x) -> p c x", c=G)
                for c in range(G):
                    for c2 in range(G):
                        w = WP + 1 if c2 < c else WP
                        pe.matmul(b[:, c, 0:w], EQ[g % 2][:, c2 * G * P + c * P:c2 * G * P + (c + 1) * P], EPART[:, G * g + c2, 0:w], start=(c2 == 0), stop=(c == 0 and c2 == G - 1))
                    o = pe.matmul(b[:, c, WP:WP + 1], EQD[g % 2][:, c, :], EPART[:, 0, WP:WP + 1], start=(c == 0), stop=True)
                o.then_inc(S["grp_sum"], 1)
                if g == 0:
                    for j, (a, n) in enumerate(CHUNKS):
                        pe.wait_ge(S["emb_act"], j + 1)
                        pe.matmul(bank(4 + j, CD, n), FW2, PHASE[0:CD, 1, a:a + n], start=True, stop=True).then_inc(S["cond_mm"], 1)
            pe.wait_ge(S["sums_out"], NG)
            pe.wait_ge(S["conds_in"], 16 * (len(STACK) + 1))
            pe.wait_ge(S["consts_ready"], 2)

            with pe.Fori(0, LAYERS) as L:
                cond_norm(at("n1", L), CWS[0])
                qkv(at("qkv", L), CWS[0][:, 0:D])
                attention(at("att", L), 4)
                t = at("wo", L)
                wait(pe, S["w3_in"], t("w3_in"), 16)
                wait(pe, S["oT_out"], t("oT_out"))
                wait(pe, S["t_out_d"], t("t_out_d"))
                update(t, [(T1, W[:, 3, :], KC)], CWS[0][:, D:2 * D])
                cond_norm(at("n2", L), CWS[1])
                wait(pe, S["w0_in"], at("up", L)("w0_in"), 16)
                groups(at("up", L), W[:, 0, :], KC)
                t = at("down", L)
                wait(pe, S["w1_in"], t("w1_in"), 16)
                wait(pe, S["out_a"], t("out_a"))
                wait(pe, S["out_d"], t("out_d"))
                update(t, [(T2, W[:, 1, :], KC)], CWS[1][:, 0:D])

            transposes(at("pre1"), V, "xn_ready")
            t = at("prop1")
            wait(pe, S["dense_ready"], t("dense_ready"))
            wait(pe, S["x_upd"], t("x_upd"))
            propagate(t, KC)
            t = at("conv1")
            wait(pe, S["out_a"], t("out_a"))
            wait(pe, S["out_d"], t("out_d"))
            wait(pe, S["yT_out"], t("yT_out"))
            wait(pe, S["w0_in"], t("w0_in"), 16)
            wait(pe, S["w1_in"], t("w1_in"), 16)
            update(t, [(T1, W[:, 0, :], KC), (T2, W[:, 1, :], KC)], CWS[0][:, 0:D])
            transposes(at("mid1"), V, "y_ready")
            t = at("prop2")
            propagate(t, KC)
            t = at("conv2")
            wait(pe, S["out_a"], t("out_a"))
            wait(pe, S["out_d"], t("out_d"))
            wait(pe, S["yT_out"], t("yT_out"))
            wait(pe, S["w2_in"], t("w2_in"), 16)
            wait(pe, S["w3_in"], t("w3_in"), 16)
            update(t, [(T1, W[:, 2, :], KC), (T2, W[:, 3, :], KC)], CWS[0][:, D:2 * D])
            transposes(at("z1"), None, "y_ready")
            wait(pe, S["cws_ready"], at("qkv2")("cws_ready"))
            qkv(at("qkv2"), CWS[1][:, 0:D])
            attention(at("att2"), BH)
            t = at("wo2")
            wait(pe, S["w3_in"], t("w3_in"), 16)
            wait(pe, S["cws_ready"], t("cws_ready"))
            wait(pe, S["oT_out"], t("oT_out"))
            wait(pe, S["t_out_d"], t("t_out_d"))
            update(t, [(T1, W[:, 3, :], KC)], CWS[0][:, 0:D])
            transposes(at("z2"), None, "y_ready")
            t = at("up2")
            wait(pe, S["w0_in"], t("w0_in"), 16)
            groups(t, W[:, 0:2, :].rearrange("p a b -> p (a b)"), 2 * KC, width=2 * D, alternate=False)
            t = at("down2")
            wait(pe, S["w2_in"], t("w2_in"), 16)
            wait(pe, S["out_a"], t("out_a"))
            update(t, [(H8, W[:, 2:4, :].rearrange("p a b -> p (a b)"), 2 * KC)], CWS[0][:, D:2 * D])
            transposes(at("pre3"), None, "xn_ready")
            t = at("r3")
            wait(pe, S["w0_in"], t("w0_in"), 16)
            wait(pe, S["cws_ready"], t("cws_ready"))
            wait(pe, S["yT_out"], t("yT_out"))
            for g in range(NT):
                grp_free(pe, t, g)
                rows_of(bank(g % 4, P, 256), g, [(T1, W[:, 0, :], KC)], CWS[1][:, 0:256], n=256).then_inc(S["grp_done"], 1)
            t = at("ct")
            wait(pe, S["out_a"], t("out_a"))
            wait(pe, S["out_d"], t("out_d"))
            for i in range(NT):
                wait(pe, S[f"c_in{i % 2}"], t(f"c_in{i % 2}"), 16 * (i // 2 + 1))
                if i >= 2:
                    wait(pe, S["dense_ready"], t("dense_ready"), i - 1)
                hv = halves(i % 2)
                for j in range(NT):
                    o = pe.transpose(hv[:, j // 2, (j % 2) * P:(j % 2 + 1) * P], CR[:, i % 2, j * P:(j + 1) * P], IDENT[0:P, 0:P])
                o.then_inc(S["ct_done"], 1)
            t = at("prop3")
            wait(pe, S["dense_ready"], t("dense_ready"))
            propagate(t, 2)
            t = at("conv3")
            wait(pe, S["w1_in"], t("w1_in"), 16)
            wait(pe, S["out_a"], t("out_a"))
            wait(pe, S["out_d"], t("out_d"))
            for i in range(NT):
                if i >= 4:
                    wait(pe, S["x_upd"], t("x_upd"), i - 3)
                for c in range(2):
                    o = pe.matmul(bank(i % 4), T2[:, c, i * P:(i + 1) * P], W[:, 1, c * D:(c + 1) * D], start=(c == 0), stop=(c == 1))
                o.then_inc(S["upd_done"], 1)


def kernel(**inputs):
    import concourse.bacc as _bacc
    from concourse import mybir as _mybir
    from concourse.bass_utils import run_bass_kernel_spmd as _run

    nc = _bacc.Bacc("TRN2", target_bir_lowering=False, num_devices=1)
    f = {k: np.asarray(v) for k, v in inputs.items()}

    def parts(w):
        *lead, k, m = w.shape
        w = w.reshape(*lead, k // 128, 128, m)
        return np.moveaxis(w, -3, -2).reshape(*lead, 128, k // 128 * m)

    def cols(b):
        return np.moveaxis(b.reshape(*b.shape[:-1], -1, 128), -1, -2)

    src, dst = f["src"].reshape(P, EC), f["dst"].reshape(P, EC)
    L0, L1, L2, L3 = (lambda n, k=k: f[f"L{k}_gnn_{n}"] for k in range(4))

    def stacked(weights=None, *biases):
        a = np.zeros((SK, 2 * D), np.float32)
        if weights is not None:
            places = [p for p in range(SK) if not BIAS_ROW <= p < BIAS_ROW + 3]
            a[places] = np.tile(weights, (len(STACK), 1))
        row = np.concatenate(biases)
        a[BIAS_ROW:BIAS_ROW + 3, 0:len(row)] = row
        return a

    def cond_rows(layer, k):
        w = np.concatenate([L0(f"s{k}_w")[layer], L0(f"b{k}_w")[layer]], 1)
        b = np.concatenate([L0(f"s{k}_b")[layer], L0(f"b{k}_b")[layer]])[None]
        one = np.concatenate([np.ones((1, D), np.float32), np.zeros((1, D), np.float32)], 1)
        return np.concatenate([w, b, one])

    cw = np.stack([np.stack([stacked(cond_rows(l, 1), L0("bv")[l], L0("bo")[l]), stacked(cond_rows(l, 2), L0("m_b2")[l])])
                   for l in range(LAYERS)] + [np.stack([stacked(None, L1("b1"), L1("b2")), np.zeros((SK, 2 * D), np.float32)])])
    later = np.stack([stacked(None, L2("bv")), stacked(None, L2("bo"), L2("b2")), stacked(None, L3("b1"))])
    part_of = [0] * 54 + [1] * 36 + [2] * 6 + [0, 1, 2] + [2] * 12
    part_mask = np.eye(3, dtype=np.float32)[part_of]
    arr = {
        "x": f["x"],
        "src_pc": src, "dst_pc": dst,
        "src_cp": np.ascontiguousarray(src.T).reshape(P, EC), "dst_cp": np.ascontiguousarray(dst.T).reshape(P, EC),
        "edge_attr": f["edge_attr_8"].reshape(P, EC * BH),
        "noise": f["node_vec1"].reshape(1, N),
        "f_w1": L0("f_w1"), "f_w2": L0("f_w2"), "f_b": np.stack([L0("f_b1"), L0("f_b2")], 1),
        "w0": np.stack([parts(L0(n)) for n in ("wq", "wk", "wv", "wo", "m_w1", "m_w2")], 1),
        "colb": np.concatenate([cols(L0(n)) for n in ("bq", "bk", "m_b1")], 2),
        "cw": cw, "later_rows": later, "part_mask": part_mask,
        "w1": np.stack([parts(L1(n)) for n in ("W1_0", "W1_1", "W2_0", "W2_1")]),
        "l1_gamma": L1("gamma").reshape(1, D), "l1_beta": L1("beta").reshape(1, D),
        "w2": np.stack([parts(L2(n).T) for n in ("Wq", "Wk", "Wv", "Wo")]),
        "l2_colb": np.concatenate([cols(L2("bq")), cols(L2("bk"))], 1),
        "l2_lnb": np.stack([L2("ln_att_g"), L2("ln_att_b"), L2("ln_ff_g"), L2("ln_ff_b")]),
        "l2_b1": cols(L2("b1")), "l2_w1": parts(L2("W1").T), "l2_w2": parts(L2("W2").T),
        "l3_w1": parts(L3("W1")), "l3_w2": parts(L3("W2")),
        "l3_b2": L3("b2").reshape(1, D),
    }
    arr = {k: np.ascontiguousarray(a) for k, a in arr.items()}
    A = {k: nc.dram_tensor("in_" + k, a.shape, _mybir.dt.from_np(a.dtype), kind="ExternalInput").ap() for k, a in arr.items()}
    A["out"] = nc.dram_tensor("out", (N, D), _mybir.dt.float32, kind="ExternalOutput").ap()
    build(nc, A)
    r = _run(nc, [{"in_" + k: a for k, a in arr.items()}], core_ids=[0])
    return r.results[0]["out"]
```

```python
import numpy as np
import concourse.bass as bass
from concourse import mybir
from contextlib import ExitStack

F32 = mybir.dt.float32
BF16 = mybir.dt.bfloat16
F32R = mybir.dt.float32r
I32 = mybir.dt.int32
U32 = mybir.dt.uint32
ALU = mybir.AluOpType
ACT = mybir.ActivationFunctionType
AX = mybir.AxisListType

N, D, E = 1250, 512, 20000
P, NT = 125, 10
KC = D // 128
EC = E // P
G = 8
NG = EC // G
BH = 8
LAYERS = 4
CHUNKS = [(0, 500), (500, 500), (1000, 250)]
NO_EDGE = -1.0e30
EPS = 1e-5
CD = 16
WP = 3 * BH + 1
SK = 111
BIAS_ROW = 96
CR_ROWS = CD + 2
STACK = [(0, 0, 0), (1, 0, 18), (2, 0, 36), (0, 1, 54), (1, 1, 72), (0, 2, 90)]
HEADROOM = 40.0
COND_GROUP, NORM_GROUP = 3, 6
CLEAR_STEP, CLEAR_LATE = 5, 14
LEAD = 5
TURNS_LEFT = NT + 1 - LEAD
SPLIT_STEPS = [BH * (NT - 1) + k for k in (2, 4, 6)]
CLEARED = CLEAR_STEP * (NG - 2)
V_LOOP_STEPS = 41


class At:

    def __init__(self, base, per=0, layer=None):
        self.base, self.per, self.layer = base, per, layer

    def value(self, k):
        return self.base + k if self.layer is None else self.layer * self.per + (self.base + k)


def wait(eng, sem, at, k=0):
    if at.layer is not None:
        assert at.base + k > 0, "a loop's wait must be positive in its first turn"
    if at.base + k > 0:
        eng.wait_ge(sem, at.value(k))


def build(nc, A):
    ctx = ExitStack()
    with ctx:
        WORDS = 53200
        arena = ctx.enter_context(nc.sbuf_tensor("arena", [128, WORDS], F32))
        arena_start = nc.sbuf_base - 4 * WORDS
        top = [0]

        def region(words):
            a = top[0]
            top[0] += words
            assert top[0] <= WORDS, top[0]
            return a

        def view(at, rows, *shape):
            ap = arena[0:rows, at:at + int(np.prod(shape))]
            if len(shape) == 2:
                ap = ap.rearrange("p (a b) -> p a b", a=shape[0])
            if len(shape) == 3:
                ap = ap.rearrange("p (a b c) -> p a b c", a=shape[0], b=shape[1])
            return ap

        aX, aV = region(NT * D), region(NT * D)
        aT1, aT2, aT3 = region(KC * N), region(KC * N), region(KC * N)
        aP, aPT, aLC = region(2 * N), region(2 * N), region(2 * N)
        aW = region(4 * KC * D)
        aR = region(BH * N)
        aO = region(D)
        SMALL = 1600
        X = view(aX, P, NT, D)
        V = view(aV, P, NT, D)
        T1 = view(aT1, 128, KC, N)
        T2 = view(aT2, 128, KC, N)
        T3 = view(aT3, 128, KC, N)
        H8 = view(aT2, 128, 2 * KC, N)
        DENSE = view(aT3, P, NT, N)
        LC = view(aLC, P, 2, N)
        PR = view(aP, P, 2, N)
        PT = view(aPT, P, 2, NT * P)
        W = view(aW, 128, 4, KC * D)
        BIA = [view(aLC, P, N, BH), view(aR, P, N, BH)]
        CR = view(aW + 2 * KC * D, P, 3, N)
        OS = view(aO, P, D)
        r = aR + 904
        CWR = view(r, SK, 2 * D); r += 2 * D
        CWH, CWM = [view(r + k * D, SK, D).bitcast(BF16) for k in range(2)]; r += 2 * D
        CWS = [view(r + k * D, SK, D).bitcast(BF16) for k in range(2)]; r += 2 * D
        SPLIT_WORDS = r - aR
        CONDS = view(r, SK, N // 2).bitcast(BF16)
        DINVB = view(r, P, N); r += N
        XN = view(r, P, 2, D); r += 2 * D
        Y = view(r, P, 2, D); r += 2 * D
        ATTR = view(r, P, EC * BH)
        GB = view(r, P, 2, D); r += EC * BH
        NEG = view(r, P, 625); r += 625
        assert r <= aR + BH * N
        def part(name, at_, words):
            first = at_ // 8 * 8
            t = nc.alloc_sbuf_tensor_at(name, [128, at_ - first + words], F32R, offset=arena_start + 4 * first)
            return t[:, at_ - first:at_ - first + words]

        def by_chunk(ap):
            return ap.rearrange("p (c n) -> p c n", c=KC)

        T1P = [by_chunk(part("T1_high", aT1, KC * N)), by_chunk(part("T1_low", aW + 2 * KC * D, KC * N))]
        T2P = [[part(f"T2_{which}_{c}", a + c * N, N) for c in range(KC)] for which, a in (("high", aT2), ("low", aT3))]

        class Weight:

            def __init__(self, name, raw, high):
                self.raw = view(raw, 128, KC * D)
                self.high, self.low = part(name + "_high", high, KC * D), part(name + "_low", raw, KC * D)

        WQ, WK, WV = [Weight(n, a, a + KC * D) for n, a in (("WQ", aV), ("WK", aW), ("WV", aP))]
        WO, WU, WD = WK, WQ, WV
        WU2 = [Weight(f"WU{k}", aP + k * KC * D, aV + k * KC * D) for k in range(2)]
        s = [region(SMALL)]

        def small(rows, *shape):
            v = view(s[0], rows, *shape)
            s[0] += int(np.prod(shape))
            assert s[0] <= aO + D + SMALL, s[0]
            return v

        IDENT, ONES = small(128, 128), small(128, 128)
        COLB, QBS = small(128, 12), small(128, 4)
        BN, MV = small(P, NT, 6), small(P, NT, 2)
        VARC = small(P, NT)
        STD, RSTD, NMR = small(P, NT), small(P, NT), small(P, NT)
        DEG, FLAG, DINV, DEG1 = small(P, NT), small(P, NT), small(P, NT), small(P, NT)
        PARTM = small(SK, 3)
        BSEL = small(SK, 64).bitcast(BF16)[:, 0:P]
        MX, NMX = small(P, 2, BH), small(P, 2)
        DEN, RD = small(P, 2, BH), small(P, 2, BH)
        GMX, GALL, SHIFT, BACK = small(P, 1), small(P, 1), small(P, 1), small(P, 1)
        FRQ = small(64, 5)
        FW1, FW2, FB = small(64, CD), small(CD, CD), small(CD, 2)
        LATE, IDLE = small(P, G), small(P, 1)
        KEYI, WIDX = small(P, EC).bitcast(I32), small(P, EC).bitcast(I32)
        MRG = small(P, 5, G * BH)
        NGRP, CNT = small(P, EC), small(P, EC)

        e = aV
        KEY, SPARE, KEYC = view(e, P, EC), view(e + EC, P, EC), view(e + 2 * EC, P, EC); e += 3 * EC
        SRC, DST, SRCG, DSTG = [view(e + k * EC, P, EC) for k in range(4)]; e += 4 * EC
        SRCI, DSTI, SRCJ, DSTJ = [view(e + k * EC, P, EC).bitcast(I32) for k in range(4)]; e += 4 * EC
        EX = view(e, P, EC * BH); e += EC * BH
        TRI = view(e, P, P); e += P
        TRIB = view(e, P, 64).bitcast(BF16)[:, 0:P]; e += 64
        assert e <= aV + NT * D
        e = aT1
        KEYB = view(e, P, 2, G * P); e += 2 * G * P
        EPART = view(e, P, EC * (WP + 1) // 2).bitcast(BF16).rearrange("p (c w) -> p c w", w=WP + 1); e += EC * (WP + 1) // 2
        EQW = G * (G * P + P)
        EQ = [view(e + k * EQW // 2, P, EQW // 2).bitcast(BF16) for k in range(2)]; e += EQW
        assert e <= aP
        e = aPT
        SUMS = view(e, P, EC, WP); e += EC * WP
        assert e <= aW
        EQD = [view(aP + k * G * P // 2, P, G * P // 2).bitcast(BF16).rearrange("p (c x) -> p c x", c=G) for k in range(2)]
        TMP = view(aP + G * P, P, EC * BH)
        ZERO = view(aW, P, N)
        PHASE = view(aW + N, 64, 2, N)
        CONDF = view(aW + 3 * N, CR_ROWS, N)
        CONDP = view(aW + 4 * N, CR_ROWS, 3 * N // 2).bitcast(BF16).rearrange("p (k n) -> p k n", k=3)

        banks = ctx.enter_context(nc.psum_tensor("banks", [128, 8, 512], F32))

        def bank(b, rows=P, n=512):
            return banks[0:rows, b, 0:n]

        def halves(k):
            return banks[0:P, 3 * k:3 * k + 3, :].rearrange("p b x -> p (b x)").rearrange("p (h x) -> p h x", x=256)[:, 0:5, 0:250]

        def count_columns(i):
            return (DENSE[:, :, i * P:(i + 1) * P].rearrange("p (h k) x -> p h k x", k=2),
                    halves(i % 2).rearrange("p h (k x) -> p h k x", k=2))

        def pairs(ap):
            return ap.rearrange("p (h x) -> p h x", x=250)

        cnt_tab = nc.dram_tensor("cnt_tab", [N * N + E, 1], F32)
        bia_tab = nc.dram_tensor("bia_tab", [N * N, BH], F32)
        key_dram = nc.dram_tensor("key_dram", [E], F32)
        dinv_dram = nc.dram_tensor("dinv_dram", [NT, P], F32)
        x_dram = nc.dram_tensor("x_dram", [N, D], F32)
        cnt_rows = cnt_tab[0:N * N, :].rearrange("(t p d) o -> t p (d o)", t=NT, p=P)
        bia_rows = bia_tab[:, :].rearrange("(t p d) h -> t p (d h)", t=NT, p=P)
        x_rows = A["x"].rearrange("(t p) d -> t p d", p=P)
        xs_rows = x_dram[:, :].rearrange("(t p) d -> t p d", p=P)
        out_rows = A["out"].rearrange("(t p) d -> t p d", p=P)

        def clear_biases(eng, a, n, done):
            rows = bia_tab[:, :].rearrange("(p a) h -> p (a h)", p=P).rearrange("p (b c) -> p b c", c=625)
            eng.dma_start(rows[:, a:a + n, :], NEG.unsqueeze(1).to_broadcast([P, n, 625])).then_inc(S[done], 16)

        names = """ends_in edges_in noise_in zero_ready cnt_zeroed neg_ready bia_cleared bia_cleared_late keyc_ready keyc_out keyb_in0 keyb_in1
            consts_ready gmax_ready gmax_all shift_ready exp_ready eq_ready eqd_ready grp_sum sums_out idx_ready
            counted lsum_ready lse_log lse_ready gathered mrg_diff mrg_exp mrg_log mrg_ready scattered
            lc_pre lc_log lc_ready phase_ready emb_ready emb_mm emb_act cond_mm cond_built cond_parts conds_clear
            conds_in cwr_in cws_ready
            x_in res_in0 res_in1 stats_ready std_ready rstd_ready xn_ready cond_ready y_ready yT_ready yT_out
            w0_in w1_in w2_in w3_in col_in gb_in gb_used qbs_ready grp_done out_a out_d upd_done x_upd
            lct_in0 lct_in1 bia_first bia_in0 bia_in1 s_done max_ready negmax p_ready t_done t_out_a t_out_d pv_done o_ready oT_done oT_out
            deg_clip deg_sqrt dinv_ready dinv_out dinv_in dense_in0 dense_in1 dense_ready x_saved w4_in w5_in yT_hi oT_hi hi_ready w_ready c_in0 c_in1 c_in2 ct_done ct_out
            final_ready final_out v_step gate sp_passed""".split()
        S = {n: ctx.enter_context(nc.semaphore(n)) for n in names}
        block = ctx.enter_context(nc.Block())

        timeline = []

        def stage(name, **adds):
            timeline.append((name, adds))

        def norm_stage(name, kind, transposed=True, in_parts=False, **more):
            adds = dict(stats_ready=1, std_ready=1, rstd_ready=1, xn_ready=NT, **more)
            if kind != "relu":
                adds.update(y_ready=NT)
            if kind == "cond":
                adds.update(cond_ready=NT)
            if transposed:
                adds.update(yT_ready=NT, yT_out=NT, yT_hi=NT * in_parts)
            stage(name, **adds)

        def att_stage(name, heads, **more):
            n = heads * NT
            stage(name, s_done=n, max_ready=n, negmax=n, p_ready=n, t_done=n, t_out_a=n, t_out_d=n, pv_done=n,
                  o_ready=NT, oT_done=NT, oT_out=NT, **more)

        stage("start", x_in=16 * NT, cws_ready=1, w0_in=16, w1_in=16, hi_ready=2, w_ready=2)
        norm_stage("pre0", "relu", transposed=False)
        stage("loop")
        norm_stage("n1", "cond", in_parts=True)
        stage("qkv", w2_in=16, hi_ready=1, w_ready=1, col_in=16, cws_ready=1, qbs_ready=1, grp_done=34, out_a=17, out_d=17)
        att_stage("att", 4, w3_in=16, hi_ready=1, w_ready=1, oT_hi=NT, lct_in0=8 * NT, lct_in1=8 * NT, lc_pre=NT, lc_log=NT, lc_ready=NT, gathered=16 * EC // LAYERS,
                  mrg_diff=NG // LAYERS, mrg_exp=NG // LAYERS, mrg_log=NG // LAYERS, mrg_ready=NG // LAYERS)
        stage("wo", w4_in=16, w5_in=16, hi_ready=2, w_ready=2, upd_done=NT, x_upd=NT)
        norm_stage("n2", "cond", in_parts=True)
        stage("up", w1_in=16, hi_ready=1, w_ready=1, cws_ready=1, grp_done=12, out_a=12, out_d=12)
        stage("down", w0_in=16, hi_ready=1, w_ready=1, upd_done=NT, x_upd=NT)
        stage("end")
        stage("res1", res_in0=16, res_in1=16, x_upd=NT)
        norm_stage("pre1", "relu")
        stage("dense", dense_in0=16, dense_in1=16, dense_ready=NT)
        stage("prop1", grp_done=12, out_a=6, out_d=6)
        stage("conv1", w0_in=16, w1_in=16, upd_done=NT, x_upd=NT)
        norm_stage("mid1", "affine", gb_in=32)
        stage("prop2", grp_done=12, out_a=6, out_d=6)
        stage("conv2", w0_in=16, w1_in=16, w2_in=16, w4_in=16, w3_in=16, hi_ready=3, w_ready=3, upd_done=NT, x_upd=NT)
        norm_stage("pre2", "relu", transposed=False)
        norm_stage("z1", "affine", in_parts=True, gb_in=32, cws_ready=1)
        stage("qkv2", col_in=16, qbs_ready=1, grp_done=34, out_a=17, out_d=17)
        att_stage("att2", BH, cws_ready=1, bia_in0=8 * NT, bia_in1=8 * NT)
        stage("wo2", w3_in=16, w0_in=16, hi_ready=2, w_ready=2, upd_done=NT, x_upd=NT)
        norm_stage("z2", "affine", in_parts=True, gb_in=32, cws_ready=1)
        stage("up2", col_in=16, grp_done=24, out_a=24)
        stage("down2", w2_in=16, res_in0=16, res_in1=16, upd_done=NT, x_upd=NT)
        stage("ct", c_in0=64, c_in1=48, c_in2=48, ct_done=NT, ct_out=NT, dense_ready=NT)
        norm_stage("pre3", "relu")
        stage("r3", w0_in=16, grp_done=NT, out_d=NT)
        stage("prop3", grp_done=6, out_a=3, out_d=3)
        stage("conv3", w1_in=16, gb_in=16, upd_done=NT)
        order = [n for n, _ in timeline]
        per = {n: sum(a.get(n, 0) for _, a in timeline[order.index("loop"):order.index("end")]) for n in names}

        def at(name, layer=None):
            k = order.index(name)
            inside = order.index("loop") < k < order.index("end")
            assert inside == (layer is not None), name

            def get(sem):
                base = sum(a.get(sem, 0) for _, a in timeline[:k])
                if inside:
                    return At(base, per[sem], layer)
                return At(base + (LAYERS - 1) * per[sem] * (k >= order.index("end")))
            return get

        def cond_bank(i):
            return 2 if i % 2 and i < LEAD else 6

        def grp_free(eng, t, g, alternate=True):
            if g < 4:
                return
            if not alternate:
                wait(eng, S["out_a"], t("out_a"), g - 3)
            elif g % 2 == 0:
                wait(eng, S["out_a"], t("out_a"), (g - 4) // 2 + 1)
            else:
                wait(eng, S["out_d"], t("out_d"), (g - 4) // 2 + 1)

        @block.sync
        def _(sp):
            def load(dst, src, name):
                sp.dma_start(dst, src).then_inc(S[name], 16)

            def zero_counts():
                sp.wait_ge(S["zero_ready"], 1)
                for i in range(NT):
                    load(cnt_rows[i], ZERO, "cnt_zeroed")
                load(cnt_tab[N * N:N * N + E, :].rearrange("(p b) o -> p (b o)", p=P), ZERO[:, 0:EC], "cnt_zeroed")

            def spread_condition():
                sp.wait_ge(S["cond_parts"], 1)
                sp.wait_ge(S["conds_clear"], 1)
                for part, _, row in STACK:
                    if row < BIAS_ROW < row + CR_ROWS:
                        k = BIAS_ROW - row
                        load(CONDS[row:BIAS_ROW, :], CONDP[0:k, part, :], "conds_in")
                        load(CONDS[BIAS_ROW + 3:SK, :], CONDP[k:CR_ROWS, part, :], "conds_in")
                    else:
                        load(CONDS[row:row + CR_ROWS, :], CONDP[:, part, :], "conds_in")

            def loop_wait(name, at_, k=0):
                wait(sp, S[name], at_, k)
                sp.sem_inc(S["sp_passed"], 1)

            for dst, key in ((SRCJ, "src_cp"), (DSTJ, "dst_cp")):
                load(dst, A[key], "ends_in")
            load(PHASE[:, 0, :], A["noise"].to_broadcast([64, N]), "noise_in")
            load(PARTM, A["part_mask"], "noise_in")
            load(CWR, A["cw"][0, 0], "cwr_in")
            load(FW1, A["f_w1"], "noise_in")
            load(FW2, A["f_w2"], "noise_in")
            load(FB, A["f_b"], "noise_in")
            for dst, key in ((SRCI, "src_pc"), (DSTI, "dst_pc"), (ATTR, "edge_attr")):
                load(dst, A[key], "edges_in")
            sp.wait_ge(S["keyc_ready"], 1)
            load(key_dram[:].rearrange("(p c) -> p c", p=P), KEYC, "keyc_out")
            sp.wait_ge(S["keyc_out"], 16)
            kd = key_dram[:].rearrange("(g n) -> g n", g=NG)
            for g in range(NG):
                if g == COND_GROUP + 2:
                    spread_condition()
                if g >= 2:
                    sp.wait_ge(S["eq_ready"], g - 1)
                load(KEYB[:, g % 2, :], kd[g:g + 1, :].to_broadcast([P, G * P]), f"keyb_in{g % 2}")
                if g == 1:
                    zero_counts()
                    for i in range(NT):
                        load(X[:, i, :], x_rows[i], "x_in")
                    sp.wait_ge(S["neg_ready"], 1)
                if g >= 2:
                    clear_biases(sp, CLEAR_STEP * (g - 2), CLEAR_STEP, "bia_cleared")
            sp.wait_ge(S["cnt_zeroed"], 16 * (NT + 1))
            sp.wait_ge(S["conds_in"], 16 * (len(STACK) + 1))
            load(WK.raw, A["w0"][0, 1], "w1_in")
            sp.wait_ge(S["idx_ready"], NG)
            load(WQ.raw, A["w0"][0, 0], "w0_in")
            sp.wait_ge(S["lse_ready"], 1)

            with sp.Fori(0, LAYERS) as L:
                w0 = A["w0"][bass.ds(L, 1), :, :, :].rearrange("o m p x -> (o m) p x")
                w0_next = A["w0"][bass.ds(L + 1, 1), :, :, :].rearrange("o m p x -> (o m) p x")
                load(WV.raw, w0[2], "w2_in")
                load(COLB, A["colb"][bass.ds(L, 1), :, :].rearrange("o p x -> (o p) x"), "col_in")
                loop_wait("cws_ready", at("n1", L)("cws_ready"))
                load(CWR, A["cw"][bass.ds(L, 1), 1, :, :].rearrange("o p x -> (o p) x"), "cwr_in")
                t = at("att", L)
                sp.wait_ge(S["counted"], 16 * EC)
                for i in range(NT):
                    if i >= 2:
                        loop_wait("max_ready", t("max_ready"), 4 * (i - 1))
                    load(LC[:, i % 2, :], cnt_rows[i], f"lct_in{i % 2}")
                    if i == 1:
                        loop_wait("grp_done", t("grp_done"))
                        load(WO.raw, w0[3], "w3_in")
                        loop_wait("cws_ready", t("cws_ready"))
                        load(CWR, A["cw"][bass.ds(L + 1, 1), 0, :, :].rearrange("o p x -> (o p) x"), "cwr_in")
                t = at("wo", L)
                loop_wait("pv_done", t("pv_done"))
                load(WU.raw, w0[4], "w4_in")
                load(WD.raw, w0[5], "w5_in")
                loop_wait("upd_done", t("upd_done"), NT)
                load(WK.raw, w0_next[1], "w1_in")
                loop_wait("grp_done", at("down", L)("grp_done"))
                load(WQ.raw, w0_next[0], "w0_in")
                loop_wait("x_upd", at("down", L)("x_upd"), NT)

            for k in range(2):
                load(V[:, 5 * k:5 * k + 5, :], A["x"].rearrange("(t p) d -> p t d", p=P)[:, 5 * k:5 * k + 5, :], f"res_in{k}")
            sp.wait_ge(S["dinv_ready"], 1)
            with nc.allow_non_contiguous_dma(reason="ten words of each partition, 5 KB in all"):
                load(dinv_dram[:, :].rearrange("t p -> p t"), DINV, "dinv_out")
            for k in range(2):
                load(DENSE[:, 5 * k:5 * k + 5, :], cnt_rows[5 * k:5 * k + 5].rearrange("t p d -> p t d"), f"dense_in{k}")
            sp.wait_ge(S["dinv_out"], 16)
            load(DINVB, dinv_dram[:, :].rearrange("(o t) p -> o (t p)", o=1).to_broadcast([P, N]), "dinv_in")
            load(W[:, 0, :], A["w1"][0], "w0_in")
            load(W[:, 1, :], A["w1"][1], "w1_in")
            load(GB[:, 0, :], A["l1_gamma"].to_broadcast([P, D]), "gb_in")
            load(GB[:, 1, :], A["l1_beta"].to_broadcast([P, D]), "gb_in")
            load(W[:, 2, :], A["w1"][2], "w2_in")
            load(W[:, 3, :], A["w1"][3], "w3_in")
            wait(sp, S["grp_done"], at("conv2")("grp_done"))
            load(WK.raw, A["w2"][1], "w1_in")
            load(WQ.raw, A["w2"][0], "w0_in")
            load(WV.raw, A["w2"][2], "w4_in")
            t = at("conv2")
            for i in range(NT):
                wait(sp, S["x_upd"], t("x_upd"), i + 1)
                load(xs_rows[i], X[:, i, :], "x_saved")
            wait(sp, S["gb_used"], At(0), 1)
            load(CWR, A["later_rows"][0], "cwr_in")
            for k in range(2):
                load(GB[:, k, :], A["l2_lnb"][k:k + 1, :].to_broadcast([P, D]), "gb_in")
            load(COLB[:, 0:8], A["l2_colb"], "col_in")
            sp.wait_ge(S["scattered"], 16 * EC)
            wait(sp, S["yT_out"], at("qkv2")("yT_out"))
            load(BIA[1].rearrange("p d h -> p (d h)")[:, SPLIT_WORDS:], bia_rows[0][:, SPLIT_WORDS:], "bia_first")
            t = at("att2")
            wait(sp, S["grp_done"], t("grp_done"))
            wait(sp, S["yT_out"], t("yT_out"))
            wait(sp, S["out_a"], t("out_a"))
            wait(sp, S["out_d"], t("out_d"))
            for i in range(NT):
                if i >= 2:
                    wait(sp, S["max_ready"], t("max_ready"), BH * (i - 1))
                words = slice(0, SPLIT_WORDS if i == 0 else N * BH)
                load(BIA[(i + 1) % 2].rearrange("p d h -> p (d h)")[:, words], bia_rows[i][:, words], f"bia_in{i % 2}")
            wait(sp, S["max_ready"], t("max_ready"), BH * (NT - 1))
            load(CWR, A["later_rows"][1], "cwr_in")
            wait(sp, S["max_ready"], t("max_ready"), BH * NT)
            load(W[:, 3, :], A["w2"][3], "w3_in")
            for k in range(2):
                load(GB[:, k, :], A["l2_lnb"][2 + k:3 + k, :].to_broadcast([P, D]), "gb_in")
            load(COLB[:, 0:8], A["l2_b1"], "col_in")
            wait(sp, S["pv_done"], t("pv_done"), BH * NT)
            load(view(aP, 128, 2 * KC * D), A["l2_w1"], "w0_in")
            load(W[:, 0:2, :].rearrange("p a b -> p (a b)"), A["l2_w2"], "w2_in")
            wait(sp, S["cws_ready"], at("wo2")("cws_ready"))
            load(CWR, A["later_rows"][2], "cwr_in")
            wait(sp, S["grp_done"], at("down2")("grp_done"))
            sp.wait_ge(S["x_saved"], 16 * NT)
            for k in range(2):
                load(V[:, 5 * k:5 * k + 5, :], x_dram[:, :].rearrange("(t p) d -> p t d", p=P)[:, 5 * k:5 * k + 5, :], f"res_in{k}")
            t = at("ct")
            for i in range(3):
                load(CR[:, i, :], cnt_rows[i], f"c_in{i}")
            wait(sp, S["x_upd"], t("x_upd"))
            load(W[:, 0, 0:1024], A["l3_w1"], "w0_in")
            load(W[:, 1, 0:1024], A["l3_w2"], "w1_in")
            load(GB[:, 0, :], A["l3_b2"].to_broadcast([P, D]), "gb_in")
            for i in range(3, NT):
                wait(sp, S["ct_done"], t("ct_done"), i - 2)
                load(CR[:, i % 3, :], cnt_rows[i], f"c_in{i % 3}")
            for i in range(NT):
                sp.wait_ge(S["final_ready"], i + 1)
                load(out_rows[i], X[:, i, :], "final_out")
            sp.wait_ge(S["final_out"], 16 * NT)

        @block.gpsimd
        def _(gp):
            gp.memset(ONES, 1.0).then_inc(S["consts_ready"], 1)
            gp.memset(NEG, NO_EDGE).then_inc(S["neg_ready"], 1)
            gp.wait_ge(S["consts_ready"], 1)
            gp.wait_ge(S["neg_ready"], 1)
            gp.affine_select(out=IDENT, in_=ONES, compare_op=ALU.is_equal, fill=0.0, base=0,
                             pattern=[[1, 128]], channel_multiplier=-1).then_inc(S["consts_ready"], 1)
            gp.affine_select(out=TRI, in_=ONES[0:P, 0:P], compare_op=ALU.is_gt, fill=0.0, base=0,
                             pattern=[[1, P]], channel_multiplier=-1).then_inc(S["consts_ready"], 1)
            for k in range(2):
                gp.wait_ge(S["consts_ready"], 3 + k)
                gp.iota(FRQ[32 * k:32 * k + 32, 0:1].bitcast(I32), pattern=[[0, 1]], base=1,
                        channel_multiplier=1).then_inc(S["consts_ready"], 1)
            gp.wait_ge(S["consts_ready"], 5)
            gp.iota(SRCG.bitcast(I32), pattern=[[1, EC]], base=N * N, channel_multiplier=EC).then_inc(S["consts_ready"], 1)
            gp.wait_ge(S["gmax_ready"], 1)
            gp.wait_ge(S["consts_ready"], 6)
            gp.partition_all_reduce(GALL, GMX, P, bass.bass_isa.ReduceOp.max).then_inc(S["gmax_all"], 1)
            gp.wait_ge(S["cnt_zeroed"], 16 * (NT + 1))
            for g in range(NG):
                gp.wait_ge(S["idx_ready"], g + 1)
                gp.wait_ge(S["sums_out"], g + 1)
                if g:
                    gp.wait_ge(S["counted"], 16 * G * g)
                for k in range(G * g, G * g + G):
                    gp.indirect_dma_start(out=cnt_tab[:, :], out_offset=bass.IndirectOffsetOnAxis(ap=WIDX[:, k:k + 1].bitcast(U32), axis=0),
                                          in_=NGRP[:, k:k + 1], in_offset=None, bounds_check=N * N + E - 1, oob_is_err=True,
                                          compute_op=ALU.add).then_inc(S["counted"], 16)
            for a in range(CLEARED, 160, CLEAR_LATE):
                clear_biases(gp, a, CLEAR_LATE, "bia_cleared_late")
            gp.wait_ge(S["bia_cleared"], 16 * (NG - 2))
            gp.wait_ge(S["bia_cleared_late"], 16 * ((160 - CLEARED) // CLEAR_LATE))
            gp.wait_ge(S["lse_ready"], 1)
            for g in range(NG):
                if g:
                    gp.wait_ge(S["scattered"], 16 * G * g)
                for k in range(G * g, G * g + G):
                    c = k % G
                    gp.indirect_dma_start(out=MRG[:, 0, c * BH:(c + 1) * BH], out_offset=None, in_=bia_tab[:, :],
                                          in_offset=bass.IndirectOffsetOnAxis(ap=KEYI[:, k:k + 1].bitcast(U32), axis=0)).then_inc(S["gathered"], 16)
                gp.wait_ge(S["mrg_ready"], g + 1)
                for k in range(G * g, G * g + G):
                    c = k % G
                    gp.indirect_dma_start(out=bia_tab[:, :], out_offset=bass.IndirectOffsetOnAxis(ap=WIDX[:, k:k + 1].bitcast(U32), axis=0),
                                          in_=MRG[:, 4, c * BH:(c + 1) * BH], in_offset=None, bounds_check=N * N - 1,
                                          oob_is_err=False).then_inc(S["scattered"], 16)
            gp.wait_ge(S["scattered"], 16 * EC)

        @block.vector
        def _(v):
            mine = [0, None]

            def step(ins):
                mine[0] += 1
                ins.then_inc(S["v_step"], 1)
                v.wait_ge(S["v_step"], mine[0] if mine[1] is None else mine[1] * V_LOOP_STEPS + mine[0])

            def low_T(t, i, name="yT"):
                wait(v, S[name + "_hi"], t(name + "_hi"), i + 1)
                cols = slice(i * P, (i + 1) * P)
                b = banks[0:128, (4 if name == "yT" else 6) + i % 2, 0:500].rearrange("p (c x) -> p c x", c=KC)
                v.tensor_tensor(T1P[1][:, :, cols], b, T1P[0][:, :, cols].bitcast(F32), ALU.subtract).then_inc(S[name + "_out"], 1)

            def low_part(w, t, k):
                wait(v, S["hi_ready"], t("hi_ready"), k + 1)
                v.tensor_tensor(w.low, w.raw, w.high.bitcast(F32), ALU.subtract).then_inc(S["w_ready"], 1)

            def norm(t, src, kind, dst=None, slope=None, source=None, in_parts=False):
                if source is not None:
                    v.wait_ge(S["x_in"], 16 * NT)
                    for i in range(NT):
                        o = v.bn_stats(BN[:, i, :], src[:, i, :])
                    step(o)
                v.memset(IDLE, 0.0)
                for i in range(NT):
                    o = v.bn_aggr(MV[:, i, :], BN[:, i, :])
                step(o)
                v.tensor_scalar(VARC, MV[:, :, 1], EPS, None, ALU.add).then_inc(S["stats_ready"], 1)
                wait(v, S["std_ready"], t("std_ready"), 1)
                step(v.reciprocal(RSTD, STD))
                v.scalar_tensor_tensor(NMR, MV[:, :, 0], -1.0, RSTD, ALU.mult, ALU.mult).then_inc(S["rstd_ready"], 1)
                if kind == "relu":
                    return
                if kind == "affine":
                    wait(v, S["gb_in"], t("gb_in"), 32)

                def row(i):
                    y = Y[:, i % 2, :] if dst is None else dst[:, i, :]
                    wait(v, S["xn_ready"], t("xn_ready"), i + 1)
                    if i >= 2 and dst is None:
                        wait(v, S["yT_ready"], t("yT_ready"), i - 1)
                    if kind == "cond":
                        wait(v, S["cond_ready"], t("cond_ready"), i + 1)
                        b = cond_bank(i)
                        v.tensor_tensor(y, XN[:, i % 2, :], bank(b), ALU.mult).then_inc(S["gate"], 1)
                        wait_gate()
                        v.tensor_tensor(y, y, bank(b + 1), ALU.add).then_inc(S["y_ready"], 1)
                    else:
                        v.tensor_tensor(y, XN[:, i % 2, :], GB[:, 0, :], ALU.mult).then_inc(S["gate"], 1)
                        wait_gate()
                        if slope is None:
                            v.tensor_tensor(y, y, GB[:, 1, :], ALU.add).then_inc(S["y_ready"], 1)
                        else:
                            v.tensor_tensor(y, y, GB[:, 1, :], ALU.add).then_inc(S["gate"], 1)
                            wait_gate()
                            v.scalar_tensor_tensor(y, y, slope, y, ALU.mult, ALU.max).then_inc(S["y_ready"], 1)

                def turn(d):
                    if in_parts and d >= 2:
                        low_T(t, d - 2)
                    if d < NT:
                        row(d)

                for d in range(LEAD if in_parts else NT):
                    turn(d)
                return turn

            gates = [0]
            GATES_PER_LAYER = 2 * NT

            def wait_gate():
                gates[0] += 1
                v.wait_ge(S["gate"], gates[0] if mine[1] is None else mine[1] * GATES_PER_LAYER + gates[0])

            def update(t, dst, add=True, split_after={}, residual=False):
                for i in range(NT):
                    if residual:
                        wait(v, S[f"res_in{i // 5}"], t(f"res_in{i // 5}"), 16)
                        step(v.tensor_tensor(dst[:, i, :], dst[:, i, :], V[:, i, :], ALU.add))
                    wait(v, S["upd_done"], t("upd_done"), i + 1)
                    if add:
                        o = v.tensor_tensor(dst[:, i, :], dst[:, i, :], bank(i % 4), ALU.add)
                    else:
                        o = v.tensor_copy(dst[:, i, :], bank(i % 4))
                    o.then_inc(S["x_upd"], 1)
                    if i:
                        wait(v, S["x_upd"], t("x_upd"), i)
                        v.bn_stats(BN[:, i - 1, :], dst[:, i - 1, :])
                    if i in split_after:
                        low_part(split_after[i], t, list(split_after).index(i))
                wait(v, S["x_upd"], t("x_upd"), NT)
                step(v.bn_stats(BN[:, NT - 1, :], dst[:, NT - 1, :]))

            def residual(t):
                for i in range(NT):
                    wait(v, S[f"res_in{i // 5}"], t(f"res_in{i // 5}"), 16)
                    v.tensor_tensor(X[:, i, :], X[:, i, :], V[:, i, :], ALU.add).then_inc(S["x_upd"], 1)
                    if i:
                        wait(v, S["x_upd"], t("x_upd"), i)
                        v.bn_stats(BN[:, i - 1, :], X[:, i - 1, :])
                wait(v, S["x_upd"], t("x_upd"), NT)
                step(v.bn_stats(BN[:, NT - 1, :], X[:, NT - 1, :]))

            def qkv(t, scale, turn, cwr_at, counts=None):
                wait(v, S["col_in"], t("col_in"), 16)
                v.tensor_scalar(QBS, COLB[:, 0:4], scale, None, ALU.mult).then_inc(S["qbs_ready"], 1)
                turn(LEAD)
                g = 0
                for j, (a, n) in enumerate(CHUNKS):
                    for which, dst in ((0, T2), (1, T3)):
                        for m in range(KC):
                            if g % 2:
                                wait(v, S["grp_done"], t("grp_done"), g + 1)
                                b = COLB[:, 4 * which + m:4 * which + m + 1]
                                if which == 0:
                                    o = v.tensor_scalar(dst[:, m, a:a + n], bank(g % 4, 128, n), b, scale, ALU.add, ALU.mult)
                                else:
                                    o = v.tensor_scalar(dst[:, m, a:a + n], bank(g % 4, 128, n), b, None, ALU.add)
                                o.then_inc(S["out_d"], 1)
                            if g < TURNS_LEFT:
                                turn(LEAD + 1 + g)
                            g += 1
                    if j == 0 and counts is not None:
                        low_part(WV, t, 0)
                    if j == 1:
                        split(CWS[1], cwr_at)
                if counts is not None:
                    for part in range(2):
                        for i in range(2):
                            log_counts(counts, i, part)
                for i in range(NT):
                    if g % 2:
                        wait(v, S["grp_done"], t("grp_done"), g + 1)
                        v.tensor_copy(V[:, i, :], bank(g % 4)).then_inc(S["out_d"], 1)
                    g += 1

            def up(t, turn, next_keys):
                turn(LEAD)
                g = 0
                for j, (a, n) in enumerate(CHUNKS):
                    for m in range(KC):
                        wait(v, S["out_a"], t("out_a"), g + 1)
                        v.tensor_tensor(T2P[1][m][:, a:a + n], T3[:, m, a:a + n], T2P[0][m][:, a:a + n].bitcast(F32), ALU.subtract).then_inc(S["out_d"], 1)
                        if g < TURNS_LEFT:
                            turn(LEAD + 1 + g)
                        g += 1
                    if j == 1:
                        low_part(next_keys, t, 0)

            def take_groups(t, dst, chunks):
                g = 0
                for j, (a, n) in enumerate(CHUNKS):
                    for m in range(chunks):
                        if g % 2:
                            wait(v, S["grp_done"], t("grp_done"), g + 1)
                            v.tensor_copy(dst[:, m, a:a + n], bank(g % 4, 128, n)).then_inc(S["out_d"], 1)
                        g += 1

            def split(dst, at_, steps=(0, 1, 2)):
                if 0 in steps:
                    wait(v, S["cwr_in"], at_, 16)
                    step(v.tensor_copy(CWH, CWR))
                    step(v.tensor_tensor(CWR, CWR, CWH, ALU.subtract))
                if 1 in steps:
                    step(v.tensor_copy(CWM, CWR))
                    v.tensor_scalar(dst, CWH, PARTM[:, 0:1], None, ALU.mult)
                    step(v.tensor_tensor(CWR, CWR, CWM, ALU.subtract))
                if 2 in steps:
                    step(v.scalar_tensor_tensor(dst, CWM, PARTM[:, 1:2], dst, ALU.mult, ALU.add))
                    v.scalar_tensor_tensor(dst, CWR, PARTM[:, 2:3], dst, ALU.mult, ALU.add).then_inc(S["cws_ready"], 1)

            def cwr(stage_name, layer=None):
                a = at(stage_name, layer)("cws_ready")
                return At(16 * a.base, 16 * a.per, layer)

            def log_counts(t, i, part):
                c = LC[:, i % 2, :]
                if part == 0:
                    wait(v, S[f"lct_in{i % 2}"], t(f"lct_in{i % 2}"), 16 * (i // 2 + 1))
                    v.tensor_scalar(c, c, float(2.0 ** -60), 0.0, ALU.max, ALU.add, accum_out=DEG[:, i:i + 1]).then_inc(S["lc_pre"], 1)
                else:
                    wait(v, S["lc_log"], t("lc_log"), i + 1)
                    v.scalar_tensor_tensor(c, c, 1.0e30, c, ALU.mult, ALU.min).then_inc(S["lc_ready"], 1)

            def merge(t, k, part):
                new = ATTR[:, bass.ds(t("gathered").layer * (EC // LAYERS * BH) + k * G * BH, G * BH)]
                if part == 0:
                    wait(v, S["gathered"], t("gathered"), 16 * G * (k + 1))
                    v.tensor_tensor(MRG[:, 1, :], MRG[:, 0, :], new, ALU.max)
                    step(v.tensor_tensor(MRG[:, 2, :], MRG[:, 0, :], new, ALU.min))
                    v.tensor_tensor(MRG[:, 2, :], MRG[:, 2, :], MRG[:, 1, :], ALU.subtract).then_inc(S["mrg_diff"], 1)
                else:
                    wait(v, S["mrg_log"], t("mrg_log"), k + 1)
                    v.tensor_tensor(MRG[:, 4, :], MRG[:, 1, :], MRG[:, 3, :], ALU.add).then_inc(S["mrg_ready"], 1)

            def attention(t, heads, third):
                steps = heads * NT

                def scores_max(n):
                    i, h = divmod(n, heads)
                    if n >= 2:
                        wait(v, S["t_done"], t("t_done"), n - 1)
                    wait(v, S["s_done"], t("s_done"), n + 1)
                    if third:
                        if n == 0:
                            v.wait_ge(S["bia_first"], 16)
                        if h == 0:
                            wait(v, S[f"bia_in{i % 2}"], t(f"bia_in{i % 2}"), 16 * (i // 2 + 1))
                        add = BIA[(i + 1) % 2][:, :, h].rearrange("p (a x) -> p a x", x=250)
                    else:
                        if h == 0:
                            wait(v, S["lc_ready"], t("lc_ready"), i + 1)
                        add = pairs(LC[:, i % 2, :])
                    v.memset(IDLE, 0.0)
                    v.tensor_tensor_reduce(out=pairs(PR[:, n % 2, :]), in0=halves(n % 2), in1=add, scale=1.0, scalar=-3.0e38,
                                           op0=ALU.add, op1=ALU.max, accum_out=MX[:, i % 2, h:h + 1]).then_inc(S["max_ready"], 1)
                    wait(v, S["max_ready"], t("max_ready"), n + 1)
                    v.tensor_scalar(NMX[:, n % 2:n % 2 + 1], MX[:, i % 2, h:h + 1], -1.0, None, ALU.mult).then_inc(S["negmax"], 1)

                def take_blocks(n):
                    wait(v, S["t_done"], t("t_done"), n + 1)
                    if n >= 2:
                        wait(v, S["pv_done"], t("pv_done"), n - 1)
                    v.tensor_copy(pairs(PT[:, n % 2, :])[:, 0:2, :], halves(n % 2)[:, 0:2, :]).then_inc(S["t_out_d"], 1)

                def take_rows(i):
                    n = heads * (i + 1)
                    wait(v, S["p_ready"], t("p_ready"), n)
                    rd = RD[:, i % 2, 0:heads]
                    step(v.reciprocal(rd, DEN[:, i % 2, 0:heads]))
                    step(v.scalar_tensor_tensor(rd, MX[:, i % 2, 0:heads], 0.1 * NO_EDGE, rd, ALU.is_ge, ALU.mult))
                    wait(v, S["pv_done"], t("pv_done"), n)
                    if i >= 1:
                        wait(v, S["oT_done"], t("oT_done"), i)
                    v.tensor_tensor(OS.rearrange("p (h x) -> p h x", h=heads), bank(6 + i % 2).rearrange("p (h x) -> p h x", h=heads),
                                    rd.unsqueeze(2).to_broadcast([P, heads, D // heads]), ALU.mult).then_inc(S["o_ready"], 1)

                for n in range(steps + (2 if third else 4)):
                    if n < steps:
                        scores_max(n)
                    if 1 <= n <= steps:
                        take_blocks(n - 1)
                    if n >= 2 and (n - 2) % heads == heads - 1:
                        take_rows((n - 2) // heads)
                    if third and n in SPLIT_STEPS:
                        split(CWS[0], cwr("att2"), [SPLIT_STEPS.index(n)])
                    if not third and n < steps:
                        i, h = divmod(n, heads)
                        if 1 <= i < NT - 1 and h in (0, 2):
                            log_counts(t, i + 1, h // 2)
                        if n % 8 in (3, 6):
                            merge(t, n // 8, n % 8 // 4)
                        if n == 13:
                            low_part(WO, t, 0)
                    if not third and n >= 4 and (n - 4) % heads == heads - 1:
                        low_T(t, (n - 4) // heads, "oT")

            v.memset(ZERO, 0.0).then_inc(S["zero_ready"], 1)
            v.wait_ge(S["ends_in"], 16 * 2)
            v.tensor_copy(DSTG, DSTJ)
            step(v.tensor_copy(KEYC, SRCJ))
            v.scalar_tensor_tensor(KEYC, KEYC, float(N), DSTG, ALU.mult, ALU.add).then_inc(S["keyc_ready"], 1)

            v.wait_ge(S["consts_ready"], 5)
            step(v.tensor_copy(FRQ[:, 1:2], FRQ[:, 0:1].bitcast(I32)))
            step(v.tensor_scalar(FRQ[:, 1:2], FRQ[:, 1:2], float(np.float32(2.0 * np.pi / 16)), None, ALU.mult))
            step(v.memset(FRQ[:, 2:4], 0.0))
            v.memset(FRQ[32:64, 2:3], 0.25)
            step(v.memset(FRQ[32:64, 3:4], float(np.float32(np.pi / 2))))
            v.wait_ge(S["noise_in"], 16 * 5)
            ph, turns = PHASE[:, 0, :], PHASE[:, 1, :]
            two_pi = 2 * np.pi
            p1 = 6.28125
            p2 = float(np.float32(two_pi - p1))
            step(v.tensor_scalar(ph, ph, FRQ[:, 1:2], None, ALU.mult))
            step(v.tensor_scalar(turns, ph, float(1.0 / two_pi), FRQ[:, 2:3], ALU.mult, ALU.add))
            step(v.tensor_scalar(turns, turns, float(1.5 * 2 ** 23), None, ALU.add))
            step(v.tensor_scalar(turns, turns, float(1.5 * 2 ** 23), None, ALU.subtract))
            for c in (p1, p2, two_pi - p1 - p2):
                step(v.scalar_tensor_tensor(ph, turns, -c, ph, ALU.mult, ALU.add))
            step(v.tensor_scalar(ph, ph, FRQ[:, 3:4], None, ALU.add))
            v.tensor_scalar(ph, ph, 3.1415925, -3.1415925, ALU.min, ALU.max).then_inc(S["phase_ready"], 1)
            v.memset(CONDS, 0.0).then_inc(S["conds_clear"], 1)
            v.memset(BSEL, 0.0)
            step(v.memset(CONDF, 1.0))
            v.memset(BSEL[BIAS_ROW:BIAS_ROW + 3, :], 1.0)
            split(CWS[0], At(0))

            v.wait_ge(S["edges_in"], 16 * 3)
            v.tensor_copy(SRC, SRCI)
            step(v.tensor_copy(DST, DSTI))
            step(v.scalar_tensor_tensor(KEY, SRC, float(N), DST, ALU.mult, ALU.add))
            v.tensor_copy(KEYI, KEY)
            v.reduce_max(GMX, ATTR, AX.X).then_inc(S["gmax_ready"], 1)
            v.wait_ge(S["consts_ready"], 6)
            step(v.tensor_copy(SPARE, SRCG.bitcast(I32)))
            v.tensor_tensor(SPARE, SPARE, KEY, ALU.subtract)
            v.wait_ge(S["gmax_all"], 1)
            v.tensor_scalar(BACK, GALL, HEADROOM, None, ALU.subtract)
            v.tensor_scalar(SHIFT, GALL, -1.0, HEADROOM, ALU.mult, ALU.add).then_inc(S["shift_ready"], 1)
            v.wait_ge(S["exp_ready"], 1)
            ex = EX.rearrange("p (c h) -> p c h", h=BH)
            step(v.tensor_copy(EPART[:, :, 0:BH], ex))
            step(v.tensor_tensor(ex, ex, EPART[:, :, 0:BH], ALU.subtract))
            step(v.tensor_copy(EPART[:, :, BH:2 * BH], ex))
            step(v.tensor_tensor(ex, ex, EPART[:, :, BH:2 * BH], ALU.subtract))
            v.tensor_copy(EPART[:, :, 2 * BH:3 * BH], ex)
            v.memset(EPART[:, :, 3 * BH:WP + 1], 1.0)
            step(v.tensor_copy(TRIB, TRI))

            def compare(g):
                v.wait_ge(S[f"keyb_in{g % 2}"], 16 * (g // 2 + 1))
                if g >= 2:
                    v.wait_ge(S["grp_sum"], g - 1)
                q = EQ[g % 2]
                for c in range(G):
                    o = v.tensor_scalar(q[:, c * G * P:(c + 1) * G * P], KEYB[:, g % 2, :], KEY[:, G * g + c:G * g + c + 1], None, ALU.is_equal)
                o.then_inc(S["eq_ready"], 1)
                v.wait_ge(S["eq_ready"], g + 1)
                v.tensor_tensor(EQD[g % 2], q.rearrange("p (c x) -> p c x", c=G)[:, :, 0:P],
                                TRIB.unsqueeze(1).to_broadcast([P, G, P]), ALU.mult).then_inc(S["eqd_ready"], 1)

            def take_sums(g):
                v.wait_ge(S["grp_sum"], g + 1)
                b = banks[0:P, g % 2, 0:G * 32].rearrange("p (c x) -> p c x", c=G)
                gs = slice(G * g, G * g + G)
                v.tensor_copy(NGRP[:, gs], b[:, :, WP - 1])
                v.tensor_copy(SUMS[:, gs, :], b[:, :, 0:WP])
                if g:
                    v.wait_ge(S["idx_ready"], g)
                step(v.tensor_scalar(LATE, b[:, :, WP], 0.5, None, ALU.is_ge))
                v.sem_inc(S["sums_out"], 1)
                step(v.tensor_tensor(LATE, LATE, SPARE[:, gs], ALU.mult))
                step(v.tensor_tensor(LATE, LATE, KEY[:, gs], ALU.add))
                v.tensor_copy(WIDX[:, gs], LATE).then_inc(S["idx_ready"], 1)

            def take_condition():
                for j, (a, n) in enumerate(CHUNKS):
                    v.wait_ge(S["cond_mm"], j + 1)
                    v.tensor_scalar(CONDF[0:CD, a:a + n], bank(4 + j, CD, n), FB[:, 1:2], None, ALU.add).then_inc(S["cond_built"], 1)
                v.wait_ge(S["cond_built"], len(CHUNKS))
                step(v.tensor_copy(CONDP[:, 0, :], CONDF))
                step(v.tensor_tensor(CONDF, CONDF, CONDP[:, 0, :], ALU.subtract))
                step(v.tensor_copy(CONDP[:, 1, :], CONDF))
                step(v.tensor_tensor(CONDF, CONDF, CONDP[:, 1, :], ALU.subtract))
                v.tensor_copy(CONDP[:, 2, :], CONDF).then_inc(S["cond_parts"], 1)

            for g in range(NG):
                compare(g)
                if g:
                    take_sums(g - 1)
                if g == COND_GROUP:
                    take_condition()
                if g == NORM_GROUP:
                    norm(at("pre0"), X, "relu", source="x_in")
                if g == NORM_GROUP + 2:
                    wait(v, S["xn_ready"], At(0), NT)
                    for i in range(NT):
                        o = v.bn_stats(BN[:, i, :], X[:, i, :])
                    step(o)
            low_part(WK, at("start"), 0)
            take_sums(NG - 1)

            tmp = TMP.rearrange("p (c h) -> p c h", h=BH)
            attr = ATTR.rearrange("p (c h) -> p c h", h=BH)
            v.wait_ge(S["idx_ready"], NG)
            step(v.tensor_tensor(tmp, SUMS[:, :, 0:BH], SUMS[:, :, BH:2 * BH], ALU.add))
            step(v.tensor_tensor(tmp, tmp, SUMS[:, :, 2 * BH:3 * BH], ALU.add))
            v.tensor_scalar(tmp, tmp, float(2.0 ** -62), None, ALU.max).then_inc(S["lsum_ready"], 1)
            v.wait_ge(S["lse_log"], 1)
            step(v.scalar_tensor_tensor(tmp, tmp, BACK, attr, ALU.add, ALU.subtract))
            step(v.tensor_scalar(CNT, NGRP, 1.5, None, ALU.is_ge))
            step(v.tensor_tensor(tmp, tmp, CNT.unsqueeze(2).to_broadcast([P, EC, BH]), ALU.mult))
            v.tensor_tensor(attr, attr, tmp, ALU.add).then_inc(S["lse_ready"], 1)

            low_part(WQ, at("start"), 1)
            start_steps, start_gates = mine[0], gates[0]
            with v.Fori(0, LAYERS) as L:
                mine[1] = L
                t = at("n1", L)
                turn = norm(t, X, "cond", in_parts=True)
                qkv(at("qkv", L), 128.0 ** -0.5, turn, cwr("qkv", L), at("att", L))
                attention(at("att", L), 4, False)
                update(at("wo", L), X, split_after={4: WU, 6: WD})
                turn = norm(at("n2", L), X, "cond", in_parts=True)
                up(at("up", L), turn, WK)
                split(CWS[0], cwr("up", L))
                update(at("down", L), X, split_after={5: WQ})
                per_steps, per_gates = mine[0] - start_steps, gates[0] - start_gates
            assert per_steps == V_LOOP_STEPS, per_steps
            assert per_gates == GATES_PER_LAYER, per_gates
            mine[0], mine[1] = start_steps + LAYERS * per_steps, None
            gates[0] = start_gates + LAYERS * per_gates

            v.tensor_scalar(FLAG, DEG, 0.5, None, ALU.is_ge)
            v.tensor_scalar(DEG1, DEG, 1.0, None, ALU.add)
            v.tensor_scalar(DINV, DEG, 1.0, None, ALU.max).then_inc(S["deg_clip"], 1)
            v.wait_ge(S["deg_sqrt"], 1)
            step(v.reciprocal(DINV, DINV))
            v.tensor_tensor(DINV, DINV, FLAG, ALU.mult).then_inc(S["dinv_ready"], 1)
            residual(at("res1"))
            norm(at("pre1"), X, "relu")
            t = at("dense")
            v.wait_ge(S["dinv_in"], 16)
            step(v.tensor_scalar(DINVB, DINVB, -1.0, None, ALU.mult))
            for i in range(NT):
                wait(v, S[f"dense_in{i // 5}"], t(f"dense_in{i // 5}"), 16)
                v.scalar_tensor_tensor(DENSE[:, i, :], DENSE[:, i, :], DINV[:, i:i + 1], DINVB, ALU.mult, ALU.mult).then_inc(S["dense_ready"], 1)
            take_groups(at("prop1"), T2, KC)
            update(at("conv1"), V, add=False)
            norm(at("mid1"), V, "affine", dst=V, slope=0.01)
            wait(v, S["y_ready"], at("mid1")("y_ready"), NT)
            v.sem_inc(S["gb_used"], 1)
            take_groups(at("prop2"), T2, KC)
            update(at("conv2"), X, split_after={2: WK, 4: WQ, 6: WV})
            norm(at("pre2"), X, "relu")
            t = at("z1")
            for i in range(NT):
                wait(v, S["xn_ready"], t("xn_ready"), i + 1 - NT)
                o = v.bn_stats(BN[:, i, :], X[:, i, :])
            step(o)
            turn = norm(t, X, "affine", in_parts=True)
            qkv(at("qkv2"), 0.125, turn, cwr("z1"))
            attention(at("att2"), BH, True)
            update(at("wo2"), X, split_after={5: WU2[0], 7: WU2[1]})
            turn = norm(at("z2"), X, "affine", in_parts=True)
            for d in range(LEAD, NT + 2):
                turn(d)
            split(CWS[1], cwr("z2"))
            update(at("down2"), X, residual=True)
            t = at("ct")
            for i in range(NT):
                wait(v, S["ct_done"], t("ct_done"), i + 1)
                to, blocks = count_columns(i)
                step(v.tensor_copy(to[:, 0:2], blocks[:, 0:2]))
                wait(v, S["ct_out"], t("ct_out"), i + 1)
                v.tensor_tensor(DENSE[:, i, i * P:(i + 1) * P], DENSE[:, i, i * P:(i + 1) * P], IDENT[0:P, 0:P], ALU.add).then_inc(S["dense_ready"], 1)
            norm(at("pre3"), X, "relu")
            t = at("r3")
            for g in range(NT):
                wait(v, S["grp_done"], t("grp_done"), g + 1)
                v.tensor_scalar(V[:, g, 0:256], bank(g % 4, P, 256), 0.0, None, ALU.max).then_inc(S["out_d"], 1)
            take_groups(at("prop3"), T2, 2)
            t = at("conv3")
            wait(v, S["gb_in"], t("gb_in"), 16)
            for i in range(NT):
                wait(v, S["upd_done"], t("upd_done"), i + 1)
                step(v.tensor_tensor(X[:, i, :], X[:, i, :], bank(i % 4), ALU.add))
                v.sem_inc(S["x_upd"], 1)
                v.scalar_tensor_tensor(X[:, i, :], GB[:, 0, :], DEG1[:, i:i + 1], X[:, i, :], ALU.mult, ALU.add).then_inc(S["final_ready"], 1)

        @block.scalar
        def _(act):
            def high_part(w, name, t, k):
                wait(act, S[name], t(name), k)
                act.activation(w.high, w.raw, ACT.Copy).then_inc(S["hi_ready"], 1)

            def norm(t, src, kind, dst=None, transposed=True, in_parts=False):
                wait(act, S["stats_ready"], t("stats_ready"), 1)
                act.activation(STD, VARC, ACT.Sqrt).then_inc(S["std_ready"], 1)
                wait(act, S["rstd_ready"], t("rstd_ready"), 1)
                if kind == "relu":
                    for i in range(NT):
                        d = Y[:, i % 2, :] if dst is None else dst[:, i, :]
                        if dst is None and i >= 2:
                            wait(act, S["yT_ready"], t("yT_ready"), i - 1)
                        act.activation(d, src[:, i, :], ACT.Relu, bias=NMR[:, i:i + 1], scale=RSTD[:, i:i + 1]).then_inc(S["xn_ready"], 1)
                        if transposed and i:
                            take_T(t, i - 1)
                    if transposed:
                        take_T(t, NT - 1)
                    return

                def turn(d):
                    if d < NT:
                        if d >= 2:
                            wait(act, S["y_ready"], t("y_ready"), d - 1)
                        act.activation(XN[:, d % 2, :], src[:, d, :], ACT.Identity, bias=NMR[:, d:d + 1], scale=RSTD[:, d:d + 1]).then_inc(S["xn_ready"], 1)
                    if in_parts and d >= 2:
                        take_T(t, d - 2, in_parts)

                for d in range(LEAD + 1 if in_parts else NT):
                    turn(d)
                return turn

            def take_T(t, i, in_parts=False):
                wait(act, S["yT_ready"], t("yT_ready"), i + 1)
                dst, done = (T1P[0], "yT_hi") if in_parts else (T1, "yT_out")
                act.activation(dst[:, :, i * P:(i + 1) * P], banks[0:128, 4 + i % 2, 0:500].rearrange("p (c x) -> p c x", c=KC), ACT.Copy).then_inc(S[done], 1)

            def log_counts(t, i):
                wait(act, S["lc_pre"], t("lc_pre"), i + 1)
                act.activation(LC[:, i % 2, :], LC[:, i % 2, :], ACT.Ln).then_inc(S["lc_log"], 1)

            def qkv(t, scale, turn, counts=None):
                wait(act, S["col_in"], t("col_in"), 16)
                wait(act, S["qbs_ready"], t("qbs_ready"), 1)
                g = 0
                for j, (a, n) in enumerate(CHUNKS):
                    for which, dst in ((0, T2), (1, T3)):
                        for m in range(KC):
                            if g % 2 == 0:
                                wait(act, S["grp_done"], t("grp_done"), g + 1)
                                if which == 0:
                                    o = act.activation(dst[:, m, a:a + n], bank(g % 4, 128, n), ACT.Identity, bias=QBS[:, m:m + 1], scale=scale)
                                else:
                                    o = act.activation(dst[:, m, a:a + n], bank(g % 4, 128, n), ACT.Identity, bias=COLB[:, 4 + m:5 + m])
                                o.then_inc(S["out_a"], 1)
                            if g < TURNS_LEFT:
                                turn(LEAD + 1 + g)
                            g += 1
                    if j == 0 and counts is not None:
                        high_part(WV, "w2_in", t, 16)
                if counts is not None:
                    for i in range(2):
                        log_counts(counts, i)
                for i in range(NT):
                    if g % 2 == 0:
                        wait(act, S["grp_done"], t("grp_done"), g + 1)
                        act.activation(V[:, i, :], bank(g % 4), ACT.Copy).then_inc(S["out_a"], 1)
                    g += 1

            def take_groups(t, dst, chunks, func=ACT.Copy, cols=None, every=False, after=None):
                g = 0
                for j, (a, n) in enumerate(CHUNKS):
                    for m in range(chunks):
                        if g % 2 == 0 or every:
                            wait(act, S["grp_done"], t("grp_done"), g + 1)
                            if cols is None:
                                o = act.activation(dst[:, m, a:a + n], bank(g % 4, 128, n), func)
                            else:
                                o = act.activation(dst[:, m, a:a + n], bank(g % 4, 128, n), func, bias=cols[:, m:m + 1])
                            o.then_inc(S["out_a"], 1)
                        if after is not None:
                            after(g)
                        g += 1

            def columns_after(name):
                return lambda g: take_T(at(name), g) if g < NT else None

            def hidden(t, turn, cols):
                g = 0
                for j, (a, n) in enumerate(CHUNKS):
                    for m in range(KC):
                        wait(act, S["grp_done"], t("grp_done"), g + 1)
                        act.activation(T3[:, m, a:a + n], bank(g % 4, 128, n), ACT.Relu, bias=cols[:, m:m + 1])
                        act.activation(T2P[0][m][:, a:a + n], bank(g % 4, 128, n), ACT.Relu, bias=cols[:, m:m + 1]).then_inc(S["out_a"], 1)
                        if g < TURNS_LEFT:
                            turn(LEAD + 1 + g)
                        g += 1
                    if j == 0:
                        high_part(WK, "w1_in", t, 16)

            def attention(t, heads):
                steps = heads * NT

                def merge(k):
                    wait(act, S["mrg_diff"], t("mrg_diff"), k + 1)
                    act.activation(MRG[:, 3, :], MRG[:, 2, :], ACT.Exp).then_inc(S["mrg_exp"], 1)
                    wait(act, S["mrg_exp"], t("mrg_exp"), k + 1)
                    act.activation(MRG[:, 3, :], MRG[:, 3, :], ACT.Ln, bias=1.0).then_inc(S["mrg_log"], 1)

                for n in range(steps + 3):
                    if 1 <= n <= steps:
                        m = n - 1
                        wait(act, S["t_done"], t("t_done"), m + 1)
                        if m >= 2:
                            wait(act, S["pv_done"], t("pv_done"), m - 1)
                        act.activation(pairs(PT[:, m % 2, :])[:, 2:5, :], halves(m % 2)[:, 2:5, :], ACT.Copy).then_inc(S["t_out_a"], 1)
                    if n < steps:
                        i, h = divmod(n, heads)
                        wait(act, S["negmax"], t("negmax"), n + 1)
                        act.activation(PR[:, n % 2, :], PR[:, n % 2, :], ACT.Exp, bias=NMX[:, n % 2:n % 2 + 1],
                                       accum_out=DEN[:, i % 2, h:h + 1]).then_inc(S["p_ready"], 1)
                        if heads == 4 and 1 <= i < NT - 1 and h == 1:
                            log_counts(t, i + 1)
                        if heads == 4 and n % 8 == 4:
                            merge(n // 8)
                        if heads == 4 and n == 11:
                            high_part(WO, "w3_in", t, 16)
                    if n >= 3 and (n - 3) % heads == heads - 1:
                        i = (n - 3) // heads
                        wait(act, S["oT_done"], t("oT_done"), i + 1)
                        dst, done = (T1P[0], "oT_hi") if heads == 4 else (T1, "oT_out")
                        act.activation(dst[:, :, i * P:(i + 1) * P], banks[0:128, 6 + i % 2, 0:500].rearrange("p (c x) -> p c x", c=KC), ACT.Copy).then_inc(S[done], 1)

            act.wait_ge(S["phase_ready"], 1)
            act.activation(PHASE[:, 0, :], PHASE[:, 0, :], ACT.Sin).then_inc(S["emb_ready"], 1)
            act.wait_ge(S["shift_ready"], 1)
            act.wait_ge(S["edges_in"], 16 * 3)
            act.activation(EX, ATTR, ACT.Exp, bias=SHIFT).then_inc(S["exp_ready"], 1)
            for j, (a, n) in enumerate(CHUNKS):
                act.wait_ge(S["emb_mm"], j + 1)
                act.activation(PHASE[0:CD, 1, a:a + n], bank(4 + j, CD, n), ACT.Silu, bias=FB[:, 0:1]).then_inc(S["emb_act"], 1)
            norm(at("pre0"), X, "relu", dst=X, transposed=False)
            t = at("start")
            high_part(WK, "w1_in", t, 16)
            act.wait_ge(S["lsum_ready"], 1)
            act.activation(TMP, TMP, ACT.Ln).then_inc(S["lse_log"], 1)
            high_part(WQ, "w0_in", t, 16)
            with act.Fori(0, LAYERS) as L:
                turn = norm(at("n1", L), X, "cond", in_parts=True)
                qkv(at("qkv", L), 128.0 ** -0.5, turn, at("att", L))
                attention(at("att", L), 4)
                high_part(WU, "w4_in", at("wo", L), 16)
                high_part(WD, "w5_in", at("wo", L), 16)
                turn = norm(at("n2", L), X, "cond", in_parts=True)
                hidden(at("up", L), turn, COLB[:, 8:12])
                high_part(WQ, "w0_in", at("down", L), 16)
            act.wait_ge(S["deg_clip"], 1)
            act.activation(DINV, DINV, ACT.Sqrt).then_inc(S["deg_sqrt"], 1)
            norm(at("pre1"), X, "relu", dst=V)
            take_groups(at("prop1"), T2, KC)
            norm(at("mid1"), V, "affine")
            take_groups(at("prop2"), T2, KC, after=columns_after("mid1"))
            t = at("conv2")
            high_part(WK, "w1_in", t, 16)
            high_part(WQ, "w0_in", t, 16)
            high_part(WV, "w4_in", t, 16)
            act.wait_ge(S["x_saved"], 16 * NT)
            norm(at("pre2"), X, "relu", dst=X, transposed=False)
            turn = norm(at("z1"), X, "affine", in_parts=True)
            qkv(at("qkv2"), 0.125, turn)
            attention(at("att2"), BH)
            for w in WU2:
                high_part(w, "w0_in", at("wo2"), 16)
            turn = norm(at("z2"), X, "affine", in_parts=True)
            t = at("up2")
            wait(act, S["col_in"], t("col_in"), 16)
            take_groups(t, H8, 2 * KC, ACT.Silu, COLB[:, 0:8], every=True,
                        after=lambda g: turn(LEAD + 1 + g) if g < TURNS_LEFT else None)
            t = at("ct")
            for i in range(NT):
                wait(act, S["ct_done"], t("ct_done"), i + 1)
                to, blocks = count_columns(i)
                act.activation(to[:, 2:5], blocks[:, 2:5], ACT.Copy).then_inc(S["ct_out"], 1)
            norm(at("pre3"), X, "relu")
            take_groups(at("prop3"), T2, 2)

        @block.tensor
        def _(pe):
            def columns_of(t, i, src, source):
                wait(pe, S[source], t(source), i + 1)
                if i >= 2:
                    wait(pe, S["yT_out"], t("yT_out"), i - 1)
                row = Y[:, i % 2, :] if src is None else src[:, i, :]
                for c in range(KC):
                    o = pe.transpose(banks[0:128, 4 + i % 2, c * P:(c + 1) * P], row[:, c * 128:(c + 1) * 128], IDENT[0:P, 0:P])
                o.then_inc(S["yT_ready"], 1)

            def plain_norm(t):
                def turn(d):
                    columns_of(t, d - 1, None, "y_ready")

                for d in range(1, LEAD):
                    turn(d)
                return turn

            def cond_norm(t, cw):
                def turn(d):
                    if d < NT:
                        if d >= LEAD:
                            wait(pe, S["y_ready"], t("y_ready"), d)
                        elif d >= 2:
                            wait(pe, S["y_ready"], t("y_ready"), d - 1)
                        b = cond_bank(d)
                        pe.matmul(bank(b), CONDS[:, d * P:(d + 1) * P], cw[:, 0:D], start=True, stop=True)
                        pe.matmul(bank(b + 1), CONDS[:, d * P:(d + 1) * P], cw[:, D:2 * D], start=True, stop=True).then_inc(S["cond_ready"], 1)
                    if d >= 1:
                        columns_of(t, d - 1, None, "y_ready")

                wait(pe, S["rstd_ready"], t("rstd_ready"), 1)
                wait(pe, S["cws_ready"], t("cws_ready"))
                for d in range(LEAD):
                    turn(d)
                return turn

            def rows_of(out, i, parts, row, n=D):
                first = True
                for src, w, k in parts:
                    for c in range(k):
                        pe.matmul(out, src[:, c, i * P:(i + 1) * P], w[:, c * n:(c + 1) * n], start=first, stop=False)
                        first = False
                return pe.matmul(out, BSEL, row, start=False, stop=True)

            def project_parts(out, weights, m, a, n, width=D):
                for c in range(KC):
                    w, at_ = (weights[0], c) if len(weights) == 1 else (weights[c // 2], c % 2)
                    cols = slice(at_ * width + m * 128, at_ * width + (m + 1) * 128)
                    pe.matmul(out, w.high[:, cols], T1P[0][:, c, a:a + n], start=(c == 0), stop=False)
                    pe.matmul(out, w.high[:, cols], T1P[1][:, c, a:a + n], start=False, stop=False)
                    o = pe.matmul(out, w.low[:, cols], T1P[0][:, c, a:a + n], start=False, stop=(c == KC - 1))
                return o

            def rows_of_parts(out, i, src, w, row):
                for c in range(KC):
                    high, low = [x[c][:, i * P:(i + 1) * P] if isinstance(x, list) else x[:, c, i * P:(i + 1) * P] for x in src]
                    cols = slice(c * D, (c + 1) * D)
                    pe.matmul(out, high, w.high[:, cols], start=(c == 0), stop=False)
                    pe.matmul(out, high, w.low[:, cols], start=False, stop=False)
                    pe.matmul(out, low, w.high[:, cols], start=False, stop=False)
                return pe.matmul(out, BSEL, row, start=False, stop=True)

            def T1_chunk(t, j):
                a, n = CHUNKS[j]
                wait(pe, S["yT_out"], t("yT_out"), (a + n) // P - NT)

            def qkv(t, row, turn, values, row_ready=None):
                wait(pe, S["w_ready"], t("w_ready"))
                g = 0
                for j, (a, n) in enumerate(CHUNKS):
                    T1_chunk(t, j)
                    for w in (WQ, WK):
                        for m in range(KC):
                            grp_free(pe, t, g)
                            project_parts(bank(g % 4, 128, n), [w], m, a, n).then_inc(S["grp_done"], 1)
                            if g < TURNS_LEFT:
                                turn(LEAD + g)
                            g += 1
                wait(pe, S["w_ready"], values)
                if row_ready is not None:
                    wait(pe, S["cws_ready"], row_ready)
                for i in range(NT):
                    grp_free(pe, t, g)
                    rows_of_parts(bank(g % 4), i, T1P, WV, row).then_inc(S["grp_done"], 1)
                    g += 1

            def attention(t, heads):
                dh, steps = D // heads, heads * NT
                per_chunk = 128 // dh

                def scores(n):
                    i, h = divmod(n, heads)
                    if n >= 2:
                        wait(pe, S["t_out_a"], t("t_out_a"), n - 1)
                        wait(pe, S["t_out_d"], t("t_out_d"), n - 1)
                    lo = dh * (h % per_chunk)
                    q, k = T2[lo:lo + dh, h // per_chunk, i * P:(i + 1) * P], T3[lo:lo + dh, h // per_chunk, :]
                    hv = halves(n % 2)
                    for a, w in ((0, 2), (2, 2), (4, 1)):
                        o = pe.matmul(hv[:, a:a + w, :], q, k[:, a * 250:(a + w) * 250], start=True, stop=True)
                    o.then_inc(S["s_done"], 1)

                def turn(n):
                    wait(pe, S["p_ready"], t("p_ready"), n + 1)
                    hv = halves(n % 2)
                    for j in range(NT):
                        o = pe.transpose(hv[:, j // 2, (j % 2) * P:(j % 2 + 1) * P], PR[:, n % 2, j * P:(j + 1) * P], IDENT[0:P, 0:P])
                    o.then_inc(S["t_done"], 1)

                def product(n):
                    i, h = divmod(n, heads)
                    wait(pe, S["t_out_a"], t("t_out_a"), n + 1)
                    wait(pe, S["t_out_d"], t("t_out_d"), n + 1)
                    if h == 0 and i >= 2:
                        wait(pe, S["oT_out"], t("oT_out"), i - 1)
                    for j in range(NT):
                        o = pe.matmul(bank(6 + i % 2)[:, h * dh:(h + 1) * dh], PT[:, n % 2, j * P:(j + 1) * P], V[:, j, h * dh:(h + 1) * dh],
                                      start=(j == 0), stop=(j == NT - 1))
                    o.then_inc(S["pv_done"], 1)

                def turn_rows(i):
                    wait(pe, S["o_ready"], t("o_ready"), i + 1)
                    for c in range(KC):
                        o = pe.transpose(banks[0:128, 6 + i % 2, c * P:(c + 1) * P], OS[:, c * 128:(c + 1) * 128], IDENT[0:P, 0:P])
                    o.then_inc(S["oT_done"], 1)

                wait(pe, S["out_a"], t("out_a"))
                wait(pe, S["out_d"], t("out_d"))
                scores(0)
                for n in range(steps + 2):
                    if n + 1 < steps:
                        scores(n + 1)
                    if n >= 2 and (n - 2) % heads == heads - 1:
                        turn_rows((n - 2) // heads)
                    if n < steps:
                        turn(n)
                    if 1 <= n <= steps:
                        product(n - 1)

            def update_parts(t, src, w, row):
                for i in range(NT):
                    if i >= 4:
                        wait(pe, S["x_upd"], t("x_upd"), i - 3)
                    rows_of_parts(bank(i % 4), i, src, w, row).then_inc(S["upd_done"], 1)

            def update(t, parts, row):
                for i in range(NT):
                    if i >= 4:
                        wait(pe, S["x_upd"], t("x_upd"), i - 3)
                    rows_of(bank(i % 4), i, parts, row).then_inc(S["upd_done"], 1)

            def groups(t, w, chunks, turn, width=D):
                g = 0
                for j, (a, n) in enumerate(CHUNKS):
                    T1_chunk(t, j)
                    for m in range(chunks):
                        grp_free(pe, t, g, alternate=False)
                        project_parts(bank(g % 4, 128, n), w, m, a, n, width=width).then_inc(S["grp_done"], 1)
                        if g < TURNS_LEFT:
                            turn(LEAD + g)
                        g += 1

            def propagate(t, chunks, dense=None, rows=None):
                g = 0
                for j, (a, n) in enumerate(CHUNKS):
                    for m in range(chunks):
                        grp_free(pe, t, g)
                        for s_ in range(NT):
                            if g == 0 and dense is not None:
                                wait(pe, S["dense_ready"], dense("dense_ready"), s_ + 1)
                            if g == 0 and rows is not None:
                                wait(pe, S[rows[1]], rows[0](rows[1]), s_ + 1)
                            o = pe.matmul(bank(g % 4, 128, n), V[:, s_, m * 128:(m + 1) * 128], DENSE[:, s_, a:a + n], start=(s_ == 0), stop=(s_ == NT - 1))
                        o.then_inc(S["grp_done"], 1)
                        if rows is not None and g < NT:
                            columns_of(rows[0], g, V, rows[1])
                        g += 1

            pe.wait_ge(S["emb_ready"], 1)
            for j, (a, n) in enumerate(CHUNKS):
                pe.matmul(bank(4 + j, CD, n), FW1, PHASE[:, 0, a:a + n], start=True, stop=True).then_inc(S["emb_mm"], 1)
            for g in range(NG):
                pe.wait_ge(S["eqd_ready"], g + 1)
                if g >= 2:
                    pe.wait_ge(S["sums_out"], g - 1)
                b = banks[0:P, g % 2, 0:G * 32].rearrange("p (c x) -> p c x", c=G)
                for c in range(G):
                    for c2 in range(G):
                        w = WP + 1 if c2 < c else WP
                        pe.matmul(b[:, c, 0:w], EQ[g % 2][:, c2 * G * P + c * P:c2 * G * P + (c + 1) * P], EPART[:, G * g + c2, 0:w], start=(c2 == 0), stop=(c == 0 and c2 == G - 1))
                    o = pe.matmul(b[:, c, WP:WP + 1], EQD[g % 2][:, c, :], EPART[:, 0, WP:WP + 1], start=(c == 0), stop=True)
                o.then_inc(S["grp_sum"], 1)
                if g == 0:
                    for j, (a, n) in enumerate(CHUNKS):
                        pe.wait_ge(S["emb_act"], j + 1)
                        pe.matmul(bank(4 + j, CD, n), FW2, PHASE[0:CD, 1, a:a + n], start=True, stop=True).then_inc(S["cond_mm"], 1)
            pe.wait_ge(S["sums_out"], NG)
            pe.wait_ge(S["conds_in"], 16 * (len(STACK) + 1))
            pe.wait_ge(S["consts_ready"], 2)

            with pe.Fori(0, LAYERS) as L:
                turn = cond_norm(at("n1", L), CWS[0])
                t = at("qkv", L)
                w = t("w_ready")
                qkv(t, CWS[0][:, 0:D], turn, At(w.base + 1, w.per, L))
                attention(at("att", L), 4)
                t = at("wo", L)
                wait(pe, S["w_ready"], t("w_ready"))
                wait(pe, S["oT_out"], t("oT_out"))
                wait(pe, S["t_out_d"], t("t_out_d"))
                update_parts(t, T1P, WO, CWS[0][:, D:2 * D])
                turn = cond_norm(at("n2", L), CWS[1])
                wait(pe, S["w_ready"], at("up", L)("w_ready"))
                groups(at("up", L), [WU], KC, turn)
                t = at("down", L)
                wait(pe, S["out_a"], t("out_a"))
                wait(pe, S["out_d"], t("out_d"))
                update_parts(t, T2P, WD, CWS[1][:, 0:D])

            for i in range(NT):
                columns_of(at("pre1"), i, V, "xn_ready")
            t = at("prop1")
            wait(pe, S["x_upd"], t("x_upd"))
            propagate(t, KC, at("dense"))
            t = at("conv1")
            wait(pe, S["out_a"], t("out_a"))
            wait(pe, S["out_d"], t("out_d"))
            wait(pe, S["yT_out"], t("yT_out"))
            wait(pe, S["w0_in"], t("w0_in"), 16)
            wait(pe, S["w1_in"], t("w1_in"), 16)
            update(t, [(T1, W[:, 0, :], KC), (T2, W[:, 1, :], KC)], CWS[0][:, 0:D])
            t = at("prop2")
            propagate(t, KC, rows=(at("mid1"), "y_ready"))
            t = at("conv2")
            wait(pe, S["out_a"], t("out_a"))
            wait(pe, S["out_d"], t("out_d"))
            wait(pe, S["yT_out"], t("yT_out"))
            wait(pe, S["w2_in"], t("w2_in"), 16)
            wait(pe, S["w3_in"], t("w3_in"), 16)
            update(t, [(T1, W[:, 2, :], KC), (T2, W[:, 3, :], KC)], CWS[0][:, D:2 * D])
            turn = plain_norm(at("z1"))
            qkv(at("qkv2"), CWS[1][:, 0:D], turn, at("qkv2")("w_ready"), at("qkv2")("cws_ready"))
            attention(at("att2"), BH)
            t = at("wo2")
            wait(pe, S["w3_in"], t("w3_in"), 16)
            wait(pe, S["cws_ready"], t("cws_ready"))
            wait(pe, S["oT_out"], t("oT_out"))
            wait(pe, S["t_out_d"], t("t_out_d"))
            update(t, [(T1, W[:, 3, :], KC)], CWS[0][:, 0:D])
            turn = plain_norm(at("z2"))
            t = at("up2")
            wait(pe, S["w_ready"], t("w_ready"))
            groups(t, WU2, 2 * KC, turn, width=2 * D)
            t = at("down2")
            wait(pe, S["w2_in"], t("w2_in"), 16)
            wait(pe, S["out_a"], t("out_a"))
            update(t, [(H8, W[:, 0:2, :].rearrange("p a b -> p (a b)"), 2 * KC)], CWS[0][:, D:2 * D])
            t = at("ct")
            wait(pe, S["x_upd"], t("x_upd"))
            for i in range(NT):
                wait(pe, S[f"c_in{i % 3}"], t(f"c_in{i % 3}"), 16 * (i // 3 + 1))
                if i >= 2:
                    wait(pe, S["dense_ready"], t("dense_ready"), i - 1)
                hv = halves(i % 2)
                for j in range(NT):
                    o = pe.transpose(hv[:, j // 2, (j % 2) * P:(j % 2 + 1) * P], CR[:, i % 3, j * P:(j + 1) * P], IDENT[0:P, 0:P])
                o.then_inc(S["ct_done"], 1)
            t = at("pre3")
            wait(pe, S["dense_ready"], t("dense_ready"))
            for i in range(NT + 1):
                if i < NT:
                    columns_of(t, i, None, "xn_ready")
                if i == 0:
                    wait(pe, S["w0_in"], at("r3")("w0_in"), 16)
                    wait(pe, S["cws_ready"], at("r3")("cws_ready"))
                else:
                    g = i - 1
                    wait(pe, S["yT_out"], t("yT_out"), g + 1)
                    if g >= 4:
                        wait(pe, S["out_d"], at("r3")("out_d"), g - 3)
                    rows_of(bank(g % 4, P, 256), g, [(T1, W[:, 0, :], KC)], CWS[1][:, 0:256], n=256).then_inc(S["grp_done"], 1)
            t = at("prop3")
            wait(pe, S["out_a"], t("out_a"))
            wait(pe, S["out_d"], t("out_d"))
            propagate(t, 2)
            t = at("conv3")
            wait(pe, S["w1_in"], t("w1_in"), 16)
            wait(pe, S["out_a"], t("out_a"))
            wait(pe, S["out_d"], t("out_d"))
            for i in range(NT):
                if i >= 4:
                    wait(pe, S["x_upd"], t("x_upd"), i - 3)
                for c in range(2):
                    o = pe.matmul(bank(i % 4), T2[:, c, i * P:(i + 1) * P], W[:, 1, c * D:(c + 1) * D], start=(c == 0), stop=(c == 1))
                o.then_inc(S["upd_done"], 1)


def kernel(**inputs):
    import concourse.bacc as _bacc
    from concourse import mybir as _mybir
    from concourse.bass_utils import run_bass_kernel_spmd as _run

    nc = _bacc.Bacc("TRN2", target_bir_lowering=False, num_devices=1)
    f = {k: np.asarray(v) for k, v in inputs.items()}

    def parts(w):
        *lead, k, m = w.shape
        w = w.reshape(*lead, k // 128, 128, m)
        return np.moveaxis(w, -3, -2).reshape(*lead, 128, k // 128 * m)

    def cols(b):
        return np.moveaxis(b.reshape(*b.shape[:-1], -1, 128), -1, -2)

    src, dst = f["src"].reshape(P, EC), f["dst"].reshape(P, EC)
    L0, L1, L2, L3 = (lambda n, k=k: f[f"L{k}_gnn_{n}"] for k in range(4))

    def stacked(weights=None, *biases):
        a = np.zeros((SK, 2 * D), np.float32)
        if weights is not None:
            places = [p for p in range(SK) if not BIAS_ROW <= p < BIAS_ROW + 3]
            a[places] = np.tile(weights, (len(STACK), 1))
        row = np.concatenate(biases)
        a[BIAS_ROW:BIAS_ROW + 3, 0:len(row)] = row
        return a

    def cond_rows(layer, k):
        w = np.concatenate([L0(f"s{k}_w")[layer], L0(f"b{k}_w")[layer]], 1)
        b = np.concatenate([L0(f"s{k}_b")[layer], L0(f"b{k}_b")[layer]])[None]
        one = np.concatenate([np.ones((1, D), np.float32), np.zeros((1, D), np.float32)], 1)
        return np.concatenate([w, b, one])

    cw = np.stack([np.stack([stacked(cond_rows(l, 1), L0("bv")[l], L0("bo")[l]), stacked(cond_rows(l, 2), L0("m_b2")[l])])
                   for l in range(LAYERS)] + [np.stack([stacked(None, L1("b1"), L1("b2")), np.zeros((SK, 2 * D), np.float32)])])
    later = np.stack([stacked(None, L2("bv")), stacked(None, L2("bo"), L2("b2")), stacked(None, L3("b1"))])
    part_of = [0] * 54 + [1] * 36 + [2] * 6 + [0, 1, 2] + [2] * 12
    part_mask = np.eye(3, dtype=np.float32)[part_of]
    arr = {
        "x": f["x"],
        "src_pc": src, "dst_pc": dst,
        "src_cp": np.ascontiguousarray(src.T).reshape(P, EC), "dst_cp": np.ascontiguousarray(dst.T).reshape(P, EC),
        "edge_attr": f["edge_attr_8"].reshape(P, EC * BH),
        "noise": f["node_vec1"].reshape(1, N),
        "f_w1": L0("f_w1"), "f_w2": L0("f_w2"), "f_b": np.stack([L0("f_b1"), L0("f_b2")], 1),
        "w0": np.concatenate([np.stack([parts(L0(n)) for n in ("wq", "wk", "wv", "wo", "m_w1", "m_w2")], 1), np.zeros((1, 6, 128, KC * D), np.float32)]),
        "colb": np.concatenate([cols(L0(n)) for n in ("bq", "bk", "m_b1")], 2),
        "cw": cw, "later_rows": later, "part_mask": part_mask,
        "w1": np.stack([parts(L1(n)) for n in ("W1_0", "W1_1", "W2_0", "W2_1")]),
        "l1_gamma": L1("gamma").reshape(1, D), "l1_beta": L1("beta").reshape(1, D),
        "w2": np.stack([parts(L2(n).T) for n in ("Wq", "Wk", "Wv", "Wo")]),
        "l2_colb": np.concatenate([cols(L2("bq")), cols(L2("bk"))], 1),
        "l2_lnb": np.stack([L2("ln_att_g"), L2("ln_att_b"), L2("ln_ff_g"), L2("ln_ff_b")]),
        "l2_b1": cols(L2("b1")), "l2_w1": parts(L2("W1").T), "l2_w2": parts(L2("W2").T),
        "l3_w1": parts(L3("W1")), "l3_w2": parts(L3("W2")),
        "l3_b2": L3("b2").reshape(1, D),
    }
    arr = {k: np.ascontiguousarray(a) for k, a in arr.items()}
    A = {k: nc.dram_tensor("in_" + k, a.shape, _mybir.dt.from_np(a.dtype), kind="ExternalInput").ap() for k, a in arr.items()}
    A["out"] = nc.dram_tensor("out", (N, D), _mybir.dt.float32, kind="ExternalOutput").ap()
    build(nc, A)
    r = _run(nc, [{"in_" + k: a for k, a in arr.items()}], core_ids=[0])
    return r.results[0]["out"]
```
